# Optimizing a Trainium2 kernel written in Bass

```python
import numpy as np
import jax
import jax.numpy as jnp

def _softmax(x, axis=-1):
    return jax.nn.softmax(x, axis=axis)

def _gelu(x):
    return jax.nn.gelu(x, approximate=True)

def _silu(x):
    return jax.nn.silu(x)

def _sigmoid(x):
    return jax.nn.sigmoid(x)

def _layernorm(x, axis=-1, eps=1e-05):
    m = jnp.mean(x, axis=axis, keepdims=True)
    v = jnp.var(x, axis=axis, keepdims=True)
    return (x - m) / jnp.sqrt(v + eps)

def _scatter_add(tgt, idx, src, axis=0):
    return tgt.at[idx].add(src)

def _segment_sum(src, seg, n):
    return jax.ops.segment_sum(src, seg, n)
kernel_name = 'mk_gnn_resnorm_d2_gnn_r32_5162a4'

def setup_inputs(seed: int=0):
    np.random.seed(seed)
    _w = jnp.asarray

    def _rec_inputs():
        import jax
        import jax.numpy as jnp
        _gk = jax.random.key(seed)
        x = -0.000202 + 1 * jax.random.normal(jax.random.fold_in(_gk, 1), (50000, 128), jnp.float32)
        src = jax.random.randint(jax.random.fold_in(_gk, 2), (25000,), 0, 50000, jnp.int32)
        dst = jnp.minimum((50000 * jax.random.uniform(jax.random.fold_in(_gk, 3), (25000,)) ** 2.0).astype(jnp.int32), 49999)
        _o = jnp.argsort(dst, stable=True)
        src = src[_o]
        dst = dst[_o]
        edge_attr_128 = -8.16379e-05 + 0.999858 * jax.random.normal(jax.random.fold_in(_gk, 11), (25000, 128), jnp.float32)
        return (x, src, dst, edge_attr_128)
    x, src, dst, edge_attr_128 = _rec_inputs()

    def _L0_gnn_setup():
        import jax, jax.numpy as jnp
        import numpy as np
        N_NODES = 50000
        N_EDGES = 25000
        D_IN = 128
        D_HID = 128
        D_OUT = 128

        def _sage_conv(x, src, dst, Wl, bl, Wr):
            msg = x[src]
            summed = jax.ops.segment_sum(msg, dst, num_segments=N_NODES)
            cnt = jax.ops.segment_sum(jnp.ones((src.shape[0],), x.dtype), dst, num_segments=N_NODES)
            mean = summed / jnp.maximum(cnt, 1.0)[:, None]
            return mean @ Wl.T + bl + x @ Wr.T
        key = jax.random.key(seed)
        ks = jax.random.split(key, 12)
        x = jax.random.normal(ks[0], (N_NODES, D_IN), dtype=jnp.float32)
        edge_index = jax.random.randint(ks[1], (2, N_EDGES), 0, N_NODES, dtype=jnp.int64)

        def lin(k, fan_in, fan_out):
            s = 1.0 / np.sqrt(fan_in)
            return jax.random.uniform(k, (fan_out, fan_in), jnp.float32, -s, s)
        dims = [(D_IN, D_HID), (D_HID, D_HID), (D_HID, D_OUT)]
        params = {}
        ki = 2
        for i, (fi, fo) in enumerate(dims):
            params[f'Wl{i}'] = lin(ks[ki], fi, fo)
            ki += 1
            params[f'bl{i}'] = jnp.zeros((fo,), jnp.float32)
            params[f'Wr{i}'] = lin(ks[ki], fi, fo)
            ki += 1
        return {'x': x, 'edge_index': edge_index, **params}
    _L0_gnn_all = _L0_gnn_setup()
    _L0_gnn_in = {k: v for k, v in _L0_gnn_all.items() if k in ('Wl0', 'bl0', 'Wr0', 'Wl1', 'bl1', 'Wr1', 'Wl2', 'bl2', 'Wr2')}
    del _L0_gnn_all

    def _L1_gnn_setup():
        import jax, jax.numpy as jnp
        import numpy as np
        N, E, DIM = (50000, 25000, 128)
        H, EH, HD = (8, 8, 16)
        key = jax.random.key(seed)
        ks = jax.random.split(key, 10)
        s = 0.05
        return {'x': jax.random.normal(ks[0], (N, DIM), jnp.float32), 'edges': jax.random.normal(ks[1], (E, DIM), jnp.float32), 'Wq': jax.random.normal(ks[2], (DIM, DIM), jnp.float32) * s, 'Wk': jax.random.normal(ks[3], (DIM, DIM), jnp.float32) * s, 'Wv': jax.random.normal(ks[4], (DIM, EH * HD), jnp.float32) * s, 'Wek': jax.random.normal(ks[5], (DIM, DIM), jnp.float32) * s, 'Wev': jax.random.normal(ks[6], (DIM, EH * HD), jnp.float32) * s, 'W_exp': jax.random.normal(ks[7], (H, EH), jnp.float32) * s, 'W_out': jax.random.normal(ks[8], (EH * HD, DIM), jnp.float32) * s, 'edge_index': jax.random.randint(ks[9], (2, E), 0, N, jnp.int64)}
    _L1_gnn_all = _L1_gnn_setup()
    _L1_gnn_in = {k: v for k, v in _L1_gnn_all.items() if k in ('Wq', 'Wk', 'Wv', 'Wek', 'Wev', 'W_exp', 'W_out')}
    del _L1_gnn_all
    return {'x': x, 'src': src, 'dst': dst, 'edge_attr_128': edge_attr_128, 'L0_gnn_Wl0': _L0_gnn_in['Wl0'], 'L0_gnn_bl0': _L0_gnn_in['bl0'], 'L0_gnn_Wr0': _L0_gnn_in['Wr0'], 'L0_gnn_Wl1': _L0_gnn_in['Wl1'], 'L0_gnn_bl1': _L0_gnn_in['bl1'], 'L0_gnn_Wr1': _L0_gnn_in['Wr1'], 'L0_gnn_Wl2': _L0_gnn_in['Wl2'], 'L0_gnn_bl2': _L0_gnn_in['bl2'], 'L0_gnn_Wr2': _L0_gnn_in['Wr2'], 'L1_gnn_Wq': _L1_gnn_in['Wq'], 'L1_gnn_Wk': _L1_gnn_in['Wk'], 'L1_gnn_Wv': _L1_gnn_in['Wv'], 'L1_gnn_Wek': _L1_gnn_in['Wek'], 'L1_gnn_Wev': _L1_gnn_in['Wev'], 'L1_gnn_W_exp': _L1_gnn_in['W_exp'], 'L1_gnn_W_out': _L1_gnn_in['W_out']}

def reference(x, src, dst, edge_attr_128, L0_gnn_Wl0, L0_gnn_bl0, L0_gnn_Wr0, L0_gnn_Wl1, L0_gnn_bl1, L0_gnn_Wr1, L0_gnn_Wl2, L0_gnn_bl2, L0_gnn_Wr2, L1_gnn_Wq, L1_gnn_Wk, L1_gnn_Wv, L1_gnn_Wek, L1_gnn_Wev, L1_gnn_W_exp, L1_gnn_W_out):
    import jax
    import jax.numpy as jnp

    def _L0_gnn_ref(x, edge_index, Wl0, bl0, Wr0, Wl1, bl1, Wr1, Wl2, bl2, Wr2):
        import jax, jax.numpy as jnp
        import numpy as np
        N_NODES = 50000
        N_EDGES = 25000
        D_IN = 128
        D_HID = 128
        D_OUT = 128

        def _sage_conv(x, src, dst, Wl, bl, Wr):
            msg = x[src]
            summed = jax.ops.segment_sum(msg, dst, num_segments=N_NODES)
            cnt = jax.ops.segment_sum(jnp.ones((src.shape[0],), x.dtype), dst, num_segments=N_NODES)
            mean = summed / jnp.maximum(cnt, 1.0)[:, None]
            return mean @ Wl.T + bl + x @ Wr.T
        src, dst = (edge_index[0], edge_index[1])
        h = _sage_conv(x, src, dst, Wl0, bl0, Wr0)
        h = jax.nn.relu(h)
        h = _sage_conv(h, src, dst, Wl1, bl1, Wr1)
        h = jax.nn.relu(h)
        h = _sage_conv(h, src, dst, Wl2, bl2, Wr2)
        return h

    def _L1_gnn_ref(x, edges, Wq, Wk, Wv, Wek, Wev, W_exp, W_out, edge_index):
        import jax, jax.numpy as jnp
        import numpy as np
        N, E, DIM = (50000, 25000, 128)
        H, EH, HD = (8, 8, 16)
        n = x.shape[0]
        scale = HD ** (-0.5)
        src, dst = (edge_index[0], edge_index[1])
        q = (x @ Wq).reshape(n, H, HD)[src]
        k = (x @ Wk).reshape(n, H, HD)[dst]
        v_nodes = (x @ Wv).reshape(n, EH, HD)
        v = v_nodes[dst]
        ek = (edges @ Wek).reshape(-1, H, HD)
        ev = (edges @ Wev).reshape(-1, EH, HD)
        attn = jnp.einsum('ehd,ehd->eh', q, (k + ek) * scale)
        attn = attn @ W_exp
        mx = jax.ops.segment_max(attn, src, num_segments=n)
        ex = jnp.exp(attn - mx[src])
        denom = jax.ops.segment_sum(ex, src, num_segments=n)
        attn = ex / denom[src]
        out_e = attn[:, :, None] * (v + ev)
        agg = jax.ops.segment_sum(out_e, src, num_segments=n)
        out = (v_nodes - agg).reshape(n, EH * HD) @ W_out
        return out
    edge_index = jnp.stack([src, dst])
    x = _layernorm(x + _L0_gnn_ref(x, edge_index, L0_gnn_Wl0, L0_gnn_bl0, L0_gnn_Wr0, L0_gnn_Wl1, L0_gnn_bl1, L0_gnn_Wr1, L0_gnn_Wl2, L0_gnn_bl2, L0_gnn_Wr2), axis=-1)
    x = _layernorm(x + _L1_gnn_ref(x, edge_attr_128, L1_gnn_Wq, L1_gnn_Wk, L1_gnn_Wv, L1_gnn_Wek, L1_gnn_Wev, L1_gnn_W_exp, L1_gnn_W_out, edge_index), axis=-1)
    return x

_drawn_inputs = setup_inputs


def setup_inputs(seed=0):
    import zlib

    import numpy as np

    out = dict(_drawn_inputs(seed))
    spreads = {'L0_gnn_bl0': (0.0, 0.428), 'L0_gnn_bl1': (0.0, 0.1), 'L0_gnn_bl2': (0.0, 0.1)}
    factors = {'L1_gnn_Wq': 8.0, 'L1_gnn_Wk': 8.0, 'L1_gnn_Wek': 8.0, 'L1_gnn_W_exp': 8.0}
    for name, (base, spread) in spreads.items():
        noise = np.random.default_rng([zlib.crc32(name.encode()), seed]).standard_normal(out[name].shape)
        drawn = base * np.exp(spread * noise) if base else spread * noise
        out[name] = jnp.asarray(drawn.astype(out[name].dtype))
    for name, factor in factors.items():
        out[name] = (out[name] * factor).astype(out[name].dtype)
    return out
```

```python
from contextlib import ExitStack

import concourse.bass as bass
from concourse import mybir

F32 = mybir.dt.float32
I32 = mybir.dt.int32
BF16 = mybir.dt.bfloat16
ALU = mybir.AluOpType
ACT = mybir.ActivationFunctionType

P = 128
TPC = 4
CH = P * TPC
U = 8
LINE = 256
SORT = P * LINE
LOGN = SORT.bit_length() - 1
EPS = 1e-5
RESET = -1e38
FAR = float(1 << 20)


class At:

    def __init__(self, phase, j, u, last=False):
        self.phase, self.j, self.u, self.last = phase, j, u, last

    def index(self):
        return self.j * U + self.u

    def slot(self, n):
        return self.u % n

    def use(self, n):
        return self.j * (U // n) + self.u // n

    def ahead(self, k):
        u = self.u + k
        return At(self.phase, self.j, u) if not isinstance(self.j, int) else At(self.phase, self.j + u // U, u % U)


class Signal:

    def __init__(self, semaphore, name, buffers, by, phases, credit=None):
        self.n = buffers if by % 16 == 0 else 1
        self.sems = [semaphore(f"{name}{i}") for i in range(self.n)]
        self.buffers, self.by, self.phases = buffers, by, phases
        self.credit = (1 if self.n > 1 else U) if credit is None else credit

    def _had(self, phase, slot, whole):
        had = 0
        for name, chunks in self.phases:
            if name == phase and not whole:
                break
            had += -(-(chunks - slot) // self.n)
            if name == phase:
                break
        return had

    def of(self, c):
        return self.sems[c.slot(self.n)]

    def after(self, c, ago=0):
        return (c.use(self.n) + (self._had(c.phase, c.slot(self.n), False) + 1 - ago // self.n + self.credit)) * self.by

    def free(self, c):
        return self.after(c, self.buffers)

    def earlier(self, eng, c, chunks):
        for slot in range(self.n):
            had = self._had(c.phase, slot, False) + -(-(chunks - 1 - slot) // self.n)
            eng.wait_ge(self.sems[slot], (had + self.credit) * self.by)

    def end(self, eng, phase):
        for slot in range(self.n):
            eng.wait_ge(self.sems[slot], (self._had(phase, slot, True) + self.credit) * self.by)


def run(eng, phase, stages, count):
    lead = max(n for n, _ in stages)
    whole = (count - 1 - lead) // U

    def single(s):
        for n, f in stages:
            if 0 <= s + n < count:
                f(At(phase, (s + n) // U, (s + n) % U, s + n == count - 1))

    for s in range(-lead, 0):
        single(s)
    with eng.Fori(0, whole) as j:
        for u in range(U):
            for n, f in stages:
                f(At(phase, j, u + n))
    for s in range(whole * U, count):
        single(s)


def take(ap, start, n):
    return ap[start:start + n] if isinstance(start, int) else ap[bass.ds(start, n)]


def take_cols(ap, start, n):
    return ap[:, start:start + n] if isinstance(start, int) else ap[:, bass.ds(start, n)]


def by_tile(ap):
    return ap.rearrange("p (t d) -> p t d", t=TPC)


def gnn_kernel(nc, x, src, dst, ea, Wl0, bl0, Wr0, Wl1, bl1, Wr1, Wl2, bl2, Wr2,
               Wq, Wk, Wv, Wek, Wev, Wexp, Wout, out):
    N, D = x.shape
    E = src.shape[0]
    H = Wexp.shape[0]
    HD = D // H
    NC = -(-E // CH)
    NN = -(-N // CH)
    EP = NC * CH
    XW = D + 4
    HALF = N // 2
    MAG0, SRC0 = 128, 512
    assert D == P and N <= 50432 and E < 1 << 15 and EP <= SORT

    def dram(name, shape, dt=F32):
        return nc.dram_tensor(name, shape, dt, kind="Internal").ap()

    xe = dram("x_with_lookup", (N, XW))
    eae = dram("edge_attr_with_dst", (E, XW))
    xp = dram("x_prime", (N, D))
    prod_table = [dram(f"mean_product{i}", (EP + P, D)) for i in range(3)]
    key_row = [dram(f"key_row{w}", (SORT + 2,)) for w in range(2)]
    same_row = dram("same_dst_row", (SORT,))
    reset_row = dram("reset_src_row", (SORT,))

    with ExitStack() as ctx:
        def sb(name, shape, dt=F32):
            return ctx.enter_context(nc.sbuf_tensor(name, shape, dt))

        def sem(name):
            return ctx.enter_context(nc.semaphore(name))

        bank = [ctx.enter_context(nc.psum_tensor(f"bank{i}", [P, CH], F32)) for i in range(8)]

        ident = sb("ident", [P, P])
        ones = sb("ones", [P, LINE])
        eps = sb("eps", [P, 1])
        zrow = sb("zrow", [P, D])
        wraw = sb("wraw", [P, 12, D])
        wt = sb("wt", [P, 9, D])
        wexp_rows = sb("wexp_rows", [P, H])
        wexp_rep = sb("wexp_rep", [P, H, HD])
        bcol = sb("bcol", [P, 2])
        b2 = sb("b2", [3, D])
        b2part = sb("b2part", [3, 3, D], BF16)
        b2rest = sb("b2rest", [3, 2, D])
        b2mask = sb("b2mask", [3, 3, D], BF16)
        b2row = sb("b2row", [3, TPC, D], BF16)
        ones3 = sb("ones3", [3, P], BF16)
        hsrc = sb("hsrc", [P, EP])
        carved = [0]

        def part(shape, dt=F32):
            n = 1
            for k in shape:
                n *= k
            ap = hsrc[:, carved[0]:carved[0] + n]
            carved[0] += n
            names = " ".join("abcd"[:len(shape)])
            if len(shape) > 1:
                ap = ap.rearrange(f"p ({names}) -> p {names}", **dict(zip("abcd", shape[:-1])))
            return ap if dt == F32 else ap.bitcast(dt)

        kin = part([2, LINE], I32)
        pos = part([LINE], I32)
        gray = part([2, LINE], I32)
        flip = part([2, 2, LINE], I32)
        V = [part([2, LINE]) for _ in range(2)]
        work = [part([LINE], I32) for _ in range(6)]
        keyf = part([2, LINE])
        near = part([2, 2, LINE])
        same = part([LINE])
        resetf = part([LINE])
        local = part([2, LINE])
        value = part([8, LINE])
        carry_row = sb("carry_row", [1, 3, P + 1])
        carry_col = sb("carry_col", [P, 1])
        col_f = sb("col_f", [P, 2, LINE])
        col_i = sb("col_i", [P, 6, LINE], I32)
        lookup = sb("lookup", [P, LINE], I32)
        XB = part([4, TPC, XW])
        EB = part([4, TPC, XW])
        dsti = sb("dsti", [P, 4, TPC], I32)
        XN = sb("XN", [P, U, TPC, D])
        GX = sb("GX", [P, U, TPC, XW])
        idx_a = sb("idx_a", [P, U, TPC], I32)
        idx_b = sb("idx_b", [P, U, TPC], I32)
        idx_c = sb("idx_c", [P, U, TPC], I32)
        idx_d = sb("idx_d", [P, U, TPC], I32)
        lval = sb("lval", [P, U, TPC])
        flag = sb("flag", [P, 4, CH])
        h0, h1, h2 = (sb(f"h{i}", [P, 2, CH]) for i in range(3))
        seg = sb("seg", [P, 2, CH])
        prod = sb("prod", [P, 4, TPC, D])
        res = sb("res", [P, 2, TPC, D])
        normed = sb("normed", [P, 4, TPC, D])
        stats = sb("stats", [P, 2, TPC, 6])
        mv = sb("mv", [P, 2, TPC, 2])
        logv = sb("logv", [P, 2, TPC])
        rstd = sb("rstd", [P, 2, TPC])

        carved[0] = 0
        PL = part([U, 3, TPC, D])
        carved[0] = 0
        GP = part([U, TPC, D])
        GD = part([U, TPC, D])
        qk = part([CH])
        k_sb = part([CH])
        qr = part([CH])
        runmax = part([2, CH + 1])
        dmax = part([2, CH])
        decay = part([CH])
        weight = part([CH])
        den = part([2, CH])
        num = part([2, CH])
        agg = part([2, CH])

        (W_L0, W_R0, W_L1, W_R1, W_L2, W_R2, W_V, W_OUT, W_Q, W_K, W_EK, W_EV) = range(12)
        W_FILES = [Wl0, Wr0, Wl1, Wr1, Wl2, Wr2, Wv, Wout, Wq, Wk, Wek, Wev]
        T_L, T_R, T_V, T_VO, T_NOUT = (0, 2, 4), (1, 3, 5), 6, 7, 8
        V_SRC_A, V_DST_A, V_PUT_A, V_ID_B, V_SRC_B, V_PUT_B, V_POS, V_INV = range(8)

        go = sem("go")
        held = {e: sem(f"held_{e}") for e in ("sp", "pool", "dve")}
        pool_const = sem("pool_const")
        keys_loaded = sem("keys_loaded")
        w_loaded = sem("w_loaded")
        small_loaded = sem("small_loaded")
        dve_step = sem("dve_step")
        const_ready = sem("const_ready")
        w_turned = sem("w_turned")
        w_ready = sem("w_ready")
        vo_done = sem("vo_done")
        sort_step = sem("sort_step")
        turned = sem("turned")
        keys_out, near_in, rows_out = sem("keys_out"), sem("near_in"), sem("rows_out")
        keys_made, flags_made = sem("keys_made"), sem("flags_made")
        carry_turned = sem("carry_turned")
        carry_made = sem("carry_made")
        value_ready = sem("value_ready")
        value_turned = sem("value_turned")
        cols_ready = sem("cols_ready")
        zero_out = sem("zero_out")
        pad_ready = sem("pad_ready")
        all_out = sem("all_out")

        signals = []

        def signal(name, buffers, by, phases, credit=None):
            signals.append(Signal(sem, name, buffers, by, phases, credit))
            return signals[-1]

        XE, EA, LK = [("xe", NN)], [("ea", NC)], [("lk", NC)]
        xe_in, xe_out = signal("xe_in", 4, 16, XE), signal("xe_out", 4, 16, XE)
        ea_in, ea_out = signal("ea_in", 4, 32, EA), signal("ea_out", 4, 16, EA)
        ea_dst = signal("ea_dst", 4, 1, EA)
        MEANS = [(f"mean{i}", NC) for i in range(3)]
        CHAIN = [("dense", NN), ("dst", NC)]
        NODES = [("dense", NN), ("final", NN)]
        TURN = [("dense", NN), ("dst", NC), ("final", NN)]
        NORM = [("dense", NN), ("dst", NC), ("final", NN), ("attend", NC)]
        DST, ATT = [("dst", NC)], [("attend", NC)]
        POOLED = [("lk", NC), *MEANS, ("dst", NC)]
        idx_ready = signal("idx_ready", U, 1, POOLED + ATT)
        put_ready = signal("put_ready", U, 1, DST + ATT)
        lk_done = signal("lk_done", U, 64, LK, 0)
        gathered = signal("gathered", U, 64, MEANS + DST + ATT, 0)
        m_turned = signal("m_turned", 2, 1, MEANS)
        m_h = signal("m_h", 2, 1, MEANS)
        m_seg = signal("m_seg", 2, 1, MEANS)
        m_prod = signal("m_prod", 2, 1, MEANS)
        m_scaled = signal("m_scaled", 2, 1, MEANS)
        m_stored = signal("m_stored", 4, 16, MEANS)
        m_look = signal("m_look", U, 1, [("mean0", NC)])
        flag_in = signal("flag_in", 4, 16, MEANS + ATT)
        x_in = signal("x_in", U, 16, NODES)
        pl_in = signal("pl_in", U, 48, DST)
        t_done, t_kept = signal("t_done", 2, 1, TURN), signal("t_kept", 2, 1, TURN)
        u1_done, u1_kept = signal("u1_done", 2, 1, CHAIN), signal("u1_kept", 2, 1, CHAIN)
        u2_done, u2_kept = signal("u2_done", 2, 1, CHAIN), signal("u2_kept", 2, 1, CHAIN)
        y_done = signal("y_done", 2, 1, NORM)
        added0 = signal("added0", 2, 1, DST)
        added = signal("added", 2, 1, NORM)
        n_stats, n_aggr = signal("n_stats", 2, 1, NORM), signal("n_aggr", 2, 1, NORM)
        n_log, n_rstd = signal("n_log", 2, 1, NORM), signal("n_rstd", 2, 1, NORM)
        n_done = signal("n_done", 2, 1, NORM)
        x_out = signal("x_out", 4, 16, NODES)
        put_done = signal("put_done", 4, 64, DST + ATT, 0)
        put_free = signal("put_free", 4, 1, DST + ATT)
        ea_got = signal("ea_got", U, 64, ATT, 0)
        dst_got = signal("dst_got", U, 64, ATT, 0)
        dst_idx = signal("dst_idx", U, 1, ATT)
        a_turned = signal("a_turned", 1, 3, ATT)
        a_kept = signal("a_kept", 1, 3, ATT)
        a_qkv = signal("a_qkv", 1, 3, ATT)
        a_k = signal("a_k", 1, 1, ATT)
        a_qk = signal("a_qk", 1, 1, ATT)
        a_logit = signal("a_logit", 1, 1, ATT)
        a_carry = signal("a_carry", 1, 1, ATT)
        a_max = signal("a_max", 2, 1, ATT)
        a_step1 = signal("a_step1", 1, 1, ATT)
        a_dmax = signal("a_dmax", 1, 2, ATT)
        a_exp = signal("a_exp", 1, 2, ATT)
        a_den = signal("a_den", 2, 1, ATT)
        a_wv = signal("a_wv", 1, 1, ATT)
        a_num = signal("a_num", 2, 1, ATT)
        a_rden = signal("a_rden", 1, 1, ATT)
        a_agg = signal("a_agg", 2, 1, ATT)

        def hold(eng, name):
            eng.sem_inc(held[name], 1)

        def file_rows(table, rows, c):
            return take(table, rows - CH if c.last else c.index() * CH, CH).rearrange("(q t) d -> q t d", t=TPC)

        def sorted_rows(table, c):
            return take(table, c.index() * CH, CH).rearrange("(t q) d -> q t d", q=P)

        def on_all(row, c):
            return take(row, c.index() * CH, CH).rearrange("(a n) -> a n", a=1).to_broadcast([P, CH])

        plan = []
        for k in range(1, LOGN + 1):
            if k > 8:
                plan.append(("turn", 0))
            for b in range(k - 1, -1, -1):
                if k > 8 and b == 7:
                    plan.append(("turn", 0))
                plan.append(("compare", 1 << (b - 8 if b > 7 else b)))
            if k < LOGN:
                plan.append(("flip", k))

        block = ctx.enter_context(nc.Block())

        @block.sync
        def _(sp):
            for s in signals:
                for one in s.sems:
                    if s.credit:
                        sp.sem_inc(one, s.credit * s.by)
            sp.sem_inc(go, 1)
            sp.wait_ge(pad_ready, 2)
            whole = E // LINE
            for w, row in enumerate((dst, src)):
                sp.dma_start(kin[0:whole, w, :], row[0:whole * LINE].rearrange("(p f) -> p f", f=LINE)).then_inc(keys_loaded, 16)
                sp.dma_start(kin[whole:whole + 1, w, 0:E - whole * LINE], row[whole * LINE:E].rearrange("(a f) -> a f", a=1)).then_inc(keys_loaded, 16)
            for i, w in enumerate(W_FILES):
                sp.dma_start(wraw[:, i, :], w).then_inc(w_loaded, 16)
            for h in range(H):
                sp.dma_start(wexp_rows[HD * h:HD * (h + 1), :], Wexp[h:h + 1, :].to_broadcast([HD, H])).then_inc(small_loaded, 16)
            for i, b in enumerate((bl0, bl1)):
                sp.dma_start(bcol[:, i:i + 1], b.rearrange("(p a) -> p a", a=1)).then_inc(small_loaded, 16)
            sp.dma_start(b2[:, :], bl2.rearrange("(a n) -> a n", a=1).to_broadcast([3, D])).then_inc(small_loaded, 16)
            for i in range(2):
                sp.dma_start(prod_table[i][EP:EP + P, :], zrow[:, :]).then_inc(zero_out, 16)
            for w in range(2):
                for at in (0, SORT + 1):
                    sp.dma_start(key_row[w][at:at + 1].rearrange("(a n) -> a n", a=1), zrow[0:1, 0:1]).then_inc(zero_out, 16)

            def ea_load(c):
                s = c.slot(4)
                sp.wait_ge(ea_out.of(c), ea_out.free(c))
                hold(sp, "sp")
                sp.dma_start(EB[:, s, :, 0:D], file_rows(ea, E, c)).then_inc(ea_in.of(c), 16)
                sp.dma_start(dsti[:, s, :], take(dst, E - CH if c.last else c.index() * CH, CH).rearrange("(q t) -> q t", t=TPC)).then_inc(ea_in.of(c), 16)

            def ea_store(c):
                if c.last:
                    ea_out.earlier(sp, c, NC)
                sp.wait_ge(ea_in.of(c), ea_in.after(c))
                hold(sp, "sp")
                sp.wait_ge(ea_dst.of(c), ea_dst.after(c))
                hold(sp, "sp")
                sp.dma_start(file_rows(eae, E, c), EB[:, c.slot(4), :, :]).then_inc(ea_out.of(c), 16)

            run(sp, "ea", [(2, ea_load), (0, ea_store)], NC)

            sp.wait_ge(keys_made, 1)
            for w in range(2):
                sp.dma_start(key_row[w][1:SORT + 1].rearrange("(p f) -> p f", f=LINE), keyf[:, w, :]).then_inc(keys_out, 16)
            sp.wait_ge(keys_out, 32)
            sp.wait_ge(zero_out, 16 * 6)
            for w in range(2):
                for side in range(2):
                    sp.dma_start(near[:, w, side, :], key_row[w][2 * side:2 * side + SORT].rearrange("(p f) -> p f", f=LINE)).then_inc(near_in, 16)
            sp.wait_ge(flags_made, 1)
            sp.dma_start(same_row.rearrange("(p f) -> p f", f=LINE), same[:, :]).then_inc(rows_out, 16)
            sp.dma_start(reset_row.rearrange("(p f) -> p f", f=LINE), resetf[:, :]).then_inc(rows_out, 16)
            sp.wait_ge(rows_out, 32)

            def x_load(c):
                sp.wait_ge(added.of(c), added.after(c, U))
                sp.dma_start(XN[:, c.slot(U), :, :], file_rows(x if c.phase == "dense" else xp, N, c)).then_inc(x_in.of(c), 16)

            def x_store(c):
                if c.last:
                    x_out.earlier(sp, c, NN)
                sp.wait_ge(n_done.of(c), n_done.after(c))
                sp.dma_start(file_rows(xp if c.phase == "dense" else out, N, c), normed[:, c.slot(4), :, :]).then_inc(x_out.of(c), 16)

            run(sp, "dense", [(7, x_load), (0, x_store)], NN)

            def flag_load(c):
                sig = m_seg if c.phase != "attend" else a_step1
                sp.wait_ge(sig.of(c), sig.after(c, 4))
                sp.dma_start(flag[:, c.slot(4), :], on_all(reset_row if c.phase == "attend" else same_row, c)).then_inc(flag_in.of(c), 16)

            def prod_store(c):
                sp.wait_ge(m_scaled.of(c), m_scaled.after(c))
                hold(sp, "sp")
                sp.dma_start(sorted_rows(prod_table[int(c.phase[-1])], c), prod[:, c.slot(4), :, :]).then_inc(m_stored.of(c), 16)

            for i in range(3):
                run(sp, f"mean{i}", [(3, flag_load), (0, prod_store)], NC)
            m_stored.end(sp, "mean2")

            def pl_load(c):
                sp.wait_ge(u2_done.of(c), u2_done.after(c, U))
                hold(sp, "sp")
                sp.wait_ge(added.of(c), added.after(c, U))
                hold(sp, "sp")
                for i in range(3):
                    sp.dma_start(PL[:, c.slot(U), i, :, :], sorted_rows(prod_table[i], c)).then_inc(pl_in.of(c), 16)

            run(sp, "dst", [(0, pl_load)], NC)
            put_done.end(sp, "dst")
            run(sp, "final", [(7, x_load), (0, x_store)], NN)
            run(sp, "attend", [(0, flag_load)], NC)
            put_done.end(sp, "attend")
            x_out.end(sp, "final")
            sp.sem_inc(all_out, 1)

        @block.gpsimd
        def _(pool):
            pool.wait_ge(go, 1)
            pool.memset(ident[:, :], 0.0).then_inc(pool_const, 1)
            pool.wait_ge(pool_const, 1)
            pool.affine_select(out=ident[:, :], in_=ident[:, :], compare_op=ALU.not_equal, fill=1.0, base=0,
                               pattern=[[-1, P]], channel_multiplier=1).then_inc(pool_const, 1)
            pool.iota(pos[:, :], pattern=[[1, LINE]], base=0, channel_multiplier=LINE).then_inc(pool_const, 1)
            for s in range(4):
                pool.memset(XB[:, s, :, D:XW], float(EP)).then_inc(pool_const, 1)
                pool.memset(EB[:, s, :, D:XW], 0.0).then_inc(pool_const, 1)
            pool.wait_ge(pool_const, 11)

            def ea_fill(c):
                s = c.slot(4)
                pool.wait_ge(ea_in.of(c), ea_in.after(c))
                hold(pool, "pool")
                pool.tensor_copy(EB[:, s, :, D:D + 1], dsti[:, s, :].rearrange("p (t a) -> p t a", a=1)).then_inc(ea_dst.of(c), 1)

            run(pool, "ea", [(0, ea_fill)], NC)

            def stage(ap, signal_, buf):
                def f(c):
                    pool.tensor_copy(buf[:, c.slot(U), :], take_cols(ap, c.index() * TPC, TPC)).then_inc(signal_.of(c), 1)
                return f

            def gather(buf, table, idx, width, c, sig):
                for t in range(TPC):
                    pool.indirect_dma_start(buf[:, c.slot(U), t, 0:width], None, table,
                                            bass.IndirectOffsetOnAxis(ap=idx[:, c.slot(U), t:t + 1], axis=0)).then_inc(sig.of(c), 16)

            pool.wait_ge(cols_ready, 1)
            pool.wait_ge(rows_out, 32)
            xe_out.end(pool, "xe")

            def lk_stage(c):
                pool.tensor_copy(lval[:, c.slot(U), :], take_cols(col_f[:, 0, :], c.index() * TPC, TPC))
                pool.tensor_copy(idx_a[:, c.slot(U), :], take_cols(col_i[:, V_PUT_A, :], c.index() * TPC, TPC)).then_inc(idx_ready.of(c), 1)

            def lk_put(c):
                pool.wait_ge(idx_ready.of(c), idx_ready.after(c))
                hold(pool, "pool")
                for t in range(TPC):
                    pool.indirect_dma_start(xe, bass.IndirectOffsetOnAxis(ap=idx_a[:, c.slot(U), t:t + 1], axis=0),
                                            lval[:, c.slot(U), t:t + 1], None, element_offset=D,
                                            bounds_check=N - 1, oob_is_err=False).then_inc(lk_done.of(c), 16)

            def lk_settle(c):
                pool.wait_ge(lk_done.of(c), lk_done.after(c))
                hold(pool, "pool")

            run(pool, "lk", [(0, lk_settle), (7, lk_stage), (6, lk_put)], NC)
            lk_done.end(pool, "lk")

            def mean_stage(c):
                pool.wait_ge(m_turned.of(c), m_turned.after(c, U))
                cols = col_i[:, V_SRC_A, :] if c.phase == "mean0" else lookup[:, :]
                pool.tensor_copy(idx_a[:, c.slot(U), :], take_cols(cols, c.index() * TPC, TPC)).then_inc(idx_ready.of(c), 1)

            def mean_gather(c):
                pool.wait_ge(idx_ready.of(c), idx_ready.after(c))
                pool.wait_ge(m_turned.of(c), m_turned.after(c, U))
                if c.phase == "mean0":
                    pool.wait_ge(m_look.of(c), m_look.free(c))
                hold(pool, "pool")
                if c.phase == "mean0":
                    gather(GX, xe, idx_a, XW, c, gathered)
                else:
                    gather(GX, prod_table[int(c.phase[-1]) - 1], idx_a, D, c, gathered)

            for i in range(3):
                if i:
                    m_look.end(pool, "mean0")
                    m_stored.end(pool, f"mean{i - 1}")
                    pool.wait_ge(zero_out, 16 * 6)
                run(pool, f"mean{i}", [(1, mean_stage), (0, mean_gather)], NC)

            def dst_stage(c):
                pool.wait_ge(t_done.of(c), t_done.after(c, U))
                hold(pool, "pool")
                pool.tensor_copy(idx_a[:, c.slot(U), :], take_cols(col_i[:, V_DST_A, :], c.index() * TPC, TPC)).then_inc(idx_ready.of(c), 1)

            def dst_gather(c):
                pool.wait_ge(idx_ready.of(c), idx_ready.after(c))
                pool.wait_ge(added.of(c), added.after(c, U))
                hold(pool, "pool")
                gather(GX, x, idx_a, D, c, gathered)

            def put_stage(c):
                cols = col_i[:, V_PUT_A if c.phase == "dst" else V_PUT_B, :]
                pool.tensor_copy(idx_b[:, c.slot(U), :], take_cols(cols, c.index() * TPC, TPC)).then_inc(put_ready.of(c), 1)

            def put(c):
                pool.wait_ge(put_ready.of(c), put_ready.after(c))
                pool.wait_ge(n_done.of(c), n_done.after(c))
                hold(pool, "pool")
                for t in range(TPC):
                    pool.indirect_dma_start(xp if c.phase == "dst" else out,
                                            bass.IndirectOffsetOnAxis(ap=idx_b[:, c.slot(U), t:t + 1], axis=0),
                                            normed[:, c.slot(4), t, :], None,
                                            bounds_check=N - 1, oob_is_err=False).then_inc(put_done.of(c), 16)

            def settle(c):
                pool.wait_ge(put_done.of(c), put_done.after(c))
                hold(pool, "pool")
                pool.sem_inc(put_free.of(c), 1)

            m_turned.end(pool, "mean2")
            x_out.end(pool, "dense")
            run(pool, "dst", [(8, dst_stage), (7, dst_gather), (2, put_stage), (1, put), (0, settle)], NC)
            put_done.end(pool, "dst")
            ea_out.end(pool, "ea")

            def att_stage(c):
                pool.wait_ge(a_turned.of(c), a_turned.after(c, U))
                hold(pool, "pool")
                pool.tensor_copy(idx_c[:, c.slot(U), :], take_cols(col_i[:, V_SRC_B, :], c.index() * TPC, TPC))
                pool.tensor_copy(idx_a[:, c.slot(U), :], take_cols(col_i[:, V_ID_B, :], c.index() * TPC, TPC)).then_inc(idx_ready.of(c), 1)

            def att_gather(c):
                pool.wait_ge(idx_ready.of(c), idx_ready.after(c))
                pool.wait_ge(a_turned.of(c), a_turned.after(c, U))
                pool.wait_ge(dst_idx.of(c), dst_idx.free(c))
                pool.wait_ge(added.of(c), added.after(c, U))
                hold(pool, "pool")
                gather(GX, eae, idx_a, XW, c, ea_got)
                gather(GP, xp, idx_c, D, c, gathered)

            def att_dst(c):
                pool.wait_ge(ea_got.of(c), ea_got.after(c))
                pool.wait_ge(a_turned.of(c), a_turned.after(c, U))
                hold(pool, "pool")
                pool.tensor_copy(idx_d[:, c.slot(U), :], GX[:, c.slot(U), :, D:D + 1].rearrange("p t a -> p (t a)")).then_inc(dst_idx.of(c), 1)
                pool.wait_ge(dst_idx.of(c), dst_idx.after(c))
                pool.wait_ge(a_turned.of(c), a_turned.after(c, U))
                hold(pool, "pool")
                gather(GD, xp, idx_d, D, c, dst_got)

            x_out.end(pool, "final")
            run(pool, "attend", [(9, att_stage), (8, att_gather), (6, att_dst), (2, put_stage), (1, put), (0, settle)], NC)
            put_done.end(pool, "attend")

        @block.tensor
        def _(pe):
            def turn_in(dst, src):
                return pe.transpose(dst, src, ident[0:src.shape[0], 0:src.shape[0]])

            pe.wait_ge(pool_const, 11)
            pe.wait_ge(w_loaded, 16 * len(W_FILES))
            for i in range(7):
                turn_in(bank[2 + i // 4][:, i % 4 * P:(i % 4 + 1) * P], wraw[:, i, :]).then_inc(w_turned, 1)
            pe.wait_ge(w_ready, 1)
            pe.matmul(bank[4][:, 0:D], wt[:, T_V, :], wraw[:, W_OUT, :], start=True, stop=True).then_inc(vo_done, 1)

            steps = turns = side = 0
            for what, _ in plan:
                if what != "turn":
                    steps += 1
                    side ^= what == "compare"
                    continue
                pe.wait_ge(sort_step, 2 * steps + 2)
                for i in range(4):
                    last = turn_in(bank[turns % 2][:, i * P:(i + 1) * P],
                                   V[side][:, :, :].rearrange("p w f -> p (w f)")[:, i * P:(i + 1) * P])
                last.then_inc(turned, 1)
                turns += 1
            pe.wait_ge(carry_made, 1)
            for i in range(2):
                turn_in(bank[2 + i][0:1, 0:P], local[:, i, LINE - 1:LINE]).then_inc(carry_turned, 1)
            pe.wait_ge(carry_made, 2)
            turn_in(bank[4][:, 0:1], carry_row[0:1, 2, 0:P]).then_inc(carry_turned, 1)
            pe.wait_ge(value_ready, 1)
            for i in range(8):
                for a in range(2):
                    last = turn_in(bank[i][:, a * P:(a + 1) * P], value[:, i, a * P:(a + 1) * P])
                last.then_inc(value_turned, 1)
            pe.wait_ge(cols_ready, 1)

            def rows_turned(rows, c):
                pe.wait_ge(t_kept.of(c), t_kept.free(c))
                for t in range(TPC):
                    last = turn_in(bank[c.slot(2)][:, t * P:(t + 1) * P], rows[:, c.slot(U), t, 0:D])
                last.then_inc(t_done.of(c), 1)

            def chain_t(c):
                if c.phase == "dst":
                    pe.wait_ge(gathered.of(c), gathered.after(c))
                    rows_turned(GX, c)
                else:
                    pe.wait_ge(x_in.of(c), x_in.after(c))
                    rows_turned(XN, c)

            def layer(i, c, psum, before, kept_before, done, kept):
                pe.wait_ge(kept_before.of(c), kept_before.after(c))
                pe.wait_ge(kept.of(c), kept.free(c))
                dst_phase = c.phase == "dst"
                last = pe.matmul(psum[:, :], wt[:, T_R[i], :], before[:, c.slot(2), :], start=True, stop=not dst_phase)
                if dst_phase:
                    pe.wait_ge(pl_in.of(c), pl_in.after(c))
                    for t in range(TPC):
                        last = pe.matmul(psum[:, t * P:(t + 1) * P], PL[:, c.slot(U), i, t, :], ident[:, :],
                                         start=False, stop=t == TPC - 1)
                last.then_inc(done.of(c), 1)

            def chain_1(c):
                layer(0, c, bank[2 + c.slot(2)], h0, t_kept, u1_done, u1_kept)

            def chain_2(c):
                layer(1, c, bank[4 + c.slot(2)], h1, u1_kept, u2_done, u2_kept)

            def chain_y(c):
                pe.wait_ge(u2_kept.of(c), u2_kept.after(c))
                pe.wait_ge(added.of(c), added.free(c))
                y = bank[6 + c.slot(2)]
                pe.matmul(y[:, :], ones3[:, :], b2row[:, :, :].rearrange("k t d -> k (t d)"), start=True, stop=False)
                for t in range(TPC):
                    last = pe.matmul(y[:, t * P:(t + 1) * P], h2[:, c.slot(2), t * P:(t + 1) * P], wt[:, T_R[2], :],
                                     start=False, stop=t == TPC - 1)
                last.then_inc(y_done.of(c), 1)

            chain = [(3, chain_t), (2, chain_1), (1, chain_2), (0, chain_y)]
            run(pe, "dense", chain, NN)
            added.end(pe, "dense")

            def mean_turn(c):
                pe.wait_ge(gathered.of(c), gathered.after(c))
                pe.wait_ge(m_h.of(c), m_h.free(c))
                psum = bank[c.slot(2)]
                if c.phase == "mean0":
                    for t in range(TPC):
                        last = turn_in(psum[:, t * P:(t + 1) * P], GX[:, c.slot(U), t, 0:D])
                else:
                    i = int(c.phase[-1]) - 1
                    pe.matmul(psum[:, :], wt[:, T_R[i], :], take_cols(hsrc, c.index() * CH, CH), start=True, stop=False)
                    for t in range(TPC):
                        last = pe.matmul(psum[:, t * P:(t + 1) * P], GX[:, c.slot(U), t, 0:D], ident[:, :],
                                         start=False, stop=t == TPC - 1)
                last.then_inc(m_turned.of(c), 1)

            def mean_prod(c):
                pe.wait_ge(m_seg.of(c), m_seg.after(c))
                pe.wait_ge(m_scaled.of(c), m_scaled.free(c))
                for t in range(TPC):
                    last = pe.matmul(bank[2 + c.slot(2)][:, t * P:(t + 1) * P], seg[:, c.slot(2), t * P:(t + 1) * P],
                                     wt[:, T_L[int(c.phase[-1])], :], start=True, stop=True)
                last.then_inc(m_prod.of(c), 1)

            for i in range(3):
                run(pe, f"mean{i}", [(1, mean_turn), (0, mean_prod)], NC)
                m_h.end(pe, f"mean{i}")
            m_scaled.end(pe, "mean2")

            run(pe, "dst", chain, NC)
            added.end(pe, "dst")

            def final_t(c):
                pe.wait_ge(x_in.of(c), x_in.after(c))
                rows_turned(XN, c)

            def final_y(c):
                pe.wait_ge(t_kept.of(c), t_kept.after(c))
                pe.wait_ge(added.of(c), added.free(c))
                for t in range(TPC):
                    last = pe.matmul(bank[6 + c.slot(2)][:, t * P:(t + 1) * P], h0[:, c.slot(2), t * P:(t + 1) * P],
                                     wt[:, T_VO, :], start=True, stop=True)
                last.then_inc(y_done.of(c), 1)

            run(pe, "final", [(1, final_t), (0, final_y)], NN)
            t_kept.end(pe, "final")
            added.end(pe, "final")

            def att_turn(c):
                for i, (rows, sig) in enumerate(((GX, ea_got), (GP, gathered), (GD, dst_got))):
                    pe.wait_ge(sig.of(c), sig.after(c))
                    if i < 2:
                        pe.wait_ge(a_kept.of(c), a_kept.after(c, 1) - 1 + i)
                    else:
                        pe.wait_ge(a_kept.of(c), a_kept.after(c) - 2)
                    for t in range(TPC):
                        last = turn_in(bank[(3 * c.u + i) % 2][:, t * P:(t + 1) * P], rows[:, c.slot(U), t, 0:D])
                    last.then_inc(a_turned.of(c), 1)

            def att_qkv(c):
                s = c.slot(2)
                pe.wait_ge(a_kept.of(c), a_kept.after(c))
                pe.wait_ge(a_qk.of(c), a_qk.free(c))
                pe.matmul(bank[2][:, :], wraw[:, W_Q, :], XN[:, c.slot(U), :, :].rearrange("p t d -> p (t d)"),
                          start=True, stop=True).then_inc(a_qkv.of(c), 1)
                pe.matmul(bank[3][:, :], wraw[:, W_K, :], h2[:, s, :], start=True, stop=False)
                pe.matmul(bank[3][:, :], wraw[:, W_EK, :], h0[:, s, :], start=False, stop=True).then_inc(a_qkv.of(c), 1)
                pe.wait_ge(a_wv.of(c), a_wv.free(c))
                pe.matmul(bank[4][:, :], wraw[:, W_V, :], h2[:, s, :], start=True, stop=False)
                pe.matmul(bank[4][:, :], wraw[:, W_EV, :], h0[:, s, :], start=False, stop=True).then_inc(a_qkv.of(c), 1)

            def att_logit(c):
                pe.wait_ge(a_qk.of(c), a_qk.after(c))
                pe.wait_ge(a_dmax.of(c), a_dmax.free(c))
                pe.matmul(bank[5][:, :], wexp_rep[:, :, :].rearrange("p h d -> p (h d)"), qk[:, :],
                          start=True, stop=True).then_inc(a_logit.of(c), 1)

            def att_y(c):
                pe.wait_ge(a_agg.of(c), a_agg.after(c))
                pe.wait_ge(added.of(c), added.free(c))
                y = bank[6 + c.slot(2)]
                for t in range(TPC):
                    pe.matmul(y[:, t * P:(t + 1) * P], XN[:, c.slot(U), t, :], wt[:, T_VO, :], start=True, stop=False)
                    last = pe.matmul(y[:, t * P:(t + 1) * P], agg[:, c.slot(2), t * P:(t + 1) * P], wt[:, T_NOUT, :],
                                     start=False, stop=True)
                last.then_inc(y_done.of(c), 1)

            run(pe, "attend", [(2, att_turn), (1, att_qkv), (1, att_logit), (0, att_y)], NC)

        @block.scalar
        def _(act):
            act.preload_act_table_set("natural_log_exp_and_others")
            act.wait_ge(go, 1)
            act.wait_ge(pool_const, 11)

            def xe_load(c):
                act.wait_ge(xe_out.of(c), xe_out.free(c))
                act.dma_start(XB[:, c.slot(4), :, 0:D], file_rows(x, N, c)).then_inc(xe_in.of(c), 16)

            def xe_store(c):
                if c.last:
                    xe_out.earlier(act, c, NN)
                act.wait_ge(xe_in.of(c), xe_in.after(c))
                act.dma_start(file_rows(xe, N, c), XB[:, c.slot(4), :, :]).then_inc(xe_out.of(c), 16)

            run(act, "xe", [(2, xe_load), (0, xe_store)], NN)
            act.wait_ge(cols_ready, 1)

            def keep_t(c):
                act.wait_ge(t_done.of(c), t_done.after(c))
                if c.phase == "final":
                    act.wait_ge(y_done.of(c), y_done.free(c))
                else:
                    act.wait_ge(u1_done.of(c), u1_done.free(c))
                act.activation(h0[:, c.slot(2), :], bank[c.slot(2)][:, :], ACT.Copy).then_inc(t_kept.of(c), 1)

            def keep_1(c):
                act.wait_ge(u1_done.of(c), u1_done.after(c))
                act.wait_ge(u2_done.of(c), u2_done.free(c))
                act.activation(h1[:, c.slot(2), :], bank[2 + c.slot(2)][:, :], ACT.Relu, bias=bcol[:, 0:1]).then_inc(u1_kept.of(c), 1)

            def keep_2(c):
                act.wait_ge(u2_done.of(c), u2_done.after(c))
                act.wait_ge(y_done.of(c), y_done.free(c))
                act.activation(h2[:, c.slot(2), :], bank[4 + c.slot(2)][:, :], ACT.Relu, bias=bcol[:, 1:2]).then_inc(u2_kept.of(c), 1)

            def inverse_root(c):
                s = c.slot(2)
                act.wait_ge(n_aggr.of(c), n_aggr.after(c))
                act.activation(logv[:, s, :], mv[:, s, :, 1], ACT.Ln, bias=eps[:, 0:1]).then_inc(n_log.of(c), 1)
                act.wait_ge(n_log.of(c), n_log.after(c))
                act.wait_ge(n_done.of(c), n_done.free(c))
                act.activation(rstd[:, s, :], logv[:, s, :], ACT.Exp, scale=-0.5).then_inc(n_rstd.of(c), 1)

            chain = [(3, keep_t), (2, keep_1), (1, keep_2), (0, inverse_root)]
            run(act, "dense", chain, NN)

            def mean_keep(c):
                act.wait_ge(m_turned.of(c), m_turned.after(c))
                i = int(c.phase[-1])
                h = take_cols(hsrc, c.index() * CH, CH)
                if i == 0:
                    act.activation(h, bank[c.slot(2)][:, :], ACT.Copy).then_inc(m_h.of(c), 1)
                else:
                    act.activation(h, bank[c.slot(2)][:, :], ACT.Relu, bias=bcol[:, i - 1:i]).then_inc(m_h.of(c), 1)

            for i in range(3):
                if i:
                    m_seg.end(act, f"mean{i - 1}")
                run(act, f"mean{i}", [(0, mean_keep)], NC)
            y_done.end(act, "dense")
            run(act, "dst", chain, NC)
            y_done.end(act, "dst")
            run(act, "final", [(1, keep_t), (0, inverse_root)], NN)
            y_done.end(act, "final")

            def att_keep(c):
                ring = c.u * 3
                act.wait_ge(a_turned.of(c), a_turned.after(c) - 2)
                act.wait_ge(a_qkv.of(c), a_qkv.after(c, 2))
                act.activation(h0[:, c.slot(2), :], bank[ring % 2][:, :], ACT.Copy).then_inc(a_kept.of(c), 1)
                act.wait_ge(a_turned.of(c), a_turned.after(c) - 1)
                act.wait_ge(y_done.of(c), y_done.after(c, U))
                act.activation(XN[:, c.slot(U), :, :].rearrange("p t d -> p (t d)"), bank[(ring + 1) % 2][:, :],
                               ACT.Copy).then_inc(a_kept.of(c), 1)
                act.wait_ge(a_turned.of(c), a_turned.after(c))
                act.activation(h2[:, c.slot(2), :], bank[ring % 2][:, :], ACT.Copy).then_inc(a_kept.of(c), 1)

            def att_k(c):
                act.wait_ge(a_qkv.of(c), a_qkv.after(c) - 1)
                act.wait_ge(a_qk.of(c), a_qk.free(c))
                act.activation(k_sb[:, :], bank[3][:, :], ACT.Copy).then_inc(a_k.of(c), 1)

            def att_exp(c):
                act.wait_ge(a_dmax.of(c), a_dmax.after(c) - 1)
                act.wait_ge(a_num.of(c), a_num.after(c, 1))
                act.activation(decay[:, :], dmax[:, 0, :], ACT.Exp).then_inc(a_exp.of(c), 1)
                act.wait_ge(a_dmax.of(c), a_dmax.after(c))
                act.activation(weight[:, :], dmax[:, 1, :], ACT.Exp).then_inc(a_exp.of(c), 1)

            run(act, "attend", [(2, att_keep), (1, att_k), (1, att_exp), (0, inverse_root)], NC)

        @block.vector
        def _(dve):
            done = [0]

            def link(ins):
                done[0] += 1
                ins.then_inc(dve_step, 1)
                dve.wait_ge(dve_step, done[0])

            dve.memset(kin[:, :, :], N).then_inc(pad_ready, 1)
            dve.memset(zrow[:, :], 0.0).then_inc(pad_ready, 1)
            link(dve.memset(ones[:, :], 1.0))
            link(dve.memset(ones3[:, :], 1.0))
            link(dve.memset(eps[:, :], EPS))
            link(dve.memset(carry_row[:, :, :], 0.0))
            link(dve.memset(seg[:, :, :], 0.0))

            dve.wait_ge(w_turned, 7)
            link(dve.tensor_copy(wt[:, 0:4, :], by_tile(bank[2][:, :])))
            dve.tensor_copy(wt[:, 4:7, :], bank[3][:, 0:3 * P].rearrange("p (t d) -> p t d", t=3)).then_inc(w_ready, 1)
            dve.wait_ge(w_ready, 1)
            dve.wait_ge(vo_done, 1)
            link(dve.tensor_copy(wt[:, T_VO, :], bank[4][:, 0:D]))
            link(dve.tensor_scalar(wt[:, T_NOUT, :], wraw[:, W_OUT, :], -1.0, None, ALU.mult))
            dve.wait_ge(small_loaded, 16 * (H + 3))
            link(dve.tensor_scalar(wexp_rep[:, :, :], wexp_rows[:, :].rearrange("p (h a) -> p h a", a=1).to_broadcast([P, H, HD]),
                                   float(HD) ** -0.5, None, ALU.mult))
            link(dve.tensor_copy(b2part[:, 0, :], b2[:, :]))
            link(dve.tensor_tensor(b2rest[:, 0, :], b2[:, :], b2part[:, 0, :], ALU.subtract))
            link(dve.tensor_copy(b2part[:, 1, :], b2rest[:, 0, :]))
            link(dve.tensor_tensor(b2rest[:, 1, :], b2rest[:, 0, :], b2part[:, 1, :], ALU.subtract))
            link(dve.tensor_copy(b2part[:, 2, :], b2rest[:, 1, :]))
            for i in range(3):
                link(dve.tensor_scalar(b2mask[:, i, :], b2part[:, i, :], ident[0:3, i:i + 1], None, ALU.mult))
            link(dve.tensor_tensor(b2mask[:, 0, :], b2mask[:, 0, :], b2mask[:, 1, :], ALU.add))
            link(dve.tensor_tensor(b2mask[:, 0, :], b2mask[:, 0, :], b2mask[:, 2, :], ALU.add))
            for t in range(TPC):
                link(dve.tensor_copy(b2row[:, t, :], b2mask[:, 0, :]))

            w = [one[:, :] for one in work]
            a_bits, b_bits = V[0][:, 0, :].bitcast(I32), V[0][:, 1, :].bitcast(I32)
            dve.wait_ge(keys_loaded, 64)
            dst_k, src_k = kin[:, 0, :], kin[:, 1, :]
            link(dve.tensor_scalar(w[0], dst_k, float(HALF), None, ALU.is_lt))
            link(dve.tensor_scalar(w[1], dst_k, -float(HALF), None, ALU.add))
            link(dve.tensor_scalar(w[2], w[0], -2.0, 1.0, ALU.mult, ALU.add))
            link(dve.tensor_tensor(w[1], w[1], w[2], ALU.mult))
            link(dve.tensor_scalar(w[1], w[1], float(MAG0), None, ALU.add))
            link(dve.tensor_scalar(w[1], w[1], 16, None, ALU.logical_shift_left))
            link(dve.tensor_scalar(w[0], w[0], 31, None, ALU.logical_shift_left))
            link(dve.tensor_tensor(w[1], w[1], w[0], ALU.bitwise_or))
            link(dve.tensor_tensor(a_bits, w[1], src_k, ALU.bitwise_or))
            link(dve.tensor_scalar(w[3], src_k, float(SRC0), None, ALU.add))
            link(dve.tensor_scalar(w[3], w[3], 15, None, ALU.logical_shift_left))
            link(dve.tensor_tensor(b_bits, w[3], pos[:, :], ALU.bitwise_or))
            link(dve.tensor_scalar(w[4], pos[:, :], 1, None, ALU.logical_shift_right))
            for i in range(2):
                link(dve.tensor_tensor(gray[:, i, :], pos[:, :], w[4], ALU.bitwise_xor))
                link(dve.tensor_scalar(flip[:, 0, i, :], w[4], 31, None, ALU.logical_shift_left))
            all_bits = V[0][:, :, :].bitcast(I32)
            dve.tensor_tensor(all_bits, all_bits, flip[:, 0, :, :], ALU.bitwise_xor).then_inc(sort_step, 2)

            steps = turns = side = 0
            in_psum = False
            flat = [one[:, :, :].rearrange("p w f -> p (w f)") for one in V]
            now = flat[0]
            for what, n in plan:
                if what == "turn":
                    turns += 1
                    dve.wait_ge(turned, turns)
                    now = bank[(turns - 1) % 2][:, :]
                    in_psum = True
                    continue
                if what == "flip":
                    one = flip[:, n % 2, :, :]
                    link(dve.tensor_scalar(one, gray[:, :, :], n, None, ALU.logical_shift_right))
                    link(dve.tensor_scalar(one, one, 31, None, ALU.logical_shift_left))
                    dve.wait_ge(sort_step, 2 * steps + 2)
                    bits = V[side][:, :, :].bitcast(I32)
                    dve.tensor_tensor(bits, bits, one, ALU.bitwise_xor).then_inc(sort_step, 2)
                    steps += 1
                    continue
                pairs = now.rearrange("p (g two s) -> p g two s", two=2, s=n)
                upper = pairs[:, :, 1, :]
                if in_psum:
                    upper = flat[side].rearrange("p (g two s) -> p g two s", two=2, s=n)[:, :, 1, :]
                    link(dve.tensor_copy(upper, pairs[:, :, 1, :]))
                    in_psum = False
                side ^= 1
                to = flat[side].rearrange("p (g two s) -> p g two s", two=2, s=n)
                dve.wait_ge(sort_step, 2 * steps + 2)
                dve.tensor_tensor(to[:, :, 0, :], pairs[:, :, 0, :], upper, ALU.min).then_inc(sort_step, 1)
                dve.tensor_tensor(to[:, :, 1, :], pairs[:, :, 0, :], upper, ALU.max).then_inc(sort_step, 1)
                steps += 1
                now = flat[side]
            dve.wait_ge(sort_step, 2 * steps + 2)

            va, vb = V[side][:, 0, :].bitcast(I32), V[side][:, 1, :].bitcast(I32)
            for i, (v, n) in enumerate(((va, 16), (vb, 15))):
                link(dve.tensor_scalar(w[i], v, n, None, ALU.logical_shift_right))
                link(dve.tensor_scalar(keyf[:, i, :].bitcast(I32), w[i], n, None, ALU.logical_shift_left))
            dve.memset(work[5][:, 0:1], 0.0).then_inc(keys_made, 1)
            link(dve.tensor_scalar(w[2], va, 31, None, ALU.logical_shift_right))
            link(dve.tensor_scalar(w[2], w[2], 1, None, ALU.bitwise_and))
            link(dve.tensor_scalar(w[2], w[2], -2.0, 1.0, ALU.mult, ALU.add))
            link(dve.tensor_scalar(w[0], w[0], 0x7FFF, None, ALU.bitwise_and))
            link(dve.tensor_scalar(w[0], w[0], -float(MAG0), None, ALU.add))
            link(dve.tensor_tensor(w[0], w[0], w[2], ALU.mult))
            link(dve.tensor_scalar(w[0], w[0], float(HALF), None, ALU.add))
            link(dve.tensor_scalar(w[3], va, 0xFFFF, None, ALU.bitwise_and))
            link(dve.tensor_scalar(w[1], w[1], -float(SRC0), None, ALU.add))
            link(dve.tensor_scalar(w[4], vb, 0x7FFF, None, ALU.bitwise_and))
            for to, v, most in ((V_SRC_A, w[3], N - 1), (V_DST_A, w[0], N - 1), (V_ID_B, w[4], E - 1), (V_SRC_B, w[1], N - 1)):
                link(dve.tensor_scalar(value[:, to, :], v, float(most), None, ALU.min))
            link(dve.tensor_copy(value[:, V_POS, :], pos[:, :]))
            dve.wait_ge(near_in, 64)
            link(dve.tensor_tensor(same[:, :], keyf[:, 0, :], near[:, 0, 0, :], ALU.is_equal))
            link(dve.tensor_tensor(resetf[:, :], keyf[:, 1, :], near[:, 1, 0, :], ALU.not_equal))
            dve.tensor_scalar(resetf[:, :], resetf[:, :], RESET, None, ALU.mult).then_inc(flags_made, 1)
            for i, (to, v) in enumerate(((V_PUT_A, w[0]), (V_PUT_B, w[1]))):
                link(dve.tensor_tensor(near[:, i, 1, :], keyf[:, i, :], near[:, i, 1, :], ALU.is_equal))
                link(dve.tensor_scalar(near[:, i, 1, :], near[:, i, 1, :], FAR, None, ALU.mult))
                link(dve.tensor_tensor(value[:, to, :], near[:, i, 1, :], v, ALU.add))
            link(dve.tensor_tensor_scan(local[:, 0, :], same[:, :], ones[:, :], 0.0, ALU.mult, ALU.add))
            dve.tensor_tensor_scan(local[:, 1, :], same[:, :], ones[:, :], 1.0, ALU.mult, ALU.mult).then_inc(carry_made, 1)
            dve.wait_ge(carry_turned, 2)
            for i in range(2):
                link(dve.tensor_copy(carry_row[0:1, i, 0:P], bank[2 + i][0:1, 0:P]))
            dve.tensor_tensor_scan(carry_row[0:1, 2, 1:P + 1], carry_row[0:1, 1, 0:P], carry_row[0:1, 0, 0:P], 0.0,
                                   ALU.mult, ALU.add).then_inc(carry_made, 1)
            dve.wait_ge(carry_turned, 3)
            link(dve.tensor_copy(carry_col[:, :], bank[4][:, 0:1]))
            link(dve.tensor_scalar(local[:, 1, :], local[:, 1, :], carry_col[:, 0:1], None, ALU.mult))
            link(dve.tensor_tensor(local[:, 0, :], local[:, 0, :], local[:, 1, :], ALU.add))
            dve.reciprocal(value[:, V_INV, :], local[:, 0, :]).then_inc(value_ready, 1)
            for i in range(8):
                dve.wait_ge(value_turned, i + 1)
                to = col_i[:, i, :] if i < 6 else col_f[:, i - 6, :]
                link(dve.tensor_copy(to.rearrange("q (p a) -> q a p", a=2), bank[i][:, 0:LINE].rearrange("q (a p) -> q a p", a=2)))
            dve.memset(work[5][:, 0:1], 0.0).then_inc(cols_ready, 1)

            def add(rows, c):
                s = c.slot(2)
                y = by_tile(bank[6 + s][:, :])
                dve.wait_ge(y_done.of(c), y_done.after(c))
                dve.wait_ge(n_done.of(c), n_done.free(c))
                if c.phase == "dst":
                    dve.tensor_tensor(res[:, s, :, :], y, rows, ALU.add).then_inc(added0.of(c), 1)
                    dve.wait_ge(added0.of(c), added0.after(c))
                    dve.wait_ge(pl_in.of(c), pl_in.after(c))
                    dve.tensor_tensor(res[:, s, :, :], res[:, s, :, :], PL[:, c.slot(U), 2, :, :], ALU.add).then_inc(added.of(c), 1)
                else:
                    dve.tensor_tensor(res[:, s, :, :], y, rows, ALU.add).then_inc(added.of(c), 1)
                dve.wait_ge(added.of(c), added.after(c))
                for t in range(TPC):
                    last = dve.bn_stats(stats[:, s, t, :], res[:, s, t, :])
                last.then_inc(n_stats.of(c), 1)
                dve.wait_ge(n_stats.of(c), n_stats.after(c))
                hold(dve, "dve")
                for t in range(TPC):
                    last = dve.bn_aggr(mv[:, s, t, :], stats[:, s, t, :])
                last.then_inc(n_aggr.of(c), 1)

            def norm(c):
                s = c.slot(2)
                dve.wait_ge(n_rstd.of(c), n_rstd.after(c))
                if c.phase in ("dst", "attend"):
                    dve.wait_ge(put_free.of(c), put_free.free(c))
                else:
                    dve.wait_ge(x_out.of(c), x_out.free(c))
                for t in range(TPC):
                    last = dve.tensor_scalar(normed[:, c.slot(4), t, :], res[:, s, t, :], mv[:, s, t, 0:1],
                                             rstd[:, s, t:t + 1], ALU.subtract, ALU.mult)
                last.then_inc(n_done.of(c), 1)

            def add_x(c):
                add(XN[:, c.slot(U), :, :], c)

            def add_gathered(c):
                add(GX[:, c.slot(U), :, 0:D], c)

            run(dve, "dense", [(1, add_x), (0, norm)], NN)

            def mean_seg(c):
                dve.wait_ge(m_h.of(c), m_h.after(c))
                dve.wait_ge(flag_in.of(c), flag_in.after(c))
                dve.wait_ge(m_prod.of(c), m_prod.free(c))
                before = c.ahead(-1)
                dve.wait_ge(m_seg.of(before), m_seg.after(before))
                dve.tensor_tensor_scan(seg[:, c.slot(2), :], flag[:, c.slot(4), :], take_cols(hsrc, c.index() * CH, CH),
                                       seg[:, before.slot(2), CH - 1:CH], ALU.mult, ALU.add).then_inc(m_seg.of(c), 1)
                if c.phase == "mean0":
                    dve.wait_ge(gathered.of(c), gathered.after(c))
                    dve.tensor_copy(take_cols(lookup, c.index() * TPC, TPC), GX[:, c.slot(U), :, D:D + 1].rearrange("p t a -> p (t a)"))\
                       .then_inc(m_look.of(c), 1)

            def mean_scale(c):
                dve.wait_ge(m_prod.of(c), m_prod.after(c))
                dve.wait_ge(m_stored.of(c), m_stored.free(c))
                inv = take_cols(col_f[:, 1, :], c.index() * TPC, TPC).rearrange("p (t a) -> p t a", a=1).to_broadcast([P, TPC, D])
                dve.tensor_tensor(prod[:, c.slot(4), :, :], by_tile(bank[2 + c.slot(2)][:, :]), inv, ALU.mult)\
                   .then_inc(m_scaled.of(c), 1)

            for i in range(3):
                run(dve, f"mean{i}", [(1, mean_seg), (0, mean_scale)], NC)

            x_out.end(dve, "dense")
            run(dve, "dst", [(1, add_gathered), (0, norm)], NC)
            put_done.end(dve, "dst")
            run(dve, "final", [(1, add_x), (0, norm)], NN)
            x_out.end(dve, "final")

            for sums in (runmax, den, num):
                link(dve.memset(sums[:, :, :], 0.0))

            def att_qk(c):
                dve.wait_ge(a_k.of(c), a_k.after(c))
                dve.wait_ge(a_logit.of(c), a_logit.free(c))
                dve.tensor_tensor(qk[:, :], bank[2][:, :], k_sb[:, :], ALU.mult).then_inc(a_qk.of(c), 1)

            def att_soft(c):
                s, before = c.slot(2), c.ahead(-1)
                top, prev = runmax[:, s, 1:CH + 1], runmax[:, s, 0:CH]
                reset, logit, v = flag[:, c.slot(4), :], bank[5][:, :], bank[4][:, :]
                dve.wait_ge(a_max.of(before), a_max.after(before))
                dve.tensor_copy(runmax[:, s, 0:1], runmax[:, before.slot(2), CH:CH + 1]).then_inc(a_carry.of(c), 1)
                dve.wait_ge(a_carry.of(c), a_carry.after(c))
                dve.wait_ge(flag_in.of(c), flag_in.after(c))
                dve.wait_ge(a_logit.of(c), a_logit.after(c))
                dve.tensor_tensor_scan(top, reset, logit, runmax[:, s, 0:1], ALU.add, ALU.max).then_inc(a_max.of(c), 1)
                dve.wait_ge(a_exp.of(c), a_exp.free(c))
                dve.wait_ge(a_max.of(c), a_max.after(c))
                dve.tensor_tensor(dmax[:, 0, :], prev, reset, ALU.add).then_inc(a_step1.of(c), 1)
                dve.tensor_tensor(dmax[:, 1, :], logit, top, ALU.subtract)
                dve.wait_ge(a_step1.of(c), a_step1.after(c))
                dve.tensor_tensor(dmax[:, 0, :], dmax[:, 0, :], top, ALU.subtract).then_inc(a_dmax.of(c), 2)
                dve.wait_ge(a_exp.of(c), a_exp.after(c))
                dve.wait_ge(a_den.of(before), a_den.after(before))
                dve.tensor_tensor_scan(den[:, s, :], decay[:, :], weight[:, :], den[:, before.slot(2), CH - 1:CH],
                                       ALU.mult, ALU.add).then_inc(a_den.of(c), 1)
                dve.wait_ge(a_qkv.of(c), a_qkv.after(c))
                dve.tensor_tensor(weight[:, :], weight[:, :], v, ALU.mult).then_inc(a_wv.of(c), 1)
                dve.wait_ge(a_wv.of(c), a_wv.after(c))
                dve.wait_ge(a_num.of(before), a_num.after(before))
                dve.tensor_tensor_scan(num[:, s, :], decay[:, :], weight[:, :], num[:, before.slot(2), CH - 1:CH],
                                       ALU.mult, ALU.add).then_inc(a_num.of(c), 1)
                dve.wait_ge(a_den.of(c), a_den.after(c))
                dve.reciprocal(qr[:, :], den[:, s, :]).then_inc(a_rden.of(c), 1)
                dve.wait_ge(a_rden.of(c), a_rden.after(c))
                dve.wait_ge(a_num.of(c), a_num.after(c))
                dve.wait_ge(y_done.of(c), y_done.free(c))
                dve.tensor_tensor(agg[:, s, :], num[:, s, :], qr[:, :], ALU.mult).then_inc(a_agg.of(c), 1)

            def add_src(c):
                add(GP[:, c.slot(U), :, :], c)

            run(dve, "attend", [(1, att_qk), (1, att_soft), (0, add_src), (0, norm)], NC)


_INS = ["x", "src", "dst", "edge_attr_128", "L0_gnn_Wl0", "L0_gnn_bl0", "L0_gnn_Wr0", "L0_gnn_Wl1", "L0_gnn_bl1",
        "L0_gnn_Wr1", "L0_gnn_Wl2", "L0_gnn_bl2", "L0_gnn_Wr2", "L1_gnn_Wq", "L1_gnn_Wk", "L1_gnn_Wv", "L1_gnn_Wek",
        "L1_gnn_Wev", "L1_gnn_W_exp", "L1_gnn_W_out"]


def kernel(**inputs):
    import numpy as _np
    import concourse.bacc as _bacc
    from concourse import mybir as _mybir
    from concourse.bass_utils import run_bass_kernel_spmd as _run

    nc = _bacc.Bacc("TRN2", target_bir_lowering=False, num_devices=1)
    arrays, args = {}, []
    for name in _INS:
        a = _np.ascontiguousarray(inputs[name])
        arrays[f"in_{name}_dram"] = a
        args.append(nc.dram_tensor(f"in_{name}_dram", a.shape, _mybir.dt.from_np(a.dtype), kind="ExternalInput").ap())
    x = arrays["in_x_dram"]
    args.append(nc.dram_tensor("out_0_dram", x.shape, _mybir.dt.from_np(x.dtype), kind="ExternalOutput").ap())
    gnn_kernel(nc, *args)
    r = _run(nc, [arrays], core_ids=[0])
    return r.results[0]["out_0_dram"]
```

```python
from contextlib import ExitStack

import concourse.bass as bass
from concourse import mybir

F32 = mybir.dt.float32
I32 = mybir.dt.int32
BF16 = mybir.dt.bfloat16
ALU = mybir.AluOpType
ACT = mybir.ActivationFunctionType

P = 128
TPC = 4
CH = P * TPC
U = 8
LINE = 256
SORT = P * LINE
LOGN = SORT.bit_length() - 1
EPS = 1e-5
RESET = -1e38
FAR = float(1 << 20)


class At:

    def __init__(self, phase, j, u, last=False, per=U):
        self.phase, self.j, self.u, self.last, self.per = phase, j, u, last, per

    def index(self):
        return self.j * self.per + self.u

    def slot(self, n):
        return self.u % n

    def use(self, n):
        return self.j * (self.per // n) + self.u // n

    def before(self):
        return At(self.phase, self.j, self.u - 1)

    def item(self, n, i):
        return At(self.phase, self.j, self.u * n + i, self.last and i == n - 1, self.per * n)

    def chunk(self, n):
        return At(self.phase, self.j, self.u // n, self.last, self.per // n)


class Signal:

    def __init__(self, semaphore, name, buffers, by, phases, credit=None):
        self.n = buffers if by % 16 == 0 else 1
        self.sems = [semaphore(f"{name}{i}") for i in range(self.n)]
        self.buffers, self.by, self.phases = buffers, by, phases
        self.credit = (1 if self.n > 1 else 3 * U) if credit is None else credit

    def _had(self, phase, slot, whole):
        had = 0
        for name, chunks in self.phases:
            if name == phase and not whole:
                break
            had += -(-(chunks - slot) // self.n)
            if name == phase:
                break
        return had

    def of(self, c):
        return self.sems[c.slot(self.n)]

    def after(self, c, ago=0):
        assert ago % self.n == 0
        return (c.use(self.n) + (self._had(c.phase, c.slot(self.n), False) + 1 - ago // self.n + self.credit)) * self.by

    def free(self, c):
        return self.after(c, self.buffers)

    def earlier(self, eng, c, chunks):
        for slot in range(self.n):
            had = self._had(c.phase, slot, False) + -(-(chunks - 1 - slot) // self.n)
            eng.wait_ge(self.sems[slot], (had + self.credit) * self.by)

    def end(self, eng, phase):
        for slot in range(self.n):
            eng.wait_ge(self.sems[slot], (self._had(phase, slot, True) + self.credit) * self.by)


def run(eng, phase, stages, count):
    lead = max(n for n, _ in stages)
    whole = (count - 1 - lead) // U

    def single(s):
        for n, f in stages:
            if 0 <= s + n < count:
                f(At(phase, (s + n) // U, (s + n) % U, s + n == count - 1))

    for s in range(-lead, 0):
        single(s)
    with eng.Fori(0, whole) as j:
        for u in range(U):
            for n, f in stages:
                f(At(phase, j, u + n))
    for s in range(whole * U, count):
        single(s)


def take(ap, start, n):
    return ap[start:start + n] if isinstance(start, int) else ap[bass.ds(start, n)]


def take_cols(ap, start, n):
    return ap[:, start:start + n] if isinstance(start, int) else ap[:, bass.ds(start, n)]


def by_tile(ap):
    return ap.rearrange("p (t d) -> p t d", t=TPC)


def gnn_kernel(nc, x, src, dst, ea, Wl0, bl0, Wr0, Wl1, bl1, Wr1, Wl2, bl2, Wr2,
               Wq, Wk, Wv, Wek, Wev, Wexp, Wout, out):
    N, D = x.shape
    E = src.shape[0]
    H = Wexp.shape[0]
    HD = D // H
    NC = -(-E // CH)
    NN = -(-N // CH)
    EP = NC * CH
    XW = D + 4
    HALF = N // 2
    MAG0, SRC0 = 128, 512
    assert D == P and N <= 50432 and E < 1 << 15 and EP <= SORT

    def dram(name, shape, dt=F32):
        return nc.dram_tensor(name, shape, dt, kind="Internal").ap()

    xe = dram("x_with_lookup", (N, XW))
    eae = dram("edge_attr_with_dst", (E, XW))
    xp = dram("x_prime", (N, D))
    attended = dram("attended", (EP, D))
    prod_table = [dram(f"mean_product{i}", (EP + P, D)) for i in range(3)]
    key_row = [dram(f"key_row{w}", (SORT + 2,)) for w in range(2)]
    same_row = dram("same_dst_row", (SORT,))
    reset_row = dram("reset_src_row", (SORT,))

    with ExitStack() as ctx:
        def sb(name, shape, dt=F32):
            return ctx.enter_context(nc.sbuf_tensor(name, shape, dt))

        def sem(name):
            return ctx.enter_context(nc.semaphore(name))

        bank = [ctx.enter_context(nc.psum_tensor(f"bank{i}", [P, CH], F32)) for i in range(8)]

        ident = sb("ident", [P, P])
        ones = sb("ones", [P, LINE])
        eps = sb("eps", [P, 1])
        zrow = sb("zrow", [P, D])
        wraw = sb("wraw", [P, 12, D])
        wt = sb("wt", [P, 9, D])
        wexp_rows = sb("wexp_rows", [P, H])
        wexp_rep = sb("wexp_rep", [P, H, HD])
        bcol = sb("bcol", [P, 2])
        b2 = sb("b2", [3, D])
        b2part = sb("b2part", [3, 3, D], BF16)
        b2rest = sb("b2rest", [3, 2, D])
        b2mask = sb("b2mask", [3, 3, D], BF16)
        b2row = sb("b2row", [3, TPC, D], BF16)
        ones3 = sb("ones3", [3, P], BF16)
        hsrc = sb("hsrc", [P, EP])
        carved = [0]

        def part(shape, dt=F32):
            n = 1
            for k in shape:
                n *= k
            ap = hsrc[:, carved[0]:carved[0] + n]
            carved[0] += n
            names = " ".join("abcd"[:len(shape)])
            if len(shape) > 1:
                ap = ap.rearrange(f"p ({names}) -> p {names}", **dict(zip("abcd", shape[:-1])))
            return ap if dt == F32 else ap.bitcast(dt)

        kin = part([2, LINE], I32)
        pos = part([LINE], I32)
        gray = part([2, LINE], I32)
        flip = part([2, 2, LINE], I32)
        V = [part([2, LINE]) for _ in range(2)]
        work = [part([LINE], I32) for _ in range(6)]
        keyf = part([2, LINE])
        near = part([2, 2, LINE])
        same = part([LINE])
        resetf = part([LINE])
        local = part([2, LINE])
        value = part([8, LINE])
        carry_row = sb("carry_row", [1, 3, P + 1])
        carry_col = sb("carry_col", [P, 1])
        col_f = sb("col_f", [P, 2, LINE])
        col_i = sb("col_i", [P, 6, LINE], I32)
        lookup = sb("lookup", [P, LINE], I32)
        XB = part([4, TPC, XW])
        EB = part([4, TPC, XW])
        dsti = sb("dsti", [P, 4, TPC], I32)
        XN = sb("XN", [P, U, TPC, D])
        GX = sb("GX", [P, U, TPC, XW])
        idx_a = sb("idx_a", [P, U, TPC], I32)
        idx_b = sb("idx_b", [P, U, TPC], I32)
        idx_c = sb("idx_c", [P, U, TPC], I32)
        idx_d = sb("idx_d", [P, U, TPC], I32)
        lval = sb("lval", [P, U, TPC])
        flag = sb("flag", [P, 4, CH])
        h0, h1, h2 = (sb(f"h{i}", [P, 2, CH]) for i in range(3))
        seg = sb("seg", [P, 2, CH])
        prod = sb("prod", [P, 4, TPC, D])
        res = sb("res", [P, 3, TPC, D])
        normed = sb("normed", [P, 4, TPC, D])
        stats = sb("stats", [P, 3, TPC, 6])
        mv = sb("mv", [P, 3, TPC, 2])
        logv = sb("logv", [P, 3, TPC])
        rstd = sb("rstd", [P, 3, TPC])
        shift = sb("shift", [P, 3, TPC])

        carved[0] = 0
        PL = part([U, 3, TPC, D])
        carved[0] = 0
        GP = part([U, TPC, D])
        GD = part([U, TPC, D])
        qk = part([CH])
        k_sb = part([CH])
        v_sb = part([2, CH])
        src_t = part([4, CH])
        node_t = part([4, CH])
        qr = part([CH])
        runmax = part([2, CH + 1])
        dmax = part([2, CH])
        decay = part([CH])
        weight = part([CH])
        den = part([2, CH])
        num = part([2, CH])
        agg = part([2, CH])

        (W_L0, W_R0, W_L1, W_R1, W_L2, W_R2, W_V, W_OUT, W_Q, W_K, W_EK, W_EV) = range(12)
        W_FILES = [Wl0, Wr0, Wl1, Wr1, Wl2, Wr2, Wv, Wout, Wq, Wk, Wek, Wev]
        T_L, T_R, T_V, T_VO, T_NOUT = (0, 2, 4), (1, 3, 5), 6, 7, 8
        V_SRC_A, V_DST_A, V_PUT_A, V_ID_B, V_SRC_B, V_PUT_B, V_POS, V_INV = range(8)

        go = sem("go")
        held = {e: sem(f"held_{e}") for e in ("sp", "pool", "dve")}
        pool_const = sem("pool_const")
        keys_loaded = sem("keys_loaded")
        w_loaded = sem("w_loaded")
        small_loaded = sem("small_loaded")
        dve_step = sem("dve_step")
        const_ready = sem("const_ready")
        w_turned = sem("w_turned")
        w_ready = sem("w_ready")
        vo_done = sem("vo_done")
        sort_step = sem("sort_step")
        turned = sem("turned")
        keys_out, near_in, rows_out = sem("keys_out"), sem("near_in"), sem("rows_out")
        keys_made, flags_made = sem("keys_made"), sem("flags_made")
        carry_turned = sem("carry_turned")
        carry_made = sem("carry_made")
        value_ready = sem("value_ready")
        value_turned = sem("value_turned")
        cols_ready = sem("cols_ready")
        zero_out = sem("zero_out")
        pad_ready = sem("pad_ready")
        all_out = sem("all_out")

        signals = []

        def signal(name, buffers, by, phases, credit=None):
            signals.append(Signal(sem, name, buffers, by, phases, credit))
            return signals[-1]

        XE, EA, LK = [("xe", NN)], [("ea", NC)], [("lk", NC)]
        xe_in, xe_out = signal("xe_in", 4, 16, XE), signal("xe_out", 4, 16, XE)
        ea_in, ea_out = signal("ea_in", 4, 32, EA), signal("ea_out", 4, 16, EA)
        ea_dst = signal("ea_dst", 4, 1, EA)
        MEANS = [(f"mean{i}", NC) for i in range(3)]
        CHAIN = [("dense", NN), ("dst", NC)]
        NODES = [("dense", NN), ("attend", NN)]
        NORM = [("dense", NN), ("dst", NC), ("attend", 3 * NC)]
        DST, ATT, REST = [("dst", NC)], [("attend", NC)], [("rest", NC)]
        ATT2, ATT3 = [("attend", 2 * NC)], [("attend", 3 * NC)]
        POOLED = [("lk", NC), *MEANS, ("dst", NC)]
        idx_ready = signal("idx_ready", U, 1, POOLED + ATT)
        put_ready = signal("put_ready", U, 1, DST + REST)
        gathered = signal("gathered", U, 64, MEANS + DST + ATT, 0)
        m_turned = signal("m_turned", 2, 1, MEANS)
        m_h = signal("m_h", 2, 1, MEANS)
        m_seg = signal("m_seg", 2, 1, MEANS)
        m_prod = signal("m_prod", 2, 1, MEANS)
        m_scaled = signal("m_scaled", 2, 1, MEANS)
        m_stored = signal("m_stored", 4, 16, MEANS)
        m_look = signal("m_look", U, 1, [("mean0", NC)])
        flag_in = signal("flag_in", 4, 16, MEANS + ATT)
        x_in = signal("x_in", U, 16, NODES + REST)
        pl_in = signal("pl_in", U, 48, DST)
        t_done, t_kept = signal("t_done", 2, 1, CHAIN), signal("t_kept", 2, 1, CHAIN)
        u1_done, u1_kept = signal("u1_done", 2, 1, CHAIN), signal("u1_kept", 2, 1, CHAIN)
        u2_done, u2_kept = signal("u2_done", 2, 1, CHAIN), signal("u2_kept", 2, 1, CHAIN)
        y_done = signal("y_done", 2, 1, NORM)
        added0 = signal("added0", 2, 1, DST)
        added = signal("added", 2, 1, NORM)
        n_stats, n_aggr = signal("n_stats", 2, 1, NORM), signal("n_aggr", 2, 1, NORM)
        n_log, n_rstd = signal("n_log", 2, 1, NORM), signal("n_rstd", 2, 1, NORM)
        n_done = signal("n_done", 2, 1, [("dense", NN), ("dst", NC), ("attend", NC)])
        x_out = signal("x_out", 4, 16, [("dense", NN), ("attend", 3 * NC)])
        put_done = signal("put_done", 4, 64, LK + DST + REST, 0)
        put_free = signal("put_free", 4, 1, DST + REST)
        ea_got = signal("ea_got", U, 64, ATT, 0)
        dst_got = signal("dst_got", U, 64, ATT, 0)
        dst_idx = signal("dst_idx", U, 1, ATT)
        n_shift, n_node = signal("n_shift", 1, 1, ATT2), signal("n_node", 1, 1, ATT2)
        a_turned, a_kept = signal("a_turned", 1, 1, ATT3), signal("a_kept", 1, 1, ATT3)
        f_turned, f_kept = signal("f_turned", 1, 1, ATT2), signal("f_kept", 1, 1, ATT2)
        a_qk_psum, a_v_psum = signal("a_qk_psum", 1, 1, ATT), signal("a_v_psum", 1, 1, ATT)
        a_k, a_v = signal("a_k", 1, 1, ATT), signal("a_v", 1, 1, ATT)
        a_qk = signal("a_qk", 1, 1, ATT)
        a_logit = signal("a_logit", 1, 1, ATT)
        a_carry = signal("a_carry", 1, 1, ATT)
        a_max = signal("a_max", 2, 1, ATT)
        a_step1 = signal("a_step1", 1, 1, ATT)
        a_dmax = signal("a_dmax", 1, 1, ATT)
        a_exp = signal("a_exp", 1, 1, ATT)
        a_den = signal("a_den", 2, 1, ATT)
        a_wv = signal("a_wv", 1, 1, ATT)
        a_num = signal("a_num", 2, 1, ATT)
        a_rlog, a_rden = signal("a_rlog", 1, 1, ATT), signal("a_rden", 1, 1, ATT)
        a_agg = signal("a_agg", 2, 1, ATT)

        def norm_slot(c):
            return c.slot(3 if c.phase == "attend" else 2)

        def normed_by(c):
            if c.phase != "attend":
                return n_done, c, 2
            if c.u % 3 == 1:
                return n_done, c.chunk(3), 1
            return n_node, c.chunk(3).item(2, c.u % 3 // 2), 2

        def wait_normed(eng, c):
            sig, what, _ = normed_by(c)
            eng.wait_ge(sig.of(what), sig.after(what))

        def wait_norm_slot(eng, c):
            sig, what, ago = normed_by(c)
            eng.wait_ge(sig.of(what), sig.after(what, ago))

        def hold(eng, name):
            eng.sem_inc(held[name], 1)

        def file_rows(table, rows, c):
            return take(table, rows - CH if c.last else c.index() * CH, CH).rearrange("(q t) d -> q t d", t=TPC)

        def sorted_rows(table, c):
            return take(table, c.index() * CH, CH).rearrange("(t q) d -> q t d", q=P)

        def on_all(row, c):
            return take(row, c.index() * CH, CH).rearrange("(a n) -> a n", a=1).to_broadcast([P, CH])

        plan = []
        for k in range(1, LOGN + 1):
            if k > 8:
                plan.append(("turn", 0))
            for b in range(k - 1, -1, -1):
                if k > 8 and b == 7:
                    plan.append(("turn", 0))
                plan.append(("compare", 1 << (b - 8 if b > 7 else b)))
            if k < LOGN:
                plan.append(("flip", k))

        block = ctx.enter_context(nc.Block())

        @block.sync
        def _(sp):
            for s in signals:
                for one in s.sems:
                    if s.credit:
                        sp.sem_inc(one, s.credit * s.by)
            sp.sem_inc(go, 1)
            sp.wait_ge(pad_ready, 2)
            whole = E // LINE
            for w, row in enumerate((dst, src)):
                sp.dma_start(kin[0:whole, w, :], row[0:whole * LINE].rearrange("(p f) -> p f", f=LINE)).then_inc(keys_loaded, 16)
                sp.dma_start(kin[whole:whole + 1, w, 0:E - whole * LINE], row[whole * LINE:E].rearrange("(a f) -> a f", a=1)).then_inc(keys_loaded, 16)
            for i, w in enumerate(W_FILES):
                sp.dma_start(wraw[:, i, :], w).then_inc(w_loaded, 16)
            for h in range(H):
                sp.dma_start(wexp_rows[HD * h:HD * (h + 1), :], Wexp[h:h + 1, :].to_broadcast([HD, H])).then_inc(small_loaded, 16)
            for i, b in enumerate((bl0, bl1)):
                sp.dma_start(bcol[:, i:i + 1], b.rearrange("(p a) -> p a", a=1)).then_inc(small_loaded, 16)
            sp.dma_start(b2[:, :], bl2.rearrange("(a n) -> a n", a=1).to_broadcast([3, D])).then_inc(small_loaded, 16)
            for i in range(2):
                sp.dma_start(prod_table[i][EP:EP + P, :], zrow[:, :]).then_inc(zero_out, 16)
            for w in range(2):
                for at in (0, SORT + 1):
                    sp.dma_start(key_row[w][at:at + 1].rearrange("(a n) -> a n", a=1), zrow[0:1, 0:1]).then_inc(zero_out, 16)

            def ea_load(c):
                s = c.slot(4)
                sp.wait_ge(ea_out.of(c), ea_out.free(c))
                hold(sp, "sp")
                sp.dma_start(EB[:, s, :, 0:D], file_rows(ea, E, c)).then_inc(ea_in.of(c), 16)
                sp.dma_start(dsti[:, s, :], take(dst, E - CH if c.last else c.index() * CH, CH).rearrange("(q t) -> q t", t=TPC)).then_inc(ea_in.of(c), 16)

            def ea_store(c):
                if c.last:
                    ea_out.earlier(sp, c, NC)
                sp.wait_ge(ea_in.of(c), ea_in.after(c))
                hold(sp, "sp")
                sp.wait_ge(ea_dst.of(c), ea_dst.after(c))
                hold(sp, "sp")
                sp.dma_start(file_rows(eae, E, c), EB[:, c.slot(4), :, :]).then_inc(ea_out.of(c), 16)

            run(sp, "ea", [(2, ea_load), (0, ea_store)], NC)

            sp.wait_ge(keys_made, 1)
            for w in range(2):
                sp.dma_start(key_row[w][1:SORT + 1].rearrange("(p f) -> p f", f=LINE), keyf[:, w, :]).then_inc(keys_out, 16)
            sp.wait_ge(keys_out, 32)
            sp.wait_ge(zero_out, 16 * 6)
            for w in range(2):
                for side in range(2):
                    sp.dma_start(near[:, w, side, :], key_row[w][2 * side:2 * side + SORT].rearrange("(p f) -> p f", f=LINE)).then_inc(near_in, 16)
            sp.wait_ge(flags_made, 1)
            sp.dma_start(same_row.rearrange("(p f) -> p f", f=LINE), same[:, :]).then_inc(rows_out, 16)
            sp.dma_start(reset_row.rearrange("(p f) -> p f", f=LINE), resetf[:, :]).then_inc(rows_out, 16)
            sp.wait_ge(rows_out, 32)

            def x_load(c):
                sp.wait_ge(added.of(c), added.after(c, U))
                sp.dma_start(XN[:, c.slot(U), :, :], file_rows(x, N, c)).then_inc(x_in.of(c), 16)

            def x_store(c):
                if c.last:
                    x_out.earlier(sp, c, NN)
                sp.wait_ge(n_done.of(c), n_done.after(c))
                sp.dma_start(file_rows(xp, N, c), normed[:, c.slot(4), :, :]).then_inc(x_out.of(c), 16)

            run(sp, "dense", [(7, x_load), (0, x_store)], NN)

            def flag_load(c):
                sig = m_seg if c.phase != "attend" else a_step1
                sp.wait_ge(sig.of(c), sig.after(c, 4))
                sp.dma_start(flag[:, c.slot(4), :], on_all(reset_row if c.phase == "attend" else same_row, c)).then_inc(flag_in.of(c), 16)

            def prod_store(c):
                sp.wait_ge(m_scaled.of(c), m_scaled.after(c))
                hold(sp, "sp")
                sp.dma_start(sorted_rows(prod_table[int(c.phase[-1])], c), prod[:, c.slot(4), :, :]).then_inc(m_stored.of(c), 16)

            for i in range(3):
                run(sp, f"mean{i}", [(3, flag_load), (0, prod_store)], NC)
            m_stored.end(sp, "mean2")

            def pl_load(c):
                sp.wait_ge(u2_done.of(c), u2_done.after(c, U))
                hold(sp, "sp")
                sp.wait_ge(added.of(c), added.after(c, U))
                hold(sp, "sp")
                for i in range(3):
                    sp.dma_start(PL[:, c.slot(U), i, :, :], sorted_rows(prod_table[i], c)).then_inc(pl_in.of(c), 16)

            run(sp, "dst", [(0, pl_load)], NC)
            put_done.end(sp, "dst")

            def node_load(half):
                def f(c):
                    node, item = c.item(2, half), c.item(3, 2 * half)
                    sp.wait_ge(added.of(item), added.after(item, 3 * U // 2))
                    sp.dma_start(XN[:, node.slot(U), :, :], file_rows(xp, N, node)).then_inc(x_in.of(node), 16)
                return f

            def att_store(i):
                def f(c):
                    item = c.item(3, i)
                    if item.last:
                        x_out.earlier(sp, item, 3 * NC)
                    wait_normed(sp, item)
                    to = sorted_rows(attended, c) if i == 1 else file_rows(out, N, c.item(2, i // 2))
                    sp.dma_start(to, normed[:, item.slot(4), :, :]).then_inc(x_out.of(item), 16)
                return f

            run(sp, "attend", [(3, flag_load), (2, node_load(0)), (2, node_load(1)), (0, att_store(0)),
                               (0, att_store(1)), (0, att_store(2))], NC)
            x_out.end(sp, "attend")

            def rest_load(c):
                sp.wait_ge(put_free.of(c), put_free.after(c, U))
                hold(sp, "sp")
                sp.dma_start(XN[:, c.slot(U), :, :], sorted_rows(attended, c)).then_inc(x_in.of(c), 16)

            run(sp, "rest", [(0, rest_load)], NC)
            put_done.end(sp, "rest")
            sp.sem_inc(all_out, 1)

        @block.gpsimd
        def _(pool):
            pool.wait_ge(go, 1)
            pool.memset(ident[:, :], 0.0).then_inc(pool_const, 1)
            pool.wait_ge(pool_const, 1)
            pool.affine_select(out=ident[:, :], in_=ident[:, :], compare_op=ALU.not_equal, fill=1.0, base=0,
                               pattern=[[-1, P]], channel_multiplier=1).then_inc(pool_const, 1)
            pool.iota(pos[:, :], pattern=[[1, LINE]], base=0, channel_multiplier=LINE).then_inc(pool_const, 1)
            for s in range(4):
                pool.memset(XB[:, s, :, D:XW], float(EP)).then_inc(pool_const, 1)
                pool.memset(EB[:, s, :, D:XW], 0.0).then_inc(pool_const, 1)
            pool.wait_ge(pool_const, 11)

            def ea_fill(c):
                s = c.slot(4)
                pool.wait_ge(ea_in.of(c), ea_in.after(c))
                hold(pool, "pool")
                pool.tensor_copy(EB[:, s, :, D:D + 1], dsti[:, s, :].rearrange("p (t a) -> p t a", a=1)).then_inc(ea_dst.of(c), 1)

            run(pool, "ea", [(0, ea_fill)], NC)

            def stage(ap, signal_, buf):
                def f(c):
                    pool.tensor_copy(buf[:, c.slot(U), :], take_cols(ap, c.index() * TPC, TPC)).then_inc(signal_.of(c), 1)
                return f

            def gather(buf, table, idx, width, c, sig):
                for t in range(TPC):
                    pool.indirect_dma_start(buf[:, c.slot(U), t, 0:width], None, table,
                                            bass.IndirectOffsetOnAxis(ap=idx[:, c.slot(U), t:t + 1], axis=0)).then_inc(sig.of(c), 16)

            pool.wait_ge(cols_ready, 1)
            pool.wait_ge(rows_out, 32)
            xe_out.end(pool, "xe")

            def lk_stage(c):
                pool.tensor_copy(lval[:, c.slot(4), :], take_cols(col_f[:, 0, :], c.index() * TPC, TPC))
                pool.tensor_copy(idx_a[:, c.slot(4), :], take_cols(col_i[:, V_PUT_A, :], c.index() * TPC, TPC)).then_inc(idx_ready.of(c), 1)

            def lk_put(c):
                pool.wait_ge(idx_ready.of(c), idx_ready.after(c))
                hold(pool, "pool")
                for t in range(TPC):
                    pool.indirect_dma_start(xe, bass.IndirectOffsetOnAxis(ap=idx_a[:, c.slot(4), t:t + 1], axis=0),
                                            lval[:, c.slot(4), t:t + 1], None, element_offset=D,
                                            bounds_check=N - 1, oob_is_err=False).then_inc(put_done.of(c), 16)

            def lk_settle(c):
                pool.wait_ge(put_done.of(c), put_done.after(c))
                hold(pool, "pool")

            run(pool, "lk", [(0, lk_settle), (3, lk_stage), (2, lk_put)], NC)
            put_done.end(pool, "lk")

            def mean_stage(c):
                pool.wait_ge(m_turned.of(c), m_turned.after(c, U))
                cols = col_i[:, V_SRC_A, :] if c.phase == "mean0" else lookup[:, :]
                pool.tensor_copy(idx_a[:, c.slot(U), :], take_cols(cols, c.index() * TPC, TPC)).then_inc(idx_ready.of(c), 1)

            def mean_gather(c):
                pool.wait_ge(idx_ready.of(c), idx_ready.after(c))
                pool.wait_ge(m_turned.of(c), m_turned.after(c, U))
                if c.phase == "mean0":
                    pool.wait_ge(m_look.of(c), m_look.free(c))
                hold(pool, "pool")
                if c.phase == "mean0":
                    gather(GX, xe, idx_a, XW, c, gathered)
                else:
                    gather(GX, prod_table[int(c.phase[-1]) - 1], idx_a, D, c, gathered)

            for i in range(3):
                if i:
                    m_look.end(pool, "mean0")
                    m_stored.end(pool, f"mean{i - 1}")
                    pool.wait_ge(zero_out, 16 * 6)
                run(pool, f"mean{i}", [(1, mean_stage), (0, mean_gather)], NC)

            def dst_stage(c):
                pool.wait_ge(t_done.of(c), t_done.after(c, U))
                hold(pool, "pool")
                pool.tensor_copy(idx_a[:, c.slot(U), :], take_cols(col_i[:, V_DST_A, :], c.index() * TPC, TPC)).then_inc(idx_ready.of(c), 1)

            def dst_gather(c):
                pool.wait_ge(idx_ready.of(c), idx_ready.after(c))
                pool.wait_ge(added.of(c), added.after(c, U))
                hold(pool, "pool")
                gather(GX, x, idx_a, D, c, gathered)

            def put_stage(c):
                cols = col_i[:, V_PUT_A if c.phase == "dst" else V_PUT_B, :]
                pool.tensor_copy(idx_b[:, c.slot(U), :], take_cols(cols, c.index() * TPC, TPC)).then_inc(put_ready.of(c), 1)

            def put(c):
                pool.wait_ge(put_ready.of(c), put_ready.after(c))
                if c.phase == "dst":
                    pool.wait_ge(n_done.of(c), n_done.after(c))
                    table, rows = xp, normed[:, c.slot(4), :, :]
                else:
                    pool.wait_ge(x_in.of(c), x_in.after(c))
                    table, rows = out, XN[:, c.slot(U), :, :]
                hold(pool, "pool")
                for t in range(TPC):
                    pool.indirect_dma_start(table,
                                            bass.IndirectOffsetOnAxis(ap=idx_b[:, c.slot(U), t:t + 1], axis=0),
                                            rows[:, t, :], None,
                                            bounds_check=N - 1, oob_is_err=False).then_inc(put_done.of(c), 16)

            def settle(c):
                pool.wait_ge(put_done.of(c), put_done.after(c))
                hold(pool, "pool")
                pool.sem_inc(put_free.of(c), 1)

            m_turned.end(pool, "mean2")
            x_out.end(pool, "dense")
            run(pool, "dst", [(8, dst_stage), (7, dst_gather), (2, put_stage), (1, put), (0, settle)], NC)
            put_done.end(pool, "dst")
            ea_out.end(pool, "ea")

            def rows_used(c):
                item = c.item(3, 2)
                pool.wait_ge(a_turned.of(item), a_turned.after(item, 3 * U))

            def att_stage(c):
                rows_used(c)
                hold(pool, "pool")
                pool.tensor_copy(idx_c[:, c.slot(U), :], take_cols(col_i[:, V_SRC_B, :], c.index() * TPC, TPC))
                pool.tensor_copy(idx_a[:, c.slot(U), :], take_cols(col_i[:, V_ID_B, :], c.index() * TPC, TPC)).then_inc(idx_ready.of(c), 1)

            def att_gather(c):
                item = c.item(3, 1)
                pool.wait_ge(idx_ready.of(c), idx_ready.after(c))
                rows_used(c)
                pool.wait_ge(dst_idx.of(c), dst_idx.free(c))
                pool.wait_ge(added.of(item), added.after(item, 3 * U))
                hold(pool, "pool")
                gather(GX, eae, idx_a, XW, c, ea_got)
                gather(GP, xp, idx_c, D, c, gathered)

            def att_dst(c):
                pool.wait_ge(ea_got.of(c), ea_got.after(c))
                rows_used(c)
                hold(pool, "pool")
                pool.tensor_copy(idx_d[:, c.slot(U), :], GX[:, c.slot(U), :, D:D + 1].rearrange("p t a -> p (t a)")).then_inc(dst_idx.of(c), 1)
                pool.wait_ge(dst_idx.of(c), dst_idx.after(c))
                hold(pool, "pool")
                gather(GD, xp, idx_d, D, c, dst_got)

            run(pool, "attend", [(9, att_stage), (8, att_gather), (6, att_dst)], NC)

            x_out.end(pool, "attend")
            run(pool, "rest", [(3, put_stage), (2, put), (0, settle)], NC)
            put_done.end(pool, "rest")

        @block.tensor
        def _(pe):
            def turn_in(dst, src):
                return pe.transpose(dst, src, ident[0:src.shape[0], 0:src.shape[0]])

            pe.wait_ge(pool_const, 11)
            pe.wait_ge(w_loaded, 16 * len(W_FILES))
            for i in range(7):
                turn_in(bank[2 + i // 4][:, i % 4 * P:(i % 4 + 1) * P], wraw[:, i, :]).then_inc(w_turned, 1)
            pe.wait_ge(w_ready, 1)
            pe.matmul(bank[4][:, 0:D], wt[:, T_V, :], wraw[:, W_OUT, :], start=True, stop=True).then_inc(vo_done, 1)

            steps = turns = side = 0
            for what, _ in plan:
                if what != "turn":
                    steps += 1
                    side ^= what == "compare"
                    continue
                pe.wait_ge(sort_step, 2 * steps + 2)
                for i in range(4):
                    last = turn_in(bank[turns % 2][:, i * P:(i + 1) * P],
                                   V[side][:, :, :].rearrange("p w f -> p (w f)")[:, i * P:(i + 1) * P])
                last.then_inc(turned, 1)
                turns += 1
            pe.wait_ge(carry_made, 1)
            for i in range(2):
                turn_in(bank[2 + i][0:1, 0:P], local[:, i, LINE - 1:LINE]).then_inc(carry_turned, 1)
            pe.wait_ge(carry_made, 2)
            turn_in(bank[4][:, 0:1], carry_row[0:1, 2, 0:P]).then_inc(carry_turned, 1)
            pe.wait_ge(value_ready, 1)
            for i in range(8):
                for a in range(2):
                    last = turn_in(bank[i][:, a * P:(a + 1) * P], value[:, i, a * P:(a + 1) * P])
                last.then_inc(value_turned, 1)
            pe.wait_ge(cols_ready, 1)

            def rows_turned(rows, c):
                pe.wait_ge(t_kept.of(c), t_kept.free(c))
                for t in range(TPC):
                    last = turn_in(bank[c.slot(2)][:, t * P:(t + 1) * P], rows[:, c.slot(U), t, 0:D])
                last.then_inc(t_done.of(c), 1)

            def chain_t(c):
                if c.phase == "dst":
                    pe.wait_ge(gathered.of(c), gathered.after(c))
                    rows_turned(GX, c)
                else:
                    pe.wait_ge(x_in.of(c), x_in.after(c))
                    rows_turned(XN, c)

            def layer(i, c, psum, before, kept_before, done, kept):
                pe.wait_ge(kept_before.of(c), kept_before.after(c))
                pe.wait_ge(kept.of(c), kept.free(c))
                dst_phase = c.phase == "dst"
                last = pe.matmul(psum[:, :], wt[:, T_R[i], :], before[:, c.slot(2), :], start=True, stop=not dst_phase)
                if dst_phase:
                    pe.wait_ge(pl_in.of(c), pl_in.after(c))
                    for t in range(TPC):
                        last = pe.matmul(psum[:, t * P:(t + 1) * P], PL[:, c.slot(U), i, t, :], ident[:, :],
                                         start=False, stop=t == TPC - 1)
                last.then_inc(done.of(c), 1)

            def chain_1(c):
                layer(0, c, bank[2 + c.slot(2)], h0, t_kept, u1_done, u1_kept)

            def chain_2(c):
                layer(1, c, bank[4 + c.slot(2)], h1, u1_kept, u2_done, u2_kept)

            def chain_y(c):
                pe.wait_ge(u2_kept.of(c), u2_kept.after(c))
                pe.wait_ge(added.of(c), added.free(c))
                y = bank[6 + c.slot(2)]
                pe.matmul(y[:, :], ones3[:, :], b2row[:, :, :].rearrange("k t d -> k (t d)"), start=True, stop=False)
                for t in range(TPC):
                    last = pe.matmul(y[:, t * P:(t + 1) * P], h2[:, c.slot(2), t * P:(t + 1) * P], wt[:, T_R[2], :],
                                     start=False, stop=t == TPC - 1)
                last.then_inc(y_done.of(c), 1)

            chain = [(3, chain_t), (2, chain_1), (1, chain_2), (0, chain_y)]
            run(pe, "dense", chain, NN)
            added.end(pe, "dense")

            def mean_turn(c):
                pe.wait_ge(gathered.of(c), gathered.after(c))
                pe.wait_ge(m_h.of(c), m_h.free(c))
                psum = bank[c.slot(2)]
                if c.phase == "mean0":
                    for t in range(TPC):
                        last = turn_in(psum[:, t * P:(t + 1) * P], GX[:, c.slot(U), t, 0:D])
                else:
                    i = int(c.phase[-1]) - 1
                    pe.matmul(psum[:, :], wt[:, T_R[i], :], take_cols(hsrc, c.index() * CH, CH), start=True, stop=False)
                    for t in range(TPC):
                        last = pe.matmul(psum[:, t * P:(t + 1) * P], GX[:, c.slot(U), t, 0:D], ident[:, :],
                                         start=False, stop=t == TPC - 1)
                last.then_inc(m_turned.of(c), 1)

            def mean_prod(c):
                pe.wait_ge(m_seg.of(c), m_seg.after(c))
                pe.wait_ge(m_scaled.of(c), m_scaled.free(c))
                for t in range(TPC):
                    last = pe.matmul(bank[2 + c.slot(2)][:, t * P:(t + 1) * P], seg[:, c.slot(2), t * P:(t + 1) * P],
                                     wt[:, T_L[int(c.phase[-1])], :], start=True, stop=True)
                last.then_inc(m_prod.of(c), 1)

            for i in range(3):
                run(pe, f"mean{i}", [(1, mean_turn), (0, mean_prod)], NC)
                m_h.end(pe, f"mean{i}")
            m_scaled.end(pe, "mean2")

            run(pe, "dst", chain, NC)
            added.end(pe, "dst")

            def att_turn(i):
                rows, sig = ((GX, ea_got), (GP, gathered), (GD, dst_got))[i]
                def f(c):
                    item = c.item(3, i)
                    pe.wait_ge(sig.of(c), sig.after(c))
                    pe.wait_ge(a_kept.of(item), a_kept.free(item))
                    for t in range(TPC):
                        last = turn_in(bank[0][:, t * P:(t + 1) * P], rows[:, c.slot(U), t, 0:D])
                    last.then_inc(a_turned.of(item), 1)
                return f

            def node_turn(half):
                def f(c):
                    node = c.item(2, half)
                    pe.wait_ge(x_in.of(node), x_in.after(node))
                    pe.wait_ge(f_kept.of(node), f_kept.free(node))
                    for t in range(TPC):
                        last = turn_in(bank[1][:, t * P:(t + 1) * P], XN[:, node.slot(U), t, :])
                    last.then_inc(f_turned.of(node), 1)
                return f

            def att_qkv(c):
                s, kept = c.slot(2), c.item(3, 2)
                pe.wait_ge(a_kept.of(kept), a_kept.after(kept))
                pe.wait_ge(a_qk.of(c), a_qk.free(c))
                pe.matmul(bank[2][:, :], wraw[:, W_Q, :], src_t[:, c.slot(4), :], start=True, stop=True)
                pe.matmul(bank[3][:, :], wraw[:, W_K, :], h2[:, s, :], start=True, stop=False)
                pe.matmul(bank[3][:, :], wraw[:, W_EK, :], h0[:, s, :], start=False, stop=True).then_inc(a_qk_psum.of(c), 1)
                pe.wait_ge(a_v.of(c), a_v.free(c))
                pe.matmul(bank[4][:, :], wraw[:, W_V, :], h2[:, s, :], start=True, stop=False)
                pe.matmul(bank[4][:, :], wraw[:, W_EV, :], h0[:, s, :], start=False, stop=True).then_inc(a_v_psum.of(c), 1)

            def att_logit(c):
                pe.wait_ge(a_qk.of(c), a_qk.after(c))
                pe.wait_ge(a_dmax.of(c), a_dmax.free(c))
                pe.matmul(bank[5][:, :], wexp_rep[:, :, :].rearrange("p h d -> p (h d)"), qk[:, :],
                          start=True, stop=True).then_inc(a_logit.of(c), 1)

            def att_y(c):
                item = c.item(3, 1)
                y = bank[6 + item.slot(2)]
                pe.wait_ge(a_agg.of(c), a_agg.after(c))
                pe.wait_ge(added.of(item), added.free(item))
                for t in range(TPC):
                    pe.matmul(y[:, t * P:(t + 1) * P], src_t[:, c.slot(4), t * P:(t + 1) * P], wt[:, T_VO, :], start=True, stop=False)
                    last = pe.matmul(y[:, t * P:(t + 1) * P], agg[:, c.slot(2), t * P:(t + 1) * P], wt[:, T_NOUT, :],
                                     start=False, stop=True)
                last.then_inc(y_done.of(item), 1)

            def node_y(half):
                def f(c):
                    item, node = c.item(3, 2 * half), c.item(2, half)
                    pe.wait_ge(f_kept.of(node), f_kept.after(node))
                    pe.wait_ge(added.of(item), added.free(item))
                    for t in range(TPC):
                        last = pe.matmul(bank[6 + item.slot(2)][:, t * P:(t + 1) * P],
                                         node_t[:, node.slot(4), t * P:(t + 1) * P], wt[:, T_VO, :], start=True, stop=True)
                    last.then_inc(y_done.of(item), 1)
                return f

            run(pe, "attend", [(0, node_y(0)), (0, att_y), (0, node_y(1)), (2, att_qkv), (3, att_turn(0)), (1, node_turn(0)),
                               (3, att_turn(1)), (1, node_turn(1)), (3, att_turn(2)), (2, att_logit)], NC)

        @block.scalar
        def _(act):
            act.preload_act_table_set("natural_log_exp_and_others")
            act.wait_ge(go, 1)
            act.wait_ge(pool_const, 11)

            def xe_load(c):
                act.wait_ge(xe_out.of(c), xe_out.free(c))
                act.dma_start(XB[:, c.slot(4), :, 0:D], file_rows(x, N, c)).then_inc(xe_in.of(c), 16)

            def xe_store(c):
                if c.last:
                    xe_out.earlier(act, c, NN)
                act.wait_ge(xe_in.of(c), xe_in.after(c))
                act.dma_start(file_rows(xe, N, c), XB[:, c.slot(4), :, :]).then_inc(xe_out.of(c), 16)

            run(act, "xe", [(2, xe_load), (0, xe_store)], NN)
            act.wait_ge(cols_ready, 1)

            def keep_t(c):
                act.wait_ge(t_done.of(c), t_done.after(c))
                act.wait_ge(u1_done.of(c), u1_done.free(c))
                act.activation(h0[:, c.slot(2), :], bank[c.slot(2)][:, :], ACT.Copy).then_inc(t_kept.of(c), 1)

            def keep_1(c):
                act.wait_ge(u1_done.of(c), u1_done.after(c))
                act.wait_ge(u2_done.of(c), u2_done.free(c))
                act.activation(h1[:, c.slot(2), :], bank[2 + c.slot(2)][:, :], ACT.Relu, bias=bcol[:, 0:1]).then_inc(u1_kept.of(c), 1)

            def keep_2(c):
                act.wait_ge(u2_done.of(c), u2_done.after(c))
                act.wait_ge(y_done.of(c), y_done.free(c))
                act.activation(h2[:, c.slot(2), :], bank[4 + c.slot(2)][:, :], ACT.Relu, bias=bcol[:, 1:2]).then_inc(u2_kept.of(c), 1)

            def inverse_root(c):
                s = norm_slot(c)
                act.wait_ge(n_aggr.of(c), n_aggr.after(c))
                act.activation(logv[:, s, :], mv[:, s, :, 1], ACT.Ln, bias=eps[:, 0:1]).then_inc(n_log.of(c), 1)
                act.wait_ge(n_log.of(c), n_log.after(c))
                wait_norm_slot(act, c)
                act.activation(rstd[:, s, :], logv[:, s, :], ACT.Exp, scale=-0.5).then_inc(n_rstd.of(c), 1)

            chain = [(3, keep_t), (2, keep_1), (1, keep_2), (0, inverse_root)]
            run(act, "dense", chain, NN)

            def mean_keep(c):
                act.wait_ge(m_turned.of(c), m_turned.after(c))
                i = int(c.phase[-1])
                h = take_cols(hsrc, c.index() * CH, CH)
                if i == 0:
                    act.activation(h, bank[c.slot(2)][:, :], ACT.Copy).then_inc(m_h.of(c), 1)
                else:
                    act.activation(h, bank[c.slot(2)][:, :], ACT.Relu, bias=bcol[:, i - 1:i]).then_inc(m_h.of(c), 1)

            for i in range(3):
                if i:
                    m_seg.end(act, f"mean{i - 1}")
                run(act, f"mean{i}", [(0, mean_keep)], NC)
            y_done.end(act, "dense")
            run(act, "dst", chain, NC)
            y_done.end(act, "dst")

            def att_keep(i):
                def f(c):
                    item, y = c.item(3, i), c.item(3, 1)
                    act.wait_ge(a_turned.of(item), a_turned.after(item))
                    if i == 1:
                        act.wait_ge(y_done.of(y), y_done.after(y, 12))
                        to = src_t[:, c.slot(4), :]
                    else:
                        act.wait_ge(a_v_psum.of(c), a_v_psum.after(c, 2))
                        to = (h2 if i else h0)[:, c.slot(2), :]
                    act.activation(to, bank[0][:, :], ACT.Copy).then_inc(a_kept.of(item), 1)
                return f

            def node_keep(half):
                def f(c):
                    item, node = c.item(3, 2 * half), c.item(2, half)
                    act.wait_ge(f_turned.of(node), f_turned.after(node))
                    act.wait_ge(y_done.of(item), y_done.after(item, 6))
                    act.activation(node_t[:, node.slot(4), :], bank[1][:, :], ACT.Copy).then_inc(f_kept.of(node), 1)
                return f

            def att_k(c):
                act.wait_ge(a_qk_psum.of(c), a_qk_psum.after(c))
                act.wait_ge(a_qk.of(c), a_qk.free(c))
                act.activation(k_sb[:, :], bank[3][:, :], ACT.Copy).then_inc(a_k.of(c), 1)

            def att_v(c):
                act.wait_ge(a_v_psum.of(c), a_v_psum.after(c))
                act.wait_ge(a_wv.of(c), a_wv.after(c, 2))
                act.activation(v_sb[:, c.slot(2), :], bank[4][:, :], ACT.Copy).then_inc(a_v.of(c), 1)

            def att_exp(c):
                act.wait_ge(a_dmax.of(c), a_dmax.after(c))
                act.wait_ge(a_num.of(c), a_num.after(c, 1))
                act.activation(decay[:, :], dmax[:, 0, :], ACT.Exp)
                act.activation(weight[:, :], dmax[:, 1, :], ACT.Exp).then_inc(a_exp.of(c), 1)

            def att_reciprocal(c):
                act.wait_ge(a_den.of(c), a_den.after(c))
                act.wait_ge(a_agg.of(c), a_agg.after(c, 1))
                act.activation(qr[:, :], den[:, c.slot(2), :], ACT.Ln).then_inc(a_rlog.of(c), 1)
                act.wait_ge(a_rlog.of(c), a_rlog.after(c))
                act.activation(qr[:, :], qr[:, :], ACT.Exp, scale=-1.0).then_inc(a_rden.of(c), 1)

            def root(i):
                return lambda c: inverse_root(c.item(3, i))

            def node_norm(half):
                def f(c):
                    item, node = c.item(3, 2 * half), c.item(2, half)
                    s = norm_slot(item)
                    act.wait_ge(n_shift.of(node), n_shift.after(node))
                    act.wait_ge(x_out.of(item), x_out.free(item))
                    for t in range(TPC):
                        last = act.activation(normed[:, item.slot(4), t, :], res[:, s, t, :], ACT.Identity,
                                              bias=shift[:, s, t:t + 1], scale=rstd[:, s, t:t + 1])
                    last.then_inc(n_node.of(node), 1)
                return f

            run(act, "attend", [(0, root(0)), (0, root(1)), (2, att_k), (0, root(2)), (0, node_norm(0)),
                                (3, att_keep(0)), (1, node_keep(0)), (3, att_keep(1)), (1, att_exp), (1, node_keep(1)),
                                (3, att_keep(2)), (1, att_reciprocal), (2, att_v), (0, node_norm(1))], NC)

        @block.vector
        def _(dve):
            done = [0]

            def link(ins):
                done[0] += 1
                ins.then_inc(dve_step, 1)
                dve.wait_ge(dve_step, done[0])

            dve.memset(kin[:, :, :], N).then_inc(pad_ready, 1)
            dve.memset(zrow[:, :], 0.0).then_inc(pad_ready, 1)
            link(dve.memset(ones[:, :], 1.0))
            link(dve.memset(ones3[:, :], 1.0))
            link(dve.memset(eps[:, :], EPS))
            link(dve.memset(carry_row[:, :, :], 0.0))
            link(dve.memset(seg[:, :, :], 0.0))

            dve.wait_ge(w_turned, 7)
            link(dve.tensor_copy(wt[:, 0:4, :], by_tile(bank[2][:, :])))
            dve.tensor_copy(wt[:, 4:7, :], bank[3][:, 0:3 * P].rearrange("p (t d) -> p t d", t=3)).then_inc(w_ready, 1)
            dve.wait_ge(w_ready, 1)
            dve.wait_ge(vo_done, 1)
            link(dve.tensor_copy(wt[:, T_VO, :], bank[4][:, 0:D]))
            link(dve.tensor_scalar(wt[:, T_NOUT, :], wraw[:, W_OUT, :], -1.0, None, ALU.mult))
            dve.wait_ge(small_loaded, 16 * (H + 3))
            link(dve.tensor_scalar(wexp_rep[:, :, :], wexp_rows[:, :].rearrange("p (h a) -> p h a", a=1).to_broadcast([P, H, HD]),
                                   float(HD) ** -0.5, None, ALU.mult))
            link(dve.tensor_copy(b2part[:, 0, :], b2[:, :]))
            link(dve.tensor_tensor(b2rest[:, 0, :], b2[:, :], b2part[:, 0, :], ALU.subtract))
            link(dve.tensor_copy(b2part[:, 1, :], b2rest[:, 0, :]))
            link(dve.tensor_tensor(b2rest[:, 1, :], b2rest[:, 0, :], b2part[:, 1, :], ALU.subtract))
            link(dve.tensor_copy(b2part[:, 2, :], b2rest[:, 1, :]))
            for i in range(3):
                link(dve.tensor_scalar(b2mask[:, i, :], b2part[:, i, :], ident[0:3, i:i + 1], None, ALU.mult))
            link(dve.tensor_tensor(b2mask[:, 0, :], b2mask[:, 0, :], b2mask[:, 1, :], ALU.add))
            link(dve.tensor_tensor(b2mask[:, 0, :], b2mask[:, 0, :], b2mask[:, 2, :], ALU.add))
            for t in range(TPC):
                link(dve.tensor_copy(b2row[:, t, :], b2mask[:, 0, :]))

            w = [one[:, :] for one in work]
            a_bits, b_bits = V[0][:, 0, :].bitcast(I32), V[0][:, 1, :].bitcast(I32)
            dve.wait_ge(keys_loaded, 64)
            dst_k, src_k = kin[:, 0, :], kin[:, 1, :]
            link(dve.tensor_scalar(w[0], dst_k, float(HALF), None, ALU.is_lt))
            link(dve.tensor_scalar(w[1], dst_k, -float(HALF), None, ALU.add))
            link(dve.tensor_scalar(w[2], w[0], -2.0, 1.0, ALU.mult, ALU.add))
            link(dve.tensor_tensor(w[1], w[1], w[2], ALU.mult))
            link(dve.tensor_scalar(w[1], w[1], float(MAG0), None, ALU.add))
            link(dve.tensor_scalar(w[1], w[1], 16, None, ALU.logical_shift_left))
            link(dve.tensor_scalar(w[0], w[0], 31, None, ALU.logical_shift_left))
            link(dve.tensor_tensor(w[1], w[1], w[0], ALU.bitwise_or))
            link(dve.tensor_tensor(a_bits, w[1], src_k, ALU.bitwise_or))
            link(dve.tensor_scalar(w[3], src_k, float(SRC0), None, ALU.add))
            link(dve.tensor_scalar(w[3], w[3], 15, None, ALU.logical_shift_left))
            link(dve.tensor_tensor(b_bits, w[3], pos[:, :], ALU.bitwise_or))
            link(dve.tensor_scalar(w[4], pos[:, :], 1, None, ALU.logical_shift_right))
            for i in range(2):
                link(dve.tensor_tensor(gray[:, i, :], pos[:, :], w[4], ALU.bitwise_xor))
                link(dve.tensor_scalar(flip[:, 0, i, :], w[4], 31, None, ALU.logical_shift_left))
            all_bits = V[0][:, :, :].bitcast(I32)
            dve.tensor_tensor(all_bits, all_bits, flip[:, 0, :, :], ALU.bitwise_xor).then_inc(sort_step, 2)

            steps = turns = side = 0
            in_psum = False
            flat = [one[:, :, :].rearrange("p w f -> p (w f)") for one in V]
            now = flat[0]
            for what, n in plan:
                if what == "turn":
                    turns += 1
                    dve.wait_ge(turned, turns)
                    now = bank[(turns - 1) % 2][:, :]
                    in_psum = True
                    continue
                if what == "flip":
                    one = flip[:, n % 2, :, :]
                    link(dve.tensor_scalar(one, gray[:, :, :], n, None, ALU.logical_shift_right))
                    link(dve.tensor_scalar(one, one, 31, None, ALU.logical_shift_left))
                    dve.wait_ge(sort_step, 2 * steps + 2)
                    bits = V[side][:, :, :].bitcast(I32)
                    dve.tensor_tensor(bits, bits, one, ALU.bitwise_xor).then_inc(sort_step, 2)
                    steps += 1
                    continue
                pairs = now.rearrange("p (g two s) -> p g two s", two=2, s=n)
                upper = pairs[:, :, 1, :]
                if in_psum:
                    upper = flat[side].rearrange("p (g two s) -> p g two s", two=2, s=n)[:, :, 1, :]
                    link(dve.tensor_copy(upper, pairs[:, :, 1, :]))
                    in_psum = False
                side ^= 1
                to = flat[side].rearrange("p (g two s) -> p g two s", two=2, s=n)
                dve.wait_ge(sort_step, 2 * steps + 2)
                dve.tensor_tensor(to[:, :, 0, :], pairs[:, :, 0, :], upper, ALU.min).then_inc(sort_step, 1)
                dve.tensor_tensor(to[:, :, 1, :], pairs[:, :, 0, :], upper, ALU.max).then_inc(sort_step, 1)
                steps += 1
                now = flat[side]
            dve.wait_ge(sort_step, 2 * steps + 2)

            va, vb = V[side][:, 0, :].bitcast(I32), V[side][:, 1, :].bitcast(I32)
            for i, (v, n) in enumerate(((va, 16), (vb, 15))):
                link(dve.tensor_scalar(w[i], v, n, None, ALU.logical_shift_right))
                link(dve.tensor_scalar(keyf[:, i, :].bitcast(I32), w[i], n, None, ALU.logical_shift_left))
            dve.memset(work[5][:, 0:1], 0.0).then_inc(keys_made, 1)
            link(dve.tensor_scalar(w[2], va, 31, None, ALU.logical_shift_right))
            link(dve.tensor_scalar(w[2], w[2], 1, None, ALU.bitwise_and))
            link(dve.tensor_scalar(w[2], w[2], -2.0, 1.0, ALU.mult, ALU.add))
            link(dve.tensor_scalar(w[0], w[0], 0x7FFF, None, ALU.bitwise_and))
            link(dve.tensor_scalar(w[0], w[0], -float(MAG0), None, ALU.add))
            link(dve.tensor_tensor(w[0], w[0], w[2], ALU.mult))
            link(dve.tensor_scalar(w[0], w[0], float(HALF), None, ALU.add))
            link(dve.tensor_scalar(w[3], va, 0xFFFF, None, ALU.bitwise_and))
            link(dve.tensor_scalar(w[1], w[1], -float(SRC0), None, ALU.add))
            link(dve.tensor_scalar(w[4], vb, 0x7FFF, None, ALU.bitwise_and))
            for to, v, most in ((V_SRC_A, w[3], N - 1), (V_DST_A, w[0], N - 1), (V_ID_B, w[4], E - 1), (V_SRC_B, w[1], N - 1)):
                link(dve.tensor_scalar(value[:, to, :], v, float(most), None, ALU.min))
            link(dve.tensor_copy(value[:, V_POS, :], pos[:, :]))
            dve.wait_ge(near_in, 64)
            link(dve.tensor_tensor(same[:, :], keyf[:, 0, :], near[:, 0, 0, :], ALU.is_equal))
            link(dve.tensor_tensor(resetf[:, :], keyf[:, 1, :], near[:, 1, 0, :], ALU.not_equal))
            dve.tensor_scalar(resetf[:, :], resetf[:, :], RESET, None, ALU.mult).then_inc(flags_made, 1)
            for i, (to, v) in enumerate(((V_PUT_A, w[0]), (V_PUT_B, w[1]))):
                link(dve.tensor_tensor(near[:, i, 1, :], keyf[:, i, :], near[:, i, 1, :], ALU.is_equal))
                link(dve.tensor_scalar(near[:, i, 1, :], near[:, i, 1, :], FAR, None, ALU.mult))
                link(dve.tensor_tensor(value[:, to, :], near[:, i, 1, :], v, ALU.add))
            link(dve.tensor_tensor_scan(local[:, 0, :], same[:, :], ones[:, :], 0.0, ALU.mult, ALU.add))
            dve.tensor_tensor_scan(local[:, 1, :], same[:, :], ones[:, :], 1.0, ALU.mult, ALU.mult).then_inc(carry_made, 1)
            dve.wait_ge(carry_turned, 2)
            for i in range(2):
                link(dve.tensor_copy(carry_row[0:1, i, 0:P], bank[2 + i][0:1, 0:P]))
            dve.tensor_tensor_scan(carry_row[0:1, 2, 1:P + 1], carry_row[0:1, 1, 0:P], carry_row[0:1, 0, 0:P], 0.0,
                                   ALU.mult, ALU.add).then_inc(carry_made, 1)
            dve.wait_ge(carry_turned, 3)
            link(dve.tensor_copy(carry_col[:, :], bank[4][:, 0:1]))
            link(dve.tensor_scalar(local[:, 1, :], local[:, 1, :], carry_col[:, 0:1], None, ALU.mult))
            link(dve.tensor_tensor(local[:, 0, :], local[:, 0, :], local[:, 1, :], ALU.add))
            dve.reciprocal(value[:, V_INV, :], local[:, 0, :]).then_inc(value_ready, 1)
            for i in range(8):
                dve.wait_ge(value_turned, i + 1)
                to = col_i[:, i, :] if i < 6 else col_f[:, i - 6, :]
                link(dve.tensor_copy(to.rearrange("q (p a) -> q a p", a=2), bank[i][:, 0:LINE].rearrange("q (a p) -> q a p", a=2)))
            dve.memset(work[5][:, 0:1], 0.0).then_inc(cols_ready, 1)

            def add(rows, c):
                s = norm_slot(c)
                y = by_tile(bank[6 + c.slot(2)][:, :])
                dve.wait_ge(y_done.of(c), y_done.after(c))
                wait_norm_slot(dve, c)
                if c.phase == "dst":
                    dve.tensor_tensor(res[:, s, :, :], y, rows, ALU.add).then_inc(added0.of(c), 1)
                    dve.wait_ge(added0.of(c), added0.after(c))
                    dve.wait_ge(pl_in.of(c), pl_in.after(c))
                    dve.tensor_tensor(res[:, s, :, :], res[:, s, :, :], PL[:, c.slot(U), 2, :, :], ALU.add).then_inc(added.of(c), 1)
                else:
                    dve.tensor_tensor(res[:, s, :, :], y, rows, ALU.add).then_inc(added.of(c), 1)
                dve.wait_ge(added.of(c), added.after(c))
                for t in range(TPC):
                    last = dve.bn_stats(stats[:, s, t, :], res[:, s, t, :])
                last.then_inc(n_stats.of(c), 1)
                dve.wait_ge(n_stats.of(c), n_stats.after(c))
                hold(dve, "dve")
                for t in range(TPC):
                    last = dve.bn_aggr(mv[:, s, t, :], stats[:, s, t, :])
                last.then_inc(n_aggr.of(c), 1)

            def norm(c):
                s, (sig, what, _) = norm_slot(c), normed_by(c)
                dve.wait_ge(n_rstd.of(c), n_rstd.after(c))
                if c.phase == "dst":
                    dve.wait_ge(put_free.of(c), put_free.free(c))
                else:
                    dve.wait_ge(x_out.of(c), x_out.free(c))
                for t in range(TPC):
                    last = dve.tensor_scalar(normed[:, c.slot(4), t, :], res[:, s, t, :], mv[:, s, t, 0:1],
                                             rstd[:, s, t:t + 1], ALU.subtract, ALU.mult)
                last.then_inc(sig.of(what), 1)

            def add_x(c):
                add(XN[:, c.slot(U), :, :], c)

            def add_gathered(c):
                add(GX[:, c.slot(U), :, 0:D], c)

            run(dve, "dense", [(1, add_x), (0, norm)], NN)

            def mean_seg(c):
                dve.wait_ge(m_h.of(c), m_h.after(c))
                dve.wait_ge(flag_in.of(c), flag_in.after(c))
                dve.wait_ge(m_prod.of(c), m_prod.free(c))
                before = c.before()
                dve.wait_ge(m_seg.of(before), m_seg.after(before))
                dve.tensor_tensor_scan(seg[:, c.slot(2), :], flag[:, c.slot(4), :], take_cols(hsrc, c.index() * CH, CH),
                                       seg[:, before.slot(2), CH - 1:CH], ALU.mult, ALU.add).then_inc(m_seg.of(c), 1)
                if c.phase == "mean0":
                    dve.wait_ge(gathered.of(c), gathered.after(c))
                    dve.tensor_copy(take_cols(lookup, c.index() * TPC, TPC), GX[:, c.slot(U), :, D:D + 1].rearrange("p t a -> p (t a)"))\
                       .then_inc(m_look.of(c), 1)

            def mean_scale(c):
                dve.wait_ge(m_prod.of(c), m_prod.after(c))
                dve.wait_ge(m_stored.of(c), m_stored.free(c))
                inv = take_cols(col_f[:, 1, :], c.index() * TPC, TPC).rearrange("p (t a) -> p t a", a=1).to_broadcast([P, TPC, D])
                dve.tensor_tensor(prod[:, c.slot(4), :, :], by_tile(bank[2 + c.slot(2)][:, :]), inv, ALU.mult)\
                   .then_inc(m_scaled.of(c), 1)

            for i in range(3):
                run(dve, f"mean{i}", [(1, mean_seg), (0, mean_scale)], NC)

            x_out.end(dve, "dense")
            run(dve, "dst", [(1, add_gathered), (0, norm)], NC)
            put_done.end(dve, "dst")

            for sums in (runmax, den, num):
                link(dve.memset(sums[:, :, :], 0.0))

            def att_qk(c):
                dve.wait_ge(a_k.of(c), a_k.after(c))
                dve.wait_ge(a_logit.of(c), a_logit.free(c))
                dve.tensor_tensor(qk[:, :], bank[2][:, :], k_sb[:, :], ALU.mult).then_inc(a_qk.of(c), 1)

            def att_max(c):
                s, before = c.slot(2), c.before()
                top, prev = runmax[:, s, 1:CH + 1], runmax[:, s, 0:CH]
                reset, logit = flag[:, c.slot(4), :], bank[5][:, :]
                dve.wait_ge(a_max.of(before), a_max.after(before))
                dve.tensor_copy(runmax[:, s, 0:1], runmax[:, before.slot(2), CH:CH + 1]).then_inc(a_carry.of(c), 1)
                dve.wait_ge(a_carry.of(c), a_carry.after(c))
                dve.wait_ge(flag_in.of(c), flag_in.after(c))
                dve.wait_ge(a_logit.of(c), a_logit.after(c))
                dve.tensor_tensor_scan(top, reset, logit, runmax[:, s, 0:1], ALU.add, ALU.max).then_inc(a_max.of(c), 1)
                dve.wait_ge(a_exp.of(c), a_exp.free(c))
                dve.wait_ge(a_max.of(c), a_max.after(c))
                dve.tensor_tensor(dmax[:, 0, :], prev, reset, ALU.add).then_inc(a_step1.of(c), 1)
                dve.tensor_tensor(dmax[:, 1, :], logit, top, ALU.subtract)
                dve.wait_ge(a_step1.of(c), a_step1.after(c))
                dve.tensor_tensor(dmax[:, 0, :], dmax[:, 0, :], top, ALU.subtract).then_inc(a_dmax.of(c), 1)

            def att_sums(c):
                s, before = c.slot(2), c.before()
                dve.wait_ge(a_exp.of(c), a_exp.after(c))
                dve.wait_ge(a_den.of(before), a_den.after(before))
                dve.tensor_tensor_scan(den[:, s, :], decay[:, :], weight[:, :], den[:, before.slot(2), CH - 1:CH],
                                       ALU.mult, ALU.add).then_inc(a_den.of(c), 1)
                dve.wait_ge(a_v.of(c), a_v.after(c))
                dve.tensor_tensor(weight[:, :], weight[:, :], v_sb[:, s, :], ALU.mult).then_inc(a_wv.of(c), 1)
                dve.wait_ge(a_wv.of(c), a_wv.after(c))
                dve.wait_ge(a_num.of(before), a_num.after(before))
                dve.tensor_tensor_scan(num[:, s, :], decay[:, :], weight[:, :], num[:, before.slot(2), CH - 1:CH],
                                       ALU.mult, ALU.add).then_inc(a_num.of(c), 1)
                item = c.item(3, 1)
                dve.wait_ge(a_rden.of(c), a_rden.after(c))
                dve.wait_ge(a_num.of(c), a_num.after(c))
                dve.wait_ge(y_done.of(item), y_done.after(item, 6))
                dve.tensor_tensor(agg[:, s, :], num[:, s, :], qr[:, :], ALU.mult).then_inc(a_agg.of(c), 1)

            def att_add(i):
                def f(c):
                    rows = GP[:, c.slot(U), :, :] if i == 1 else XN[:, c.item(2, i // 2).slot(U), :, :]
                    add(rows, c.item(3, i))
                return f

            def att_norm(c):
                norm(c.item(3, 1))

            def node_shift(half):
                def f(c):
                    item, node = c.item(3, 2 * half), c.item(2, half)
                    s = norm_slot(item)
                    dve.wait_ge(n_rstd.of(item), n_rstd.after(item))
                    dve.scalar_tensor_tensor(shift[:, s, :], mv[:, s, :, 0], -1.0, rstd[:, s, :], ALU.mult, ALU.mult)\
                       .then_inc(n_shift.of(node), 1)
                return f

            run(dve, "attend", [(0, att_add(0)), (0, att_add(1)), (0, node_shift(0)), (0, att_add(2)), (0, att_norm),
                                (0, node_shift(1)), (1, att_max), (2, att_qk), (1, att_sums)], NC)


_INS = ["x", "src", "dst", "edge_attr_128", "L0_gnn_Wl0", "L0_gnn_bl0", "L0_gnn_Wr0", "L0_gnn_Wl1", "L0_gnn_bl1",
        "L0_gnn_Wr1", "L0_gnn_Wl2", "L0_gnn_bl2", "L0_gnn_Wr2", "L1_gnn_Wq", "L1_gnn_Wk", "L1_gnn_Wv", "L1_gnn_Wek",
        "L1_gnn_Wev", "L1_gnn_W_exp", "L1_gnn_W_out"]


def kernel(**inputs):
    import numpy as _np
    import concourse.bacc as _bacc
    from concourse import mybir as _mybir
    from concourse.bass_utils import run_bass_kernel_spmd as _run

    nc = _bacc.Bacc("TRN2", target_bir_lowering=False, num_devices=1)
    arrays, args = {}, []
    for name in _INS:
        a = _np.ascontiguousarray(inputs[name])
        arrays[f"in_{name}_dram"] = a
        args.append(nc.dram_tensor(f"in_{name}_dram", a.shape, _mybir.dt.from_np(a.dtype), kind="ExternalInput").ap())
    x = arrays["in_x_dram"]
    args.append(nc.dram_tensor("out_0_dram", x.shape, _mybir.dt.from_np(x.dtype), kind="ExternalOutput").ap())
    gnn_kernel(nc, *args)
    r = _run(nc, [arrays], core_ids=[0])
    return r.results[0]["out_0_dram"]
```

```python
from contextlib import ExitStack

import concourse.bass as bass
from concourse import mybir

F32 = mybir.dt.float32
I32 = mybir.dt.int32
BF16 = mybir.dt.bfloat16
ALU = mybir.AluOpType
ACT = mybir.ActivationFunctionType

P = 128
TPC = 4
CH = P * TPC
U = 8
EXTRA = 9
BLOCK = 4
LINE = 256
SORT = P * LINE
LOGN = SORT.bit_length() - 1
EPS = 1e-5
RESET = -1e38
FAR = float(1 << 20)


class At:

    def __init__(self, phase, j, u, last=False, per=U):
        self.phase, self.j, self.u, self.last, self.per = phase, j, u, last, per

    def index(self):
        return self.j * self.per + self.u

    def slot(self, n):
        return self.u % n

    def use(self, n):
        return self.j * (self.per // n) + self.u // n

    def ahead(self, k):
        return At(self.phase, self.j, self.u + k, per=self.per)

    def later(self, phase, chunks):
        return At(phase, self.j, self.u + chunks, self.last)

    def item(self, n, i):
        return At(self.phase, self.j, self.u * n + i, self.last and i == n - 1, self.per * n)

    def chunk(self, n):
        return At(self.phase, self.j, self.u // n, self.last, self.per // n)


class Signal:

    def __init__(self, semaphore, name, buffers, by, phases, credit=None):
        self.n = buffers if by % 16 == 0 else 1
        self.sems = [semaphore(f"{name}{i}") for i in range(self.n)]
        self.buffers, self.by, self.phases = buffers, by, phases
        self.credit = (1 if self.n > 1 else 3 * U) if credit is None else credit

    def _had(self, phase, slot, whole):
        had = 0
        for name, chunks in self.phases:
            if name == phase and not whole:
                break
            had += -(-(chunks - slot) // self.n)
            if name == phase:
                break
        return had

    def of(self, c):
        return self.sems[c.slot(self.n)]

    def after(self, c, ago=0):
        assert ago % self.n == 0
        return (c.use(self.n) + (self._had(c.phase, c.slot(self.n), False) + 1 - ago // self.n + self.credit)) * self.by

    def free(self, c):
        return self.after(c, self.buffers)

    def earlier(self, eng, c, chunks):
        for slot in range(self.n):
            had = self._had(c.phase, slot, False) + -(-(chunks - 1 - slot) // self.n)
            eng.wait_ge(self.sems[slot], (had + self.credit) * self.by)

    def end(self, eng, phase):
        for slot in range(self.n):
            eng.wait_ge(self.sems[slot], (self._had(phase, slot, True) + self.credit) * self.by)


def run(eng, phase, stages, count, to_end=True):
    stages = [(*one, count)[:3] for one in stages]
    whole = min(chunks - 1 - lead for lead, _, chunks in stages) // U

    def single(s):
        for lead, f, chunks in stages:
            if 0 <= s + lead < chunks:
                f(At(phase, (s + lead) // U, (s + lead) % U, to_end and s + lead == chunks - 1))

    for s in range(-max(lead for lead, _, _ in stages), 0):
        single(s)
    with eng.Fori(0, whole) as j:
        for u in range(U):
            for lead, f, _ in stages:
                f(At(phase, j, u + lead))
    for s in range(whole * U, count):
        single(s)


def take(ap, start, n):
    return ap[start:start + n] if isinstance(start, int) else ap[bass.ds(start, n)]


def take_cols(ap, start, n):
    return ap[:, start:start + n] if isinstance(start, int) else ap[:, bass.ds(start, n)]


def by_tile(ap):
    return ap.rearrange("p (t d) -> p t d", t=TPC)


def gnn_kernel(nc, x, src, dst, ea, Wl0, bl0, Wr0, Wl1, bl1, Wr1, Wl2, bl2, Wr2,
               Wq, Wk, Wv, Wek, Wev, Wexp, Wout, out):
    N, D = x.shape
    E = src.shape[0]
    H = Wexp.shape[0]
    HD = D // H
    NC = -(-E // CH)
    NN = -(-N // CH)
    FIRST = NN - NC + EXTRA
    SECOND = NN - FIRST
    EP = NC * CH
    XW = D + 4
    HALF = N // 2
    MAG0, SRC0 = 128, 512
    assert D == P and N <= 50432 and E < 1 << 15 and EP <= SORT and NN == 2 * NC

    def dram(name, shape, dt=F32):
        return nc.dram_tensor(name, shape, dt, kind="Internal").ap()

    xe = dram("x_with_lookup", (N, XW))
    eae = dram("edge_attr_with_dst", (E, XW))
    xp = dram("x_prime", (N, D))
    attended = dram("attended", (EP, D))
    prod_table = [dram(f"mean_product{i}", (EP + P, D)) for i in range(3)]
    key_row = [dram(f"key_row{w}", (SORT + 2,)) for w in range(2)]
    same_row = dram("same_dst_row", (SORT,))
    reset_row = dram("reset_src_row", (SORT,))

    with ExitStack() as ctx:
        def sb(name, shape, dt=F32):
            return ctx.enter_context(nc.sbuf_tensor(name, shape, dt))

        def sem(name):
            return ctx.enter_context(nc.semaphore(name))

        bank = [ctx.enter_context(nc.psum_tensor(f"bank{i}", [P, CH], F32)) for i in range(8)]

        ident = sb("ident", [P, P])
        ones = sb("ones", [P, LINE])
        eps = sb("eps", [P, 1])
        zrow = sb("zrow", [P, D])
        wraw = sb("wraw", [P, 12, D])
        wt = sb("wt", [P, 9, D])
        wexp_rows = sb("wexp_rows", [P, H])
        wexp_rep = sb("wexp_rep", [P, H, HD])
        bcol = sb("bcol", [P, 2])
        b2 = sb("b2", [3, D])
        b2part = sb("b2part", [3, 3, D], BF16)
        b2rest = sb("b2rest", [3, 2, D])
        b2mask = sb("b2mask", [3, 3, D], BF16)
        b2row = sb("b2row", [3, TPC, D], BF16)
        ones3 = sb("ones3", [3, P], BF16)
        hsrc = sb("hsrc", [P, EP])
        carved = [0]

        def part(shape, dt=F32):
            n = 1
            for k in shape:
                n *= k
            ap = hsrc[:, carved[0]:carved[0] + n]
            carved[0] += n
            names = " ".join("abcd"[:len(shape)])
            if len(shape) > 1:
                ap = ap.rearrange(f"p ({names}) -> p {names}", **dict(zip("abcd", shape[:-1])))
            return ap if dt == F32 else ap.bitcast(dt)

        kin = part([2, LINE], I32)
        pos = part([LINE], I32)
        gray = part([2, LINE], I32)
        flip = part([2, 2, LINE], I32)
        V = [part([2, LINE]) for _ in range(2)]
        work = [part([LINE], I32) for _ in range(6)]
        keyf = part([2, LINE])
        near = part([2, 2, LINE])
        same = part([LINE])
        resetf = part([LINE])
        local = part([2, LINE])
        value = part([8, LINE])
        carry_row = sb("carry_row", [1, 3, P + 1])
        carry_col = sb("carry_col", [P, 1])
        col_f = sb("col_f", [P, 2, LINE])
        col_i = sb("col_i", [P, 6, LINE], I32)
        lookup = sb("lookup", [P, LINE], I32)
        XB = part([U, TPC, XW])
        dsti = sb("dsti", [P, 4, TPC], I32)
        XN = sb("XN", [P, U, TPC, D])
        XN_flat = XN[:, :, :, :].rearrange("p s t d -> p (s t d)")
        EB = XN_flat[:, 0:4 * TPC * XW].rearrange("p (s t d) -> p s t d", s=4, t=TPC)
        GX = sb("GX", [P, U, TPC, XW])
        idx_a = sb("idx_a", [P, U, TPC], I32)
        idx_b = sb("idx_b", [P, U, TPC], I32)
        idx_c = sb("idx_c", [P, U, TPC], I32)
        idx_d = sb("idx_d", [P, U, TPC], I32)
        lval = sb("lval", [P, U, TPC])
        flag = sb("flag", [P, 4, CH])
        h0, h1, h2 = (sb(f"h{i}", [P, 2, CH]) for i in range(3))
        seg = sb("seg", [P, 2, CH])
        prod = sb("prod", [P, 4, TPC, D])
        res = sb("res", [P, 3, TPC, D])
        normed = sb("normed", [P, 4, TPC, D])
        stats = sb("stats", [P, 3, TPC, 6])
        mv = sb("mv", [P, 3, TPC, 2])
        logv = sb("logv", [P, 3, TPC])
        rstd = sb("rstd", [P, 3, TPC])
        shift = sb("shift", [P, 3, TPC])

        carved[0] = 0
        PL = part([U, 3, TPC, D])
        carved[0] = 0
        GP = part([U, TPC, D])
        GD = part([U, TPC, D])
        qk = part([CH])
        k_sb = part([CH])
        v_sb = part([2, CH])
        src_t = part([4, CH])
        node_t = part([4, CH])
        qr = part([CH])
        runmax = part([2, CH + 1])
        dmax = part([2, CH])
        decay = part([CH])
        weight = part([CH])
        den = part([2, CH])
        num = part([2, CH])
        agg = part([2, CH])

        (W_L0, W_R0, W_L1, W_R1, W_L2, W_R2, W_V, W_OUT, W_Q, W_K, W_EK, W_EV) = range(12)
        W_FILES = [Wl0, Wr0, Wl1, Wr1, Wl2, Wr2, Wv, Wout, Wq, Wk, Wek, Wev]
        T_L, T_R, T_V, T_OUT, T_NOUT = (0, 2, 4), (1, 3, 5), 6, 7, 8
        V_SRC_A, V_DST_A, V_PUT_A, V_ID_B, V_SRC_B, V_PUT_B, V_POS, V_INV = range(8)

        go = sem("go")
        held = {e: sem(f"held_{e}") for e in ("sp", "pool", "dve")}
        pool_const = sem("pool_const")
        keys_loaded = sem("keys_loaded")
        w_loaded = sem("w_loaded")
        small_loaded = sem("small_loaded")
        dve_step = sem("dve_step")
        w_turned = sem("w_turned")
        w_ready = sem("w_ready")
        vo_done = sem("vo_done")
        sort_step = sem("sort_step")
        turned = sem("turned")
        keys_out, near_in, rows_out = sem("keys_out"), sem("near_in"), sem("rows_out")
        keys_made, flags_made = sem("keys_made"), sem("flags_made")
        carry_turned = sem("carry_turned")
        carry_made = sem("carry_made")
        value_ready = sem("value_ready")
        value_turned = sem("value_turned")
        cols_ready = sem("cols_ready")
        zero_out = sem("zero_out")
        pad_ready = sem("pad_ready")
        all_out = sem("all_out")

        signals = []

        def signal(name, buffers, by, phases, credit=None):
            signals.append(Signal(sem, name, buffers, by, phases, credit))
            return signals[-1]

        XE, EA, LK = [("xe", NN)], [("mean1", NC)], [("lk", NC)]
        xe_in, xe_out = signal("xe_in", U, 16, XE), signal("xe_out", U, 16, XE)
        ea_in, ea_out = signal("ea_in", 4, 32, EA), signal("ea_out", 4, 16, EA)
        ea_dst = signal("ea_dst", 4, 1, EA)
        MEANS = [(f"mean{i}", NC) for i in range(3)]
        CHAIN = [("dense", NN), ("dst", NC)]
        NODES = [("dense", NN), ("attend", NN)]
        NORM = [("dense", NN), ("dst", NC), ("attend", 3 * NC)]
        DST, ATT, REST = [("dst", NC)], [("attend", NC)], [("rest", NC)]
        ATT2, ATT3 = [("attend", 2 * NC)], [("attend", 3 * NC)]
        POOLED = [("lk", NC), *MEANS, ("dst", NC)]
        idx_ready = signal("idx_ready", U, 1, POOLED + ATT)
        put_ready = signal("put_ready", U, 1, DST + REST)
        gathered = signal("gathered", U, 64, MEANS + DST + ATT, 0)
        m_turned = signal("m_turned", 2, 1, MEANS)
        m_h = signal("m_h", 2, 1, MEANS)
        m_seg = signal("m_seg", 2, 1, MEANS)
        m_prod = signal("m_prod", 2, 1, MEANS)
        m_scaled = signal("m_scaled", 2, 1, MEANS)
        m_stored = signal("m_stored", 4, 16, MEANS)
        m_look = signal("m_look", U, 1, [("mean0", NC)])
        flag_in = signal("flag_in", 4, 16, MEANS + ATT)
        x_in = signal("x_in", U, 16, NODES + REST)
        pl_in = signal("pl_in", U, 48, DST)
        t_done, t_kept = signal("t_done", 2, 1, CHAIN), signal("t_kept", 2, 1, CHAIN)
        u1_done, u1_kept = signal("u1_done", 2, 1, CHAIN), signal("u1_kept", 2, 1, CHAIN)
        u2_done, u2_kept = signal("u2_done", 2, 1, CHAIN), signal("u2_kept", 2, 1, CHAIN)
        y_done = signal("y_done", 2, 1, NORM)
        added0 = signal("added0", 2, 1, DST)
        added = signal("added", 2, 1, CHAIN)
        n_stats, n_aggr = signal("n_stats", 2, 1, NORM), signal("n_aggr", 2, 1, NORM)
        n_log, n_rstd = signal("n_log", 2, 1, NORM), signal("n_rstd", 2, 1, NORM)
        n_done = signal("n_done", 2, 1, [("dense", NN), ("dst", NC), ("attend", NC)])
        x_out = signal("x_out", 4, 16, [("dense", NN), ("attend", 3 * NC)])
        put_done = signal("put_done", 4, 64, LK + DST + REST, 0)
        put_free = signal("put_free", 4, 1, DST + REST)
        ea_got = signal("ea_got", U, 64, ATT, 0)
        dst_got = signal("dst_got", U, 64, ATT, 0)
        dst_idx = signal("dst_idx", U, 1, ATT)
        n_shift, n_node = signal("n_shift", 1, 1, ATT2), signal("n_node", 1, 1, ATT2)
        a_turned, a_kept = signal("a_turned", 1, 1, ATT3), signal("a_kept", 1, 1, ATT3)
        f_turned, f_kept = signal("f_turned", 1, 1, ATT2), signal("f_kept", 1, 1, ATT2)
        a_qk_psum, a_v_psum = signal("a_qk_psum", 1, 1, ATT), signal("a_v_psum", 1, 1, ATT)
        a_k, a_v = signal("a_k", 1, 1, ATT), signal("a_v", 1, 1, ATT)
        a_qk = signal("a_qk", 1, 1, ATT)
        a_logit = signal("a_logit", 1, 1, ATT)
        a_carry = signal("a_carry", 1, 1, ATT)
        a_max = signal("a_max", 2, 1, ATT)
        a_step1 = signal("a_step1", 1, 1, ATT)
        a_dmax = signal("a_dmax", 1, 1, ATT)
        a_exp = signal("a_exp", 1, 1, ATT)
        a_den = signal("a_den", 2, 1, ATT)
        a_wv = signal("a_wv", 1, 1, ATT)
        a_num = signal("a_num", 2, 1, ATT)
        a_rlog, a_rden = signal("a_rlog", 1, 1, ATT), signal("a_rden", 1, 1, ATT)
        a_agg = signal("a_agg", 2, 1, ATT)

        def lookup_column(c):
            return GX[:, c.slot(U), :, D:D + 1].rearrange("p t a -> p (t a)")

        def norm_slot(c):
            return c.slot(3 if c.phase == "attend" else 2)

        def norm_rows(c):
            return by_tile(bank[6 if c.u % 3 else 7][:, :]) if c.phase == "attend" else res[:, norm_slot(c), :, :]

        def normed_by(c):
            if c.phase != "attend":
                return n_done, c, 2
            if c.u % 3 == 0:
                return n_done, c.chunk(3), 1
            return n_node, c.chunk(3).item(2, c.u % 3 - 1), 2

        def wait_normed(eng, c):
            sig, what, _ = normed_by(c)
            eng.wait_ge(sig.of(what), sig.after(what))

        def wait_norm_slot(eng, c):
            sig, what, ago = normed_by(c)
            eng.wait_ge(sig.of(what), sig.after(what, ago))

        def hold(eng, name):
            eng.sem_inc(held[name], 1)

        def file_rows(table, rows, c):
            return take(table, rows - CH if c.last else c.index() * CH, CH).rearrange("(q t) d -> q t d", t=TPC)

        def sorted_rows(table, c):
            return take(table, c.index() * CH, CH).rearrange("(t q) d -> q t d", q=P)

        def on_all(row, c):
            return take(row, c.index() * CH, CH).rearrange("(a n) -> a n", a=1).to_broadcast([P, CH])

        def second(f):
            return lambda c: f(c.later("dense", FIRST))

        plan = []
        for k in range(1, LOGN + 1):
            if k > 8:
                plan.append(("turn", 0))
            for b in range(k - 1, -1, -1):
                if k > 8 and b == 7:
                    plan.append(("turn", 0))
                plan.append(("compare", 1 << (b - 8 if b > 7 else b)))
            if k < LOGN:
                plan.append(("flip", k))

        block = ctx.enter_context(nc.Block())

        @block.sync
        def _(sp):
            for s in signals:
                for one in s.sems:
                    if s.credit:
                        sp.sem_inc(one, s.credit * s.by)
            sp.sem_inc(go, 1)
            sp.wait_ge(pad_ready, 2)
            whole = E // LINE
            for w, row in enumerate((dst, src)):
                sp.dma_start(kin[0:whole, w, :], row[0:whole * LINE].rearrange("(p f) -> p f", f=LINE)).then_inc(keys_loaded, 16)
                sp.dma_start(kin[whole:whole + 1, w, 0:E - whole * LINE], row[whole * LINE:E].rearrange("(a f) -> a f", a=1)).then_inc(keys_loaded, 16)
            for i, w in enumerate(W_FILES):
                sp.dma_start(wraw[:, i, :], w).then_inc(w_loaded, 16)
            for h in range(H):
                sp.dma_start(wexp_rows[HD * h:HD * (h + 1), :], Wexp[h:h + 1, :].to_broadcast([HD, H])).then_inc(small_loaded, 16)
            for i, b in enumerate((bl0, bl1)):
                sp.dma_start(bcol[:, i:i + 1], b.rearrange("(p a) -> p a", a=1)).then_inc(small_loaded, 16)
            sp.dma_start(b2[:, :], bl2.rearrange("(a n) -> a n", a=1).to_broadcast([3, D])).then_inc(small_loaded, 16)
            for i in range(2):
                sp.dma_start(prod_table[i][EP:EP + P, :], zrow[:, :]).then_inc(zero_out, 16)
            for w in range(2):
                for at in (0, SORT + 1):
                    sp.dma_start(key_row[w][at:at + 1].rearrange("(a n) -> a n", a=1), zrow[0:1, 0:1]).then_inc(zero_out, 16)

            sp.wait_ge(keys_made, 1)
            for w in range(2):
                sp.dma_start(key_row[w][1:SORT + 1].rearrange("(p f) -> p f", f=LINE), keyf[:, w, :]).then_inc(keys_out, 16)
            sp.wait_ge(keys_out, 32)
            sp.wait_ge(zero_out, 16 * 6)
            for w in range(2):
                for side in range(2):
                    sp.dma_start(near[:, w, side, :], key_row[w][2 * side:2 * side + SORT].rearrange("(p f) -> p f", f=LINE)).then_inc(near_in, 16)
            sp.wait_ge(flags_made, 1)
            sp.dma_start(same_row.rearrange("(p f) -> p f", f=LINE), same[:, :]).then_inc(rows_out, 16)
            sp.dma_start(reset_row.rearrange("(p f) -> p f", f=LINE), resetf[:, :]).then_inc(rows_out, 16)
            sp.wait_ge(rows_out, 32)

            def x_load(c):
                sp.wait_ge(added.of(c), added.after(c, U))
                sp.dma_start(XN[:, c.slot(U), :, :], file_rows(x, N, c)).then_inc(x_in.of(c), 16)

            def x_store(c):
                if c.last:
                    x_out.earlier(sp, c, NN)
                sp.wait_ge(n_done.of(c), n_done.after(c))
                sp.dma_start(file_rows(xp, N, c), normed[:, c.slot(4), :, :]).then_inc(x_out.of(c), 16)

            run(sp, "dense", [(7, x_load), (0, x_store)], FIRST, to_end=False)

            def flag_load(c):
                sig = m_seg if c.phase != "attend" else a_step1
                sp.wait_ge(sig.of(c), sig.after(c, 4))
                sp.dma_start(flag[:, c.slot(4), :], on_all(reset_row if c.phase == "attend" else same_row, c)).then_inc(flag_in.of(c), 16)

            def prod_store(c):
                sp.wait_ge(m_scaled.of(c), m_scaled.after(c))
                hold(sp, "sp")
                sp.dma_start(sorted_rows(prod_table[int(c.phase[-1])], c), prod[:, c.slot(4), :, :]).then_inc(m_stored.of(c), 16)

            def ea_load(c):
                s = c.slot(4)
                sp.wait_ge(ea_out.of(c), ea_out.free(c))
                hold(sp, "sp")
                sp.dma_start(EB[:, s, :, 0:D], file_rows(ea, E, c)).then_inc(ea_in.of(c), 16)
                sp.dma_start(dsti[:, s, :], take(dst, E - CH if c.last else c.index() * CH, CH).rearrange("(q t) -> q t", t=TPC)).then_inc(ea_in.of(c), 16)

            def ea_store(c):
                if c.last:
                    ea_out.earlier(sp, c, NC)
                sp.wait_ge(ea_in.of(c), ea_in.after(c))
                hold(sp, "sp")
                sp.wait_ge(ea_dst.of(c), ea_dst.after(c))
                hold(sp, "sp")
                sp.dma_start(file_rows(eae, E, c), EB[:, c.slot(4), :, :]).then_inc(ea_out.of(c), 16)

            run(sp, "mean0", [(5, flag_load), (7, second(x_load), SECOND), (0, prod_store),
                              (0, second(x_store), SECOND)], NC)
            added.end(sp, "dense")
            run(sp, "mean1", [(3, flag_load), (2, ea_load), (0, prod_store), (0, ea_store)], NC)
            run(sp, "mean2", [(3, flag_load), (0, prod_store)], NC)
            m_stored.end(sp, "mean2")

            def pl_load(c):
                sp.wait_ge(u2_done.of(c), u2_done.after(c, U))
                hold(sp, "sp")
                sp.wait_ge(added.of(c), added.after(c, U))
                hold(sp, "sp")
                for i in range(3):
                    sp.dma_start(PL[:, c.slot(U), i, :, :], sorted_rows(prod_table[i], c)).then_inc(pl_in.of(c), 16)

            run(sp, "dst", [(0, pl_load)], NC)
            put_done.end(sp, "dst")

            def node_load(half):
                def f(c):
                    node = c.item(2, half)
                    sp.wait_ge(f_turned.of(node), f_turned.after(node, U))
                    sp.dma_start(XN[:, node.slot(U), :, :], file_rows(xp, N, node)).then_inc(x_in.of(node), 16)
                return f

            def att_store(i):
                def f(c):
                    item = c.item(3, i)
                    if item.last:
                        x_out.earlier(sp, item, 3 * NC)
                    wait_normed(sp, item)
                    to = sorted_rows(attended, c) if i == 0 else file_rows(out, N, c.item(2, i - 1))
                    sp.dma_start(to, normed[:, item.slot(4), :, :]).then_inc(x_out.of(item), 16)
                return f

            ea_out.end(sp, "mean1")
            run(sp, "attend", [(3, flag_load), (2, node_load(0)), (2, node_load(1)), (0, att_store(0)),
                               (0, att_store(1)), (0, att_store(2))], NC)
            x_out.end(sp, "attend")

            def rest_load(c):
                sp.wait_ge(put_free.of(c), put_free.after(c, U))
                hold(sp, "sp")
                sp.dma_start(XN[:, c.slot(U), :, :], sorted_rows(attended, c)).then_inc(x_in.of(c), 16)

            run(sp, "rest", [(0, rest_load)], NC)
            put_done.end(sp, "rest")
            sp.sem_inc(all_out, 1)

        @block.gpsimd
        def _(pool):
            pool.wait_ge(go, 1)
            pool.memset(ident[:, :], 0.0).then_inc(pool_const, 1)
            pool.wait_ge(pool_const, 1)
            pool.affine_select(out=ident[:, :], in_=ident[:, :], compare_op=ALU.not_equal, fill=1.0, base=0,
                               pattern=[[-1, P]], channel_multiplier=1).then_inc(pool_const, 1)
            pool.iota(pos[:, :], pattern=[[1, LINE]], base=0, channel_multiplier=LINE).then_inc(pool_const, 1)
            for s in range(U):
                pool.memset(XB[:, s, :, D:XW], float(EP)).then_inc(pool_const, 1)
            pool.wait_ge(pool_const, 3 + U)

            def stage(c, signal_, *copies):
                first, count = c.slot(U), BLOCK if not isinstance(c.j, int) else min(BLOCK, NC - c.index())
                for to, cols in copies:
                    last = pool.tensor_copy(to[:, first:first + BLOCK, :].rearrange("p c t -> p (c t)"),
                                            take_cols(cols, c.index() * TPC, BLOCK * TPC))
                last.then_inc(signal_.of(c), count)

            def block_of(f):
                return lambda c: f(c) if c.u % BLOCK == 0 else None

            def gather(buf, table, idx, width, c, sig):
                for t in range(TPC):
                    pool.indirect_dma_start(buf[:, c.slot(U), t, 0:width], None, table,
                                            bass.IndirectOffsetOnAxis(ap=idx[:, c.slot(U), t:t + 1], axis=0)).then_inc(sig.of(c), 16)

            pool.wait_ge(cols_ready, 1)
            pool.wait_ge(rows_out, 32)
            xe_out.end(pool, "xe")

            def lk_stage(c):
                stage(c, idx_ready, (lval, col_f[:, 0, :]), (idx_a, col_i[:, V_PUT_A, :]))

            def lk_put(c):
                pool.wait_ge(idx_ready.of(c), idx_ready.after(c))
                hold(pool, "pool")
                for t in range(TPC):
                    pool.indirect_dma_start(xe, bass.IndirectOffsetOnAxis(ap=idx_a[:, c.slot(U), t:t + 1], axis=0),
                                            lval[:, c.slot(U), t:t + 1], None, element_offset=D,
                                            bounds_check=N - 1, oob_is_err=False).then_inc(put_done.of(c), 16)

            def lk_settle(c):
                pool.wait_ge(put_done.of(c), put_done.after(c))
                hold(pool, "pool")

            run(pool, "lk", [(0, lk_settle), (4, block_of(lk_stage)), (3, lk_put)], NC)
            put_done.end(pool, "lk")

            def mean_stage(c):
                end = c.ahead(BLOCK - 1)
                pool.wait_ge(m_turned.of(end), m_turned.after(end, U))
                stage(c, idx_ready, (idx_a, col_i[:, V_SRC_A, :] if c.phase == "mean0" else lookup[:, :]))

            def mean_gather(c):
                pool.wait_ge(idx_ready.of(c), idx_ready.after(c))
                pool.wait_ge(m_turned.of(c), m_turned.after(c, U))
                if c.phase == "mean0":
                    pool.wait_ge(m_look.of(c), m_look.free(c))
                hold(pool, "pool")
                if c.phase == "mean0":
                    gather(GX, xe, idx_a, XW, c, gathered)
                else:
                    gather(GX, prod_table[int(c.phase[-1]) - 1], idx_a, D, c, gathered)

            for i in range(3):
                if i:
                    m_look.end(pool, "mean0")
                    m_stored.end(pool, f"mean{i - 1}")
                    pool.wait_ge(zero_out, 16 * 6)
                run(pool, f"mean{i}", [(1, block_of(mean_stage)), (0, mean_gather)], NC)

            def dst_stage(c):
                end = c.ahead(BLOCK - 1)
                pool.wait_ge(t_done.of(end), t_done.after(end, U))
                hold(pool, "pool")
                stage(c, idx_ready, (idx_a, col_i[:, V_DST_A, :]))

            def dst_gather(c):
                pool.wait_ge(idx_ready.of(c), idx_ready.after(c))
                pool.wait_ge(added.of(c), added.after(c, U))
                hold(pool, "pool")
                gather(GX, x, idx_a, D, c, gathered)

            def put_stage(c):
                stage(c, put_ready, (idx_b, col_i[:, V_PUT_A if c.phase == "dst" else V_PUT_B, :]))

            def put(c):
                pool.wait_ge(put_ready.of(c), put_ready.after(c))
                if c.phase == "dst":
                    pool.wait_ge(n_done.of(c), n_done.after(c))
                    table, rows = xp, normed[:, c.slot(4), :, :]
                else:
                    pool.wait_ge(x_in.of(c), x_in.after(c))
                    table, rows = out, XN[:, c.slot(U), :, :]
                hold(pool, "pool")
                for t in range(TPC):
                    pool.indirect_dma_start(table,
                                            bass.IndirectOffsetOnAxis(ap=idx_b[:, c.slot(U), t:t + 1], axis=0),
                                            rows[:, t, :], None,
                                            bounds_check=N - 1, oob_is_err=False).then_inc(put_done.of(c), 16)

            def settle(c):
                pool.wait_ge(put_done.of(c), put_done.after(c))
                hold(pool, "pool")
                pool.sem_inc(put_free.of(c), 1)

            m_turned.end(pool, "mean2")
            x_out.end(pool, "dense")
            run(pool, "dst", [(8, block_of(dst_stage)), (7, dst_gather), (2, block_of(put_stage)), (1, put),
                              (0, settle)], NC)
            put_done.end(pool, "dst")
            ea_out.end(pool, "mean1")

            def rows_used(c):
                item = c.item(3, 2)
                pool.wait_ge(a_turned.of(item), a_turned.after(item, 3 * U))

            def att_stage(c):
                rows_used(c.ahead(BLOCK - 1))
                hold(pool, "pool")
                stage(c, idx_ready, (idx_c, col_i[:, V_SRC_B, :]), (idx_a, col_i[:, V_ID_B, :]))

            def att_gather(c):
                pool.wait_ge(idx_ready.of(c), idx_ready.after(c))
                rows_used(c)
                pool.wait_ge(dst_idx.of(c), dst_idx.free(c))
                hold(pool, "pool")
                gather(GX, eae, idx_a, XW, c, ea_got)
                gather(GP, xp, idx_c, D, c, gathered)

            def att_dst(c):
                pool.wait_ge(ea_got.of(c), ea_got.after(c))
                rows_used(c)
                hold(pool, "pool")
                pool.tensor_copy(idx_d[:, c.slot(U), :], lookup_column(c)).then_inc(dst_idx.of(c), 1)
                pool.wait_ge(dst_idx.of(c), dst_idx.after(c))
                hold(pool, "pool")
                gather(GD, xp, idx_d, D, c, dst_got)

            run(pool, "attend", [(7, block_of(att_stage)), (6, att_gather), (6, att_dst)], NC)

            x_out.end(pool, "attend")
            run(pool, "rest", [(4, block_of(put_stage)), (3, put), (0, settle)], NC)
            put_done.end(pool, "rest")

        @block.tensor
        def _(pe):
            def turn_in(dst, src):
                return pe.transpose(dst, src, ident[0:src.shape[0], 0:src.shape[0]])

            pe.wait_ge(pool_const, 3 + U)
            pe.wait_ge(w_loaded, 16 * len(W_FILES))
            for i in range(7):
                turn_in(bank[2 + i // 4][:, i % 4 * P:(i % 4 + 1) * P], wraw[:, i, :]).then_inc(w_turned, 1)
            steps = turns = side = 0
            for what, _ in plan:
                if what != "turn":
                    steps += 1
                    side ^= what == "compare"
                    continue
                pe.wait_ge(sort_step, 2 * steps + 2)
                for i in range(4):
                    last = turn_in(bank[turns % 2][:, i * P:(i + 1) * P],
                                   V[side][:, :, :].rearrange("p w f -> p (w f)")[:, i * P:(i + 1) * P])
                last.then_inc(turned, 1)
                turns += 1
            pe.wait_ge(w_ready, 1)
            pe.matmul(bank[4][:, 0:D], wt[:, T_V, :], wraw[:, W_OUT, :], start=True, stop=True).then_inc(vo_done, 1)
            pe.wait_ge(carry_made, 1)
            for i in range(2):
                turn_in(bank[2 + i][0:1, 0:P], local[:, i, LINE - 1:LINE]).then_inc(carry_turned, 1)
            pe.wait_ge(carry_made, 2)
            turn_in(bank[4][:, 0:1], carry_row[0:1, 2, 0:P]).then_inc(carry_turned, 1)
            pe.wait_ge(value_ready, 1)
            for i in range(8):
                for a in range(2):
                    last = turn_in(bank[i][:, a * P:(a + 1) * P], value[:, i, a * P:(a + 1) * P])
                last.then_inc(value_turned, 1)
            pe.wait_ge(cols_ready, 1)

            def rows_turned(rows, c):
                pe.wait_ge(t_kept.of(c), t_kept.after(c, 1))
                for t in range(TPC):
                    last = turn_in(bank[0][:, t * P:(t + 1) * P], rows[:, c.slot(U), t, 0:D])
                last.then_inc(t_done.of(c), 1)

            def chain_t(c):
                if c.phase == "dst":
                    pe.wait_ge(gathered.of(c), gathered.after(c))
                    rows_turned(GX, c)
                else:
                    pe.wait_ge(x_in.of(c), x_in.after(c))
                    rows_turned(XN, c)

            def layer(i, c, psum, before, kept_before, done, kept):
                pe.wait_ge(kept_before.of(c), kept_before.after(c))
                pe.wait_ge(kept.of(c), kept.after(c, 1))
                dst_phase = c.phase == "dst"
                last = pe.matmul(psum[:, :], wt[:, T_R[i], :], before[:, c.slot(2), :], start=True, stop=not dst_phase)
                if dst_phase:
                    pe.wait_ge(pl_in.of(c), pl_in.after(c))
                    for t in range(TPC):
                        last = pe.matmul(psum[:, t * P:(t + 1) * P], PL[:, c.slot(U), i, t, :], ident[:, :],
                                         start=False, stop=t == TPC - 1)
                last.then_inc(done.of(c), 1)

            def chain_1(c):
                layer(0, c, bank[1], h0, t_kept, u1_done, u1_kept)

            def chain_2(c):
                layer(1, c, bank[2], h1, u1_kept, u2_done, u2_kept)

            def chain_y(c):
                pe.wait_ge(u2_kept.of(c), u2_kept.after(c))
                pe.wait_ge(added.of(c), added.free(c))
                y = bank[6 + c.slot(2)]
                pe.matmul(y[:, :], ones3[:, :], b2row[:, :, :].rearrange("k t d -> k (t d)"), start=True, stop=False)
                for t in range(TPC):
                    last = pe.matmul(y[:, t * P:(t + 1) * P], h2[:, c.slot(2), t * P:(t + 1) * P], wt[:, T_R[2], :],
                                     start=False, stop=t == TPC - 1)
                last.then_inc(y_done.of(c), 1)

            chain = [(3, chain_t), (2, chain_1), (1, chain_2), (0, chain_y)]
            run(pe, "dense", chain, FIRST, to_end=False)

            def mean_turn(c):
                pe.wait_ge(gathered.of(c), gathered.after(c))
                pe.wait_ge(m_h.of(c), m_h.after(c, 1))
                psum = bank[5]
                if c.phase == "mean0":
                    for t in range(TPC):
                        last = turn_in(psum[:, t * P:(t + 1) * P], GX[:, c.slot(U), t, 0:D])
                else:
                    i = int(c.phase[-1]) - 1
                    pe.matmul(psum[:, :], wt[:, T_R[i], :], take_cols(hsrc, c.index() * CH, CH), start=True, stop=False)
                    for t in range(TPC):
                        last = pe.matmul(psum[:, t * P:(t + 1) * P], GX[:, c.slot(U), t, 0:D], ident[:, :],
                                         start=False, stop=t == TPC - 1)
                last.then_inc(m_turned.of(c), 1)

            def mean_prod(c):
                pe.wait_ge(m_seg.of(c), m_seg.after(c))
                pe.wait_ge(m_scaled.of(c), m_scaled.free(c))
                for t in range(TPC):
                    last = pe.matmul(bank[3 + c.slot(2)][:, t * P:(t + 1) * P], seg[:, c.slot(2), t * P:(t + 1) * P],
                                     wt[:, T_L[int(c.phase[-1])], :], start=True, stop=True)
                last.then_inc(m_prod.of(c), 1)

            for i in range(3):
                if i == 0:
                    run(pe, "mean0", [(3, second(chain_t), SECOND), (3, mean_turn), (2, second(chain_1), SECOND),
                                      (1, mean_prod), (1, second(chain_2), SECOND), (0, second(chain_y), SECOND)], NC)
                else:
                    run(pe, f"mean{i}", [(1, mean_turn), (0, mean_prod)], NC)
                m_h.end(pe, f"mean{i}")
            m_scaled.end(pe, "mean2")

            run(pe, "dst", chain, NC)
            added.end(pe, "dst")

            def att_turn(i):
                rows, sig = ((GX, ea_got), (GP, gathered), (GD, dst_got))[i]
                def f(c):
                    item = c.item(3, i)
                    pe.wait_ge(sig.of(c), sig.after(c))
                    pe.wait_ge(a_kept.of(item), a_kept.free(item))
                    for t in range(TPC):
                        last = turn_in(bank[0][:, t * P:(t + 1) * P], rows[:, c.slot(U), t, 0:D])
                    last.then_inc(a_turned.of(item), 1)
                return f

            def node_turn(half):
                def f(c):
                    node = c.item(2, half)
                    pe.wait_ge(x_in.of(node), x_in.after(node))
                    pe.wait_ge(f_kept.of(node), f_kept.free(node))
                    for t in range(TPC):
                        last = turn_in(bank[1][:, t * P:(t + 1) * P], XN[:, node.slot(U), t, :])
                    last.then_inc(f_turned.of(node), 1)
                return f

            def att_qkv(c):
                s, kept = c.slot(2), c.item(3, 2)
                pe.wait_ge(a_kept.of(kept), a_kept.after(kept))
                pe.wait_ge(a_qk.of(c), a_qk.free(c))
                pe.matmul(bank[2][:, :], wraw[:, W_Q, :], src_t[:, c.slot(4), :], start=True, stop=True)
                pe.matmul(bank[3][:, :], wraw[:, W_K, :], h2[:, s, :], start=True, stop=False)
                pe.matmul(bank[3][:, :], wraw[:, W_EK, :], h0[:, s, :], start=False, stop=True).then_inc(a_qk_psum.of(c), 1)
                pe.wait_ge(a_v.of(c), a_v.free(c))
                pe.matmul(bank[4][:, :], wraw[:, W_V, :], h2[:, s, :], start=True, stop=False)
                pe.matmul(bank[4][:, :], wraw[:, W_EV, :], h0[:, s, :], start=False, stop=True).then_inc(a_v_psum.of(c), 1)

            def att_logit(c):
                pe.wait_ge(a_qk.of(c), a_qk.after(c))
                pe.wait_ge(a_dmax.of(c), a_dmax.free(c))
                pe.matmul(bank[5][:, :], wexp_rep[:, :, :].rearrange("p h d -> p (h d)"), qk[:, :],
                          start=True, stop=True).then_inc(a_logit.of(c), 1)

            def att_y(c):
                item = c.item(3, 0)
                y = bank[7]
                pe.wait_ge(a_agg.of(c), a_agg.after(c))
                pe.wait_ge(n_done.of(c), n_done.after(c, 1))
                for t in range(TPC):
                    pe.matmul(y[:, t * P:(t + 1) * P], src_t[:, c.slot(4), t * P:(t + 1) * P], wt[:, T_OUT, :], start=True, stop=False)
                    last = pe.matmul(y[:, t * P:(t + 1) * P], agg[:, c.slot(2), t * P:(t + 1) * P], wt[:, T_NOUT, :],
                                     start=False, stop=True)
                last.then_inc(y_done.of(item), 1)

            def node_y(half):
                def f(c):
                    item, node = c.item(3, 1 + half), c.item(2, half)
                    pe.wait_ge(f_kept.of(node), f_kept.after(node))
                    pe.wait_ge(n_node.of(node), n_node.after(node, 1))
                    for t in range(TPC):
                        last = pe.matmul(bank[6][:, t * P:(t + 1) * P],
                                         node_t[:, node.slot(4), t * P:(t + 1) * P], wt[:, T_OUT, :], start=True, stop=True)
                    last.then_inc(y_done.of(item), 1)
                return f

            run(pe, "attend", [(0, att_y), (2, att_turn(1)), (1, node_turn(0)), (2, att_turn(2)), (1, node_turn(1)),
                                (0, node_y(0)), (2, att_qkv), (0, node_y(1)), (3, att_turn(0)), (2, att_logit)], NC)

        @block.scalar
        def _(act):
            act.preload_act_table_set("natural_log_exp_and_others")
            act.wait_ge(go, 1)
            act.wait_ge(pool_const, 3 + U)

            def xe_load(c):
                act.wait_ge(xe_out.of(c), xe_out.free(c))
                act.dma_start(XB[:, c.slot(U), :, 0:D], file_rows(x, N, c)).then_inc(xe_in.of(c), 16)

            def xe_store(c):
                if c.last:
                    xe_out.earlier(act, c, NN)
                act.wait_ge(xe_in.of(c), xe_in.after(c))
                act.dma_start(file_rows(xe, N, c), XB[:, c.slot(U), :, :]).then_inc(xe_out.of(c), 16)

            run(act, "xe", [(4, xe_load), (0, xe_store)], NN)
            act.wait_ge(cols_ready, 1)

            def keep_t(c):
                act.wait_ge(t_done.of(c), t_done.after(c))
                act.wait_ge(u1_done.of(c), u1_done.free(c))
                act.activation(h0[:, c.slot(2), :], bank[0][:, :], ACT.Copy).then_inc(t_kept.of(c), 1)

            def keep_1(c):
                act.wait_ge(u1_done.of(c), u1_done.after(c))
                act.wait_ge(u2_done.of(c), u2_done.free(c))
                act.activation(h1[:, c.slot(2), :], bank[1][:, :], ACT.Relu, bias=bcol[:, 0:1]).then_inc(u1_kept.of(c), 1)

            def keep_2(c):
                act.wait_ge(u2_done.of(c), u2_done.after(c))
                act.wait_ge(y_done.of(c), y_done.free(c))
                act.activation(h2[:, c.slot(2), :], bank[2][:, :], ACT.Relu, bias=bcol[:, 1:2]).then_inc(u2_kept.of(c), 1)

            def inverse_root(c):
                s = norm_slot(c)
                act.wait_ge(n_aggr.of(c), n_aggr.after(c))
                act.activation(logv[:, s, :], mv[:, s, :, 1], ACT.Ln, bias=eps[:, 0:1]).then_inc(n_log.of(c), 1)
                act.wait_ge(n_log.of(c), n_log.after(c))
                wait_norm_slot(act, c)
                act.activation(rstd[:, s, :], logv[:, s, :], ACT.Exp, scale=-0.5).then_inc(n_rstd.of(c), 1)

            chain = [(3, keep_t), (2, keep_1), (1, keep_2), (0, inverse_root)]
            run(act, "dense", chain, FIRST, to_end=False)

            def ea_fill(c):
                s = c.slot(4)
                act.wait_ge(ea_in.of(c), ea_in.after(c))
                act.activation(EB[:, s, :, D:XW], dsti[:, s, :].rearrange("p (t a) -> p t a", a=1).to_broadcast([P, TPC, XW - D]),
                               ACT.Copy).then_inc(ea_dst.of(c), 1)

            def mean_keep(c):
                act.wait_ge(m_turned.of(c), m_turned.after(c))
                i = int(c.phase[-1])
                h = take_cols(hsrc, c.index() * CH, CH)
                if i == 0:
                    act.activation(h, bank[5][:, :], ACT.Copy).then_inc(m_h.of(c), 1)
                else:
                    act.activation(h, bank[5][:, :], ACT.Relu, bias=bcol[:, i - 1:i]).then_inc(m_h.of(c), 1)

            for i in range(3):
                if i:
                    m_seg.end(act, f"mean{i - 1}")
                if i == 0:
                    run(act, "mean0", [(3, second(keep_t), SECOND), (3, mean_keep), (2, second(keep_1), SECOND),
                                       (1, second(keep_2), SECOND), (0, second(inverse_root), SECOND)], NC)
                else:
                    run(act, f"mean{i}", [(0, mean_keep)] + ([(1, ea_fill)] if i == 1 else []), NC)
            run(act, "dst", chain, NC)
            y_done.end(act, "dst")

            def att_keep(i):
                def f(c):
                    item, y = c.item(3, i), c.item(3, 0)
                    act.wait_ge(a_turned.of(item), a_turned.after(item))
                    if i == 1:
                        act.wait_ge(y_done.of(y), y_done.after(y, 12))
                        to = src_t[:, c.slot(4), :]
                    else:
                        act.wait_ge(a_v_psum.of(c), a_v_psum.after(c, 2))
                        to = (h2 if i else h0)[:, c.slot(2), :]
                    act.activation(to, bank[0][:, :], ACT.Copy).then_inc(a_kept.of(item), 1)
                return f

            def node_keep(half):
                def f(c):
                    item, node = c.item(3, 1 + half), c.item(2, half)
                    act.wait_ge(f_turned.of(node), f_turned.after(node))
                    act.wait_ge(y_done.of(item), y_done.after(item, 6))
                    act.activation(node_t[:, node.slot(4), :], bank[1][:, :], ACT.Copy).then_inc(f_kept.of(node), 1)
                return f

            def att_k(c):
                act.wait_ge(a_qk_psum.of(c), a_qk_psum.after(c))
                act.wait_ge(a_qk.of(c), a_qk.free(c))
                act.activation(k_sb[:, :], bank[3][:, :], ACT.Copy).then_inc(a_k.of(c), 1)

            def att_v(c):
                act.wait_ge(a_v_psum.of(c), a_v_psum.after(c))
                act.wait_ge(a_wv.of(c), a_wv.after(c, 2))
                act.activation(v_sb[:, c.slot(2), :], bank[4][:, :], ACT.Copy).then_inc(a_v.of(c), 1)

            def att_exp(c):
                act.wait_ge(a_dmax.of(c), a_dmax.after(c))
                act.wait_ge(a_num.of(c), a_num.after(c, 1))
                act.activation(decay[:, :], dmax[:, 0, :], ACT.Exp)
                act.activation(weight[:, :], dmax[:, 1, :], ACT.Exp).then_inc(a_exp.of(c), 1)

            def att_reciprocal(c):
                act.wait_ge(a_den.of(c), a_den.after(c))
                act.wait_ge(a_agg.of(c), a_agg.after(c, 1))
                act.activation(qr[:, :], den[:, c.slot(2), :], ACT.Ln).then_inc(a_rlog.of(c), 1)
                act.wait_ge(a_rlog.of(c), a_rlog.after(c))
                act.activation(qr[:, :], qr[:, :], ACT.Exp, scale=-1.0).then_inc(a_rden.of(c), 1)

            def root(i):
                return lambda c: inverse_root(c.item(3, i))

            def node_norm(half):
                def f(c):
                    item, node = c.item(3, 1 + half), c.item(2, half)
                    s = norm_slot(item)
                    act.wait_ge(n_shift.of(node), n_shift.after(node))
                    act.wait_ge(x_out.of(item), x_out.free(item))
                    for t in range(TPC):
                        last = act.activation(normed[:, item.slot(4), t, :], norm_rows(item)[:, t, :], ACT.Identity,
                                              bias=shift[:, s, t:t + 1], scale=rstd[:, s, t:t + 1])
                    last.then_inc(n_node.of(node), 1)
                return f

            run(act, "attend", [(2, att_keep(1)), (1, node_keep(0)), (2, att_keep(2)), (1, node_keep(1)), (0, root(0)),
                                (1, att_exp), (0, root(1)), (0, node_norm(0)), (2, att_k), (1, att_reciprocal),
                                (2, att_v), (3, att_keep(0)), (0, root(2)), (0, node_norm(1))], NC)

        @block.vector
        def _(dve):
            done = [0]

            def link(ins):
                done[0] += 1
                ins.then_inc(dve_step, 1)
                dve.wait_ge(dve_step, done[0])

            dve.memset(kin[:, :, :], N).then_inc(pad_ready, 1)
            dve.memset(zrow[:, :], 0.0).then_inc(pad_ready, 1)
            link(dve.memset(ones[:, :], 1.0))
            link(dve.memset(ones3[:, :], 1.0))
            link(dve.memset(eps[:, :], EPS))
            link(dve.memset(carry_row[:, :, :], 0.0))
            link(dve.memset(seg[:, :, :], 0.0))
            link(dve.memset(lookup[:, :], 0))

            w = [one[:, :] for one in work]
            a_bits, b_bits = V[0][:, 0, :].bitcast(I32), V[0][:, 1, :].bitcast(I32)
            dve.wait_ge(pool_const, 3 + U)
            dve.wait_ge(keys_loaded, 64)
            dst_k, src_k = kin[:, 0, :], kin[:, 1, :]
            link(dve.tensor_scalar(w[0], dst_k, float(HALF), None, ALU.is_lt))
            link(dve.tensor_scalar(w[1], dst_k, -float(HALF), None, ALU.add))
            link(dve.tensor_scalar(w[2], w[0], -2.0, 1.0, ALU.mult, ALU.add))
            link(dve.tensor_tensor(w[1], w[1], w[2], ALU.mult))
            link(dve.tensor_scalar(w[1], w[1], float(MAG0), None, ALU.add))
            link(dve.tensor_scalar(w[1], w[1], 16, None, ALU.logical_shift_left))
            link(dve.tensor_scalar(w[0], w[0], 31, None, ALU.logical_shift_left))
            link(dve.tensor_tensor(w[1], w[1], w[0], ALU.bitwise_or))
            link(dve.tensor_tensor(a_bits, w[1], src_k, ALU.bitwise_or))
            link(dve.tensor_scalar(w[3], src_k, float(SRC0), None, ALU.add))
            link(dve.tensor_scalar(w[3], w[3], 15, None, ALU.logical_shift_left))
            link(dve.tensor_tensor(b_bits, w[3], pos[:, :], ALU.bitwise_or))
            link(dve.tensor_scalar(w[4], pos[:, :], 1, None, ALU.logical_shift_right))
            for i in range(2):
                link(dve.tensor_tensor(gray[:, i, :], pos[:, :], w[4], ALU.bitwise_xor))
                link(dve.tensor_scalar(flip[:, 0, i, :], w[4], 31, None, ALU.logical_shift_left))
            all_bits = V[0][:, :, :].bitcast(I32)
            dve.tensor_tensor(all_bits, all_bits, flip[:, 0, :, :], ALU.bitwise_xor).then_inc(sort_step, 2)

            steps = turns = side = 0
            in_psum = False
            flat = [one[:, :, :].rearrange("p w f -> p (w f)") for one in V]
            now = flat[0]
            for what, n in plan:
                if what == "turn":
                    turns += 1
                    dve.wait_ge(turned, turns)
                    now = bank[(turns - 1) % 2][:, :]
                    in_psum = True
                    continue
                if what == "flip":
                    one = flip[:, n % 2, :, :]
                    link(dve.tensor_scalar(one, gray[:, :, :], n, 31, ALU.logical_shift_right, ALU.logical_shift_left))
                    dve.wait_ge(sort_step, 2 * steps + 2)
                    bits = V[side][:, :, :].bitcast(I32)
                    dve.tensor_tensor(bits, bits, one, ALU.bitwise_xor).then_inc(sort_step, 2)
                    steps += 1
                    continue
                pairs = now.rearrange("p (g two s) -> p g two s", two=2, s=n)
                upper = pairs[:, :, 1, :]
                if in_psum:
                    upper = flat[side].rearrange("p (g two s) -> p g two s", two=2, s=n)[:, :, 1, :]
                    link(dve.tensor_copy(upper, pairs[:, :, 1, :]))
                    in_psum = False
                side ^= 1
                to = flat[side].rearrange("p (g two s) -> p g two s", two=2, s=n)
                dve.wait_ge(sort_step, 2 * steps + 2)
                dve.tensor_tensor(to[:, :, 0, :], pairs[:, :, 0, :], upper, ALU.min).then_inc(sort_step, 1)
                dve.tensor_tensor(to[:, :, 1, :], pairs[:, :, 0, :], upper, ALU.max).then_inc(sort_step, 1)
                steps += 1
                now = flat[side]
            dve.wait_ge(sort_step, 2 * steps + 2)

            va, vb = V[side][:, 0, :].bitcast(I32), V[side][:, 1, :].bitcast(I32)
            for i, (v, n) in enumerate(((va, 16), (vb, 15))):
                link(dve.tensor_scalar(w[i], v, n, None, ALU.logical_shift_right))
                link(dve.tensor_scalar(keyf[:, i, :].bitcast(I32), w[i], n, None, ALU.logical_shift_left))
            dve.memset(work[5][:, 0:1], 0.0).then_inc(keys_made, 1)
            link(dve.tensor_scalar(w[2], va, 31, None, ALU.logical_shift_right))
            link(dve.tensor_scalar(w[2], w[2], 1, None, ALU.bitwise_and))
            link(dve.tensor_scalar(w[2], w[2], -2.0, 1.0, ALU.mult, ALU.add))
            link(dve.tensor_scalar(w[0], w[0], 0x7FFF, None, ALU.bitwise_and))
            link(dve.tensor_scalar(w[0], w[0], -float(MAG0), None, ALU.add))
            link(dve.tensor_tensor(w[0], w[0], w[2], ALU.mult))
            link(dve.tensor_scalar(w[0], w[0], float(HALF), None, ALU.add))
            link(dve.tensor_scalar(w[3], va, 0xFFFF, None, ALU.bitwise_and))
            link(dve.tensor_scalar(w[1], w[1], -float(SRC0), None, ALU.add))
            link(dve.tensor_scalar(w[4], vb, 0x7FFF, None, ALU.bitwise_and))
            for to, v, most in ((V_SRC_A, w[3], N - 1), (V_DST_A, w[0], N - 1), (V_ID_B, w[4], E - 1), (V_SRC_B, w[1], N - 1)):
                link(dve.tensor_scalar(value[:, to, :], v, float(most), None, ALU.min))
            link(dve.tensor_copy(value[:, V_POS, :], pos[:, :]))
            dve.wait_ge(w_turned, 7)
            link(dve.tensor_copy(wt[:, 0:4, :], by_tile(bank[2][:, :])))
            dve.tensor_copy(wt[:, 4:7, :], bank[3][:, 0:3 * P].rearrange("p (t d) -> p t d", t=3)).then_inc(w_ready, 1)
            dve.wait_ge(w_ready, 1)
            dve.wait_ge(vo_done, 1)
            link(dve.tensor_tensor(wt[:, T_OUT, :], bank[4][:, 0:D], ident[:, :], ALU.add))
            link(dve.tensor_scalar(wt[:, T_NOUT, :], wraw[:, W_OUT, :], -1.0, None, ALU.mult))
            dve.wait_ge(small_loaded, 16 * (H + 3))
            link(dve.tensor_scalar(wexp_rep[:, :, :], wexp_rows[:, :].rearrange("p (h a) -> p h a", a=1).to_broadcast([P, H, HD]),
                                   float(HD) ** -0.5, None, ALU.mult))
            link(dve.tensor_copy(b2part[:, 0, :], b2[:, :]))
            link(dve.tensor_tensor(b2rest[:, 0, :], b2[:, :], b2part[:, 0, :], ALU.subtract))
            link(dve.tensor_copy(b2part[:, 1, :], b2rest[:, 0, :]))
            link(dve.tensor_tensor(b2rest[:, 1, :], b2rest[:, 0, :], b2part[:, 1, :], ALU.subtract))
            link(dve.tensor_copy(b2part[:, 2, :], b2rest[:, 1, :]))
            for i in range(3):
                link(dve.tensor_scalar(b2mask[:, i, :], b2part[:, i, :], ident[0:3, i:i + 1], None, ALU.mult))
            link(dve.tensor_tensor(b2mask[:, 0, :], b2mask[:, 0, :], b2mask[:, 1, :], ALU.add))
            link(dve.tensor_tensor(b2mask[:, 0, :], b2mask[:, 0, :], b2mask[:, 2, :], ALU.add))
            for t in range(TPC):
                link(dve.tensor_copy(b2row[:, t, :], b2mask[:, 0, :]))

            dve.wait_ge(near_in, 64)
            link(dve.tensor_tensor(same[:, :], keyf[:, 0, :], near[:, 0, 0, :], ALU.is_equal))
            link(dve.tensor_tensor(resetf[:, :], keyf[:, 1, :], near[:, 1, 0, :], ALU.not_equal))
            dve.tensor_scalar(resetf[:, :], resetf[:, :], RESET, None, ALU.mult).then_inc(flags_made, 1)
            for i, (to, v) in enumerate(((V_PUT_A, w[0]), (V_PUT_B, w[1]))):
                link(dve.tensor_tensor(near[:, i, 1, :], keyf[:, i, :], near[:, i, 1, :], ALU.is_equal))
                link(dve.tensor_scalar(near[:, i, 1, :], near[:, i, 1, :], FAR, None, ALU.mult))
                link(dve.tensor_tensor(value[:, to, :], near[:, i, 1, :], v, ALU.add))
            link(dve.tensor_tensor_scan(local[:, 0, :], same[:, :], ones[:, :], 0.0, ALU.mult, ALU.add))
            dve.tensor_tensor_scan(local[:, 1, :], same[:, :], ones[:, :], 1.0, ALU.mult, ALU.mult).then_inc(carry_made, 1)
            dve.wait_ge(carry_turned, 2)
            for i in range(2):
                link(dve.tensor_copy(carry_row[0:1, i, 0:P], bank[2 + i][0:1, 0:P]))
            dve.tensor_tensor_scan(carry_row[0:1, 2, 1:P + 1], carry_row[0:1, 1, 0:P], carry_row[0:1, 0, 0:P], 0.0,
                                   ALU.mult, ALU.add).then_inc(carry_made, 1)
            dve.wait_ge(carry_turned, 3)
            link(dve.tensor_copy(carry_col[:, :], bank[4][:, 0:1]))
            link(dve.tensor_scalar(local[:, 1, :], local[:, 1, :], carry_col[:, 0:1], None, ALU.mult))
            link(dve.tensor_tensor(local[:, 0, :], local[:, 0, :], local[:, 1, :], ALU.add))
            dve.reciprocal(value[:, V_INV, :], local[:, 0, :]).then_inc(value_ready, 1)
            for i in range(8):
                dve.wait_ge(value_turned, i + 1)
                to = col_i[:, i, :] if i < 6 else col_f[:, i - 6, :]
                link(dve.tensor_copy(to.rearrange("q (p a) -> q a p", a=2), bank[i][:, 0:LINE].rearrange("q (a p) -> q a p", a=2)))
            dve.memset(work[5][:, 0:1], 0.0).then_inc(cols_ready, 1)

            def add(rows, c):
                s = norm_slot(c)
                y = by_tile(bank[6 + c.slot(2)][:, :])
                dve.wait_ge(y_done.of(c), y_done.after(c))
                wait_norm_slot(dve, c)
                if c.phase == "dst":
                    dve.tensor_tensor(res[:, s, :, :], y, rows, ALU.add).then_inc(added0.of(c), 1)
                    dve.wait_ge(added0.of(c), added0.after(c))
                    dve.wait_ge(pl_in.of(c), pl_in.after(c))
                    dve.tensor_tensor(res[:, s, :, :], res[:, s, :, :], PL[:, c.slot(U), 2, :, :], ALU.add).then_inc(added.of(c), 1)
                else:
                    dve.tensor_tensor(res[:, s, :, :], y, rows, ALU.add).then_inc(added.of(c), 1)
                dve.wait_ge(added.of(c), added.after(c))
                measure(c)

            def measure(c):
                s, rows = norm_slot(c), norm_rows(c)
                for t in range(TPC):
                    last = dve.bn_stats(stats[:, s, t, :], rows[:, t, :])
                last.then_inc(n_stats.of(c), 1)
                dve.wait_ge(n_stats.of(c), n_stats.after(c))
                hold(dve, "dve")
                for t in range(TPC):
                    last = dve.bn_aggr(mv[:, s, t, :], stats[:, s, t, :])
                last.then_inc(n_aggr.of(c), 1)

            def norm(c):
                s, (sig, what, _) = norm_slot(c), normed_by(c)
                dve.wait_ge(n_rstd.of(c), n_rstd.after(c))
                if c.phase == "dst":
                    dve.wait_ge(put_free.of(c), put_free.free(c))
                else:
                    dve.wait_ge(x_out.of(c), x_out.free(c))
                for t in range(TPC):
                    last = dve.tensor_scalar(normed[:, c.slot(4), t, :], norm_rows(c)[:, t, :], mv[:, s, t, 0:1],
                                             rstd[:, s, t:t + 1], ALU.subtract, ALU.mult)
                last.then_inc(sig.of(what), 1)

            def add_x(c):
                add(XN[:, c.slot(U), :, :], c)

            def add_gathered(c):
                add(GX[:, c.slot(U), :, 0:D], c)

            run(dve, "dense", [(1, add_x), (0, norm)], FIRST, to_end=False)

            def mean_seg(c):
                dve.wait_ge(m_h.of(c), m_h.after(c))
                dve.wait_ge(flag_in.of(c), flag_in.after(c))
                dve.wait_ge(m_prod.of(c), m_prod.free(c))
                before = c.ahead(-1)
                dve.wait_ge(m_seg.of(before), m_seg.after(before))
                dve.tensor_tensor_scan(seg[:, c.slot(2), :], flag[:, c.slot(4), :], take_cols(hsrc, c.index() * CH, CH),
                                       seg[:, before.slot(2), CH - 1:CH], ALU.mult, ALU.add).then_inc(m_seg.of(c), 1)
                if c.phase == "mean0":
                    dve.wait_ge(gathered.of(c), gathered.after(c))
                    dve.tensor_copy(take_cols(lookup, c.index() * TPC, TPC), lookup_column(c)).then_inc(m_look.of(c), 1)

            def mean_scale(c):
                dve.wait_ge(m_prod.of(c), m_prod.after(c))
                dve.wait_ge(m_stored.of(c), m_stored.free(c))
                inv = take_cols(col_f[:, 1, :], c.index() * TPC, TPC).rearrange("p (t a) -> p t a", a=1).to_broadcast([P, TPC, D])
                dve.tensor_tensor(prod[:, c.slot(4), :, :], by_tile(bank[3 + c.slot(2)][:, :]), inv, ALU.mult)\
                   .then_inc(m_scaled.of(c), 1)

            for i in range(3):
                if i == 0:
                    run(dve, "mean0", [(3, mean_seg), (1, mean_scale), (1, second(add_x), SECOND),
                                       (0, second(norm), SECOND)], NC)
                else:
                    run(dve, f"mean{i}", [(1, mean_seg), (0, mean_scale)], NC)

            x_out.end(dve, "dense")
            run(dve, "dst", [(1, add_gathered), (0, norm)], NC)
            put_done.end(dve, "dst")

            for sums in (runmax, den, num):
                link(dve.memset(sums[:, :, :], 0.0))

            def att_qk(c):
                dve.wait_ge(a_k.of(c), a_k.after(c))
                dve.wait_ge(a_logit.of(c), a_logit.free(c))
                dve.tensor_tensor(qk[:, :], bank[2][:, :], k_sb[:, :], ALU.mult).then_inc(a_qk.of(c), 1)

            def att_max(c):
                s, before = c.slot(2), c.ahead(-1)
                top, prev = runmax[:, s, 1:CH + 1], runmax[:, s, 0:CH]
                reset, logit = flag[:, c.slot(4), :], bank[5][:, :]
                dve.wait_ge(a_max.of(before), a_max.after(before))
                dve.tensor_copy(runmax[:, s, 0:1], runmax[:, before.slot(2), CH:CH + 1]).then_inc(a_carry.of(c), 1)
                dve.wait_ge(a_carry.of(c), a_carry.after(c))
                dve.wait_ge(flag_in.of(c), flag_in.after(c))
                dve.wait_ge(a_logit.of(c), a_logit.after(c))
                dve.tensor_tensor_scan(top, reset, logit, runmax[:, s, 0:1], ALU.add, ALU.max).then_inc(a_max.of(c), 1)
                dve.wait_ge(a_exp.of(c), a_exp.free(c))
                dve.wait_ge(a_max.of(c), a_max.after(c))
                dve.tensor_tensor(dmax[:, 0, :], prev, reset, ALU.add).then_inc(a_step1.of(c), 1)
                dve.tensor_tensor(dmax[:, 1, :], logit, top, ALU.subtract)
                dve.wait_ge(a_step1.of(c), a_step1.after(c))
                dve.tensor_tensor(dmax[:, 0, :], dmax[:, 0, :], top, ALU.subtract).then_inc(a_dmax.of(c), 1)

            def att_sums(c):
                s, before = c.slot(2), c.ahead(-1)
                dve.wait_ge(a_exp.of(c), a_exp.after(c))
                dve.wait_ge(a_den.of(before), a_den.after(before))
                dve.tensor_tensor_scan(den[:, s, :], decay[:, :], weight[:, :], den[:, before.slot(2), CH - 1:CH],
                                       ALU.mult, ALU.add).then_inc(a_den.of(c), 1)
                dve.wait_ge(a_v.of(c), a_v.after(c))
                dve.tensor_tensor(weight[:, :], weight[:, :], v_sb[:, s, :], ALU.mult).then_inc(a_wv.of(c), 1)
                dve.wait_ge(a_wv.of(c), a_wv.after(c))
                dve.wait_ge(a_num.of(before), a_num.after(before))
                dve.tensor_tensor_scan(num[:, s, :], decay[:, :], weight[:, :], num[:, before.slot(2), CH - 1:CH],
                                       ALU.mult, ALU.add).then_inc(a_num.of(c), 1)

            def att_agg(c):
                s, item = c.slot(2), c.item(3, 0)
                dve.wait_ge(a_rden.of(c), a_rden.after(c))
                dve.wait_ge(a_num.of(c), a_num.after(c))
                dve.wait_ge(y_done.of(item), y_done.after(item, 6))
                dve.tensor_tensor(agg[:, s, :], num[:, s, :], qr[:, :], ALU.mult).then_inc(a_agg.of(c), 1)

            def att_measure(i):
                def f(c):
                    item = c.item(3, i)
                    dve.wait_ge(y_done.of(item), y_done.after(item))
                    wait_norm_slot(dve, item)
                    measure(item)
                return f

            def att_norm(c):
                norm(c.item(3, 0))

            def node_shift(half):
                def f(c):
                    item, node = c.item(3, 1 + half), c.item(2, half)
                    s = norm_slot(item)
                    dve.wait_ge(n_rstd.of(item), n_rstd.after(item))
                    dve.scalar_tensor_tensor(shift[:, s, :], mv[:, s, :, 0], -1.0, rstd[:, s, :], ALU.mult, ALU.mult)\
                       .then_inc(n_shift.of(node), 1)
                return f

            run(dve, "attend", [(1, att_max), (0, att_measure(0)), (0, att_measure(1)), (0, att_norm),
                                (0, node_shift(0)), (1, att_sums), (2, att_qk), (1, att_agg), (0, att_measure(2)),
                                (0, node_shift(1))], NC)


_INS = ["x", "src", "dst", "edge_attr_128", "L0_gnn_Wl0", "L0_gnn_bl0", "L0_gnn_Wr0", "L0_gnn_Wl1", "L0_gnn_bl1",
        "L0_gnn_Wr1", "L0_gnn_Wl2", "L0_gnn_bl2", "L0_gnn_Wr2", "L1_gnn_Wq", "L1_gnn_Wk", "L1_gnn_Wv", "L1_gnn_Wek",
        "L1_gnn_Wev", "L1_gnn_W_exp", "L1_gnn_W_out"]


def kernel(**inputs):
    import numpy as _np
    import concourse.bacc as _bacc
    from concourse import mybir as _mybir
    from concourse.bass_utils import run_bass_kernel_spmd as _run

    nc = _bacc.Bacc("TRN2", target_bir_lowering=False, num_devices=1)
    arrays, args = {}, []
    for name in _INS:
        a = _np.ascontiguousarray(inputs[name])
        arrays[f"in_{name}_dram"] = a
        args.append(nc.dram_tensor(f"in_{name}_dram", a.shape, _mybir.dt.from_np(a.dtype), kind="ExternalInput").ap())
    x = arrays["in_x_dram"]
    args.append(nc.dram_tensor("out_0_dram", x.shape, _mybir.dt.from_np(x.dtype), kind="ExternalOutput").ap())
    gnn_kernel(nc, *args)
    r = _run(nc, [arrays], core_ids=[0])
    return r.results[0]["out_0_dram"]
```
